# Optimizing a Trainium2 kernel written in Bass

```python
import numpy as np
import jax
import jax.numpy as jnp

def _softmax(x, axis=-1):
    return jax.nn.softmax(x, axis=axis)

def _gelu(x):
    return jax.nn.gelu(x, approximate=True)

def _silu(x):
    return jax.nn.silu(x)

def _sigmoid(x):
    return jax.nn.sigmoid(x)

def _layernorm(x, axis=-1, eps=1e-05):
    m = jnp.mean(x, axis=axis, keepdims=True)
    v = jnp.var(x, axis=axis, keepdims=True)
    return (x - m) / jnp.sqrt(v + eps)

def _scatter_add(tgt, idx, src, axis=0):
    return tgt.at[idx].add(src)

def _segment_sum(src, seg, n):
    return jax.ops.segment_sum(src, seg, n)
kernel_name = 'mk_seq_postln_d1_jaxref_r8_36a04b'

def setup_inputs(seed: int=0):
    np.random.seed(seed)
    _w = jnp.asarray

    def _L0_attn_setup():
        import jax, jax.numpy as jnp
        import numpy as np
        B, S, D_IN = (2, 256, 128)
        D_OUT, H, WINDOW = (128, 16, 64)
        HD = D_OUT // H
        key = jax.random.key(seed)
        k1, k2, k3, k4 = jax.random.split(key, 4)
        scale_in = 1.0 / np.sqrt(D_IN)
        scale_out = 1.0 / np.sqrt(D_OUT)
        return {'x': jax.random.normal(k1, (B, S, D_IN), dtype=jnp.float32), 'w_qkv': jax.random.normal(k2, (3 * D_OUT, D_IN), dtype=jnp.float32) * scale_in, 'w_out': jax.random.normal(k3, (D_OUT, D_OUT), dtype=jnp.float32) * scale_out, 'b_out': jax.random.normal(k4, (D_OUT,), dtype=jnp.float32) * scale_out}
    _L0_attn_in = _L0_attn_setup()

    def _L0_ffn_setup():
        import jax, jax.numpy as jnp
        import numpy as np
        B, S, H = (2, 128, 128)
        DFF = 256
        E = 8
        TOPK = 2

        def _expert_ffn(x, w1, b1, w2, b2, wg, bg, w3, b3):
            x1 = jnp.einsum('bsh,hf->bsf', x, w1) + b1
            x2 = jnp.einsum('bsh,hf->bsf', x, w2) + b2
            z = x1 * x2
            s = jax.nn.silu(jnp.einsum('bsf,fg->bsg', z, wg) + bg)
            return jnp.einsum('bsg,gh->bsh', s, w3) + b3
        key = jax.random.key(seed)
        ks = jax.random.split(key, 12)
        sc = 0.02
        return {'x': jax.random.normal(ks[0], (B, S, H), jnp.float32), 'gate_w': jax.random.normal(ks[1], (H, E), jnp.float32) * sc, 'gate_b': jnp.zeros((E,), jnp.float32), 'w1': jax.random.normal(ks[2], (E, H, DFF), jnp.float32) * sc, 'b1': jnp.zeros((E, DFF), jnp.float32), 'w2': jax.random.normal(ks[3], (E, H, DFF), jnp.float32) * sc, 'b2': jnp.zeros((E, DFF), jnp.float32), 'wg': jax.random.normal(ks[4], (E, DFF, DFF), jnp.float32) * sc, 'bg': jnp.zeros((E, DFF), jnp.float32), 'w3': jax.random.normal(ks[5], (E, DFF, H), jnp.float32) * sc, 'b3': jnp.zeros((E, H), jnp.float32)}
    _L0_ffn_in = _L0_ffn_setup()
    _d = {'L0_attn_x': _L0_attn_in['x'], 'L0_attn_w_qkv': _L0_attn_in['w_qkv'], 'L0_attn_w_out': _L0_attn_in['w_out'], 'L0_attn_b_out': _L0_attn_in['b_out'], 'L0_ffn_gate_w': _L0_ffn_in['gate_w'], 'L0_ffn_gate_b': _L0_ffn_in['gate_b'], 'L0_ffn_w1': _L0_ffn_in['w1'], 'L0_ffn_b1': _L0_ffn_in['b1'], 'L0_ffn_w2': _L0_ffn_in['w2'], 'L0_ffn_b2': _L0_ffn_in['b2'], 'L0_ffn_wg': _L0_ffn_in['wg'], 'L0_ffn_bg': _L0_ffn_in['bg'], 'L0_ffn_w3': _L0_ffn_in['w3'], 'L0_ffn_b3': _L0_ffn_in['b3']}
    _x0 = _d['L0_attn_x']
    _d['L0_attn_x'] = jax.random.normal(jax.random.fold_in(jax.random.key(seed), 1), (4, 512, 128), dtype=_x0.dtype)
    del _x0
    return _d

def reference(L0_attn_x, L0_attn_w_qkv, L0_attn_w_out, L0_attn_b_out, L0_ffn_gate_w, L0_ffn_gate_b, L0_ffn_w1, L0_ffn_b1, L0_ffn_w2, L0_ffn_b2, L0_ffn_wg, L0_ffn_bg, L0_ffn_w3, L0_ffn_b3):

    def _L0_attn_ref(x, w_qkv, w_out, b_out):
        import jax, jax.numpy as jnp
        import numpy as np
        B, S, D_IN = (2, 256, 128)
        D_OUT, H, WINDOW = (128, 16, 64)
        HD = D_OUT // H
        b, s, _ = x.shape
        qkv = jnp.einsum('bsi,oi->bso', x, w_qkv)
        q, k, v = jnp.split(qkv, 3, axis=-1)

        def heads(t):
            return t.reshape(b, s, H, HD).transpose(0, 2, 1, 3)
        q, k, v = (heads(q), heads(k), heads(v))
        scores = jnp.einsum('bhqd,bhkd->bhqk', q, k) / jnp.sqrt(jnp.asarray(HD, x.dtype))
        i = jnp.arange(s)[:, None]
        j = jnp.arange(s)[None, :]
        allowed = (j <= i) & (i - j < WINDOW)
        scores = jnp.where(allowed[None, None], scores, jnp.asarray(-jnp.inf, x.dtype))
        attn = jax.nn.softmax(scores, axis=-1)
        ctx = jnp.einsum('bhqk,bhkd->bhqd', attn, v)
        ctx = ctx.transpose(0, 2, 1, 3).reshape(b, s, D_OUT)
        return jnp.einsum('bso,po->bsp', ctx, w_out) + b_out

    def _L0_ffn_ref(x, gate_w, gate_b, w1, b1, w2, b2, wg, bg, w3, b3):
        import jax, jax.numpy as jnp
        import numpy as np
        B, S, H = (2, 128, 128)
        DFF = 256
        E = 8
        TOPK = 2

        def _expert_ffn(x, w1, b1, w2, b2, wg, bg, w3, b3):
            x1 = jnp.einsum('bsh,hf->bsf', x, w1) + b1
            x2 = jnp.einsum('bsh,hf->bsf', x, w2) + b2
            z = x1 * x2
            s = jax.nn.silu(jnp.einsum('bsf,fg->bsg', z, wg) + bg)
            return jnp.einsum('bsg,gh->bsh', s, w3) + b3
        logits = jnp.einsum('bsh,he->bse', x, gate_w) + gate_b
        topv, topi = jax.lax.top_k(logits, TOPK)
        probs = jax.nn.softmax(topv, axis=-1)
        out = jnp.zeros_like(x)
        for e in range(E):
            we = jnp.sum(probs * (topi == e), axis=-1)
            y = _expert_ffn(x, w1[e], b1[e], w2[e], b2[e], wg[e], bg[e], w3[e], b3[e])
            out = out + we[..., None] * y
        return out
    x = L0_attn_x
    x = _layernorm(x + _L0_attn_ref(x, L0_attn_w_qkv, L0_attn_w_out, L0_attn_b_out), axis=-1)
    x = _layernorm(x + _L0_ffn_ref(x, L0_ffn_gate_w, L0_ffn_gate_b, L0_ffn_w1, L0_ffn_b1, L0_ffn_w2, L0_ffn_b2, L0_ffn_wg, L0_ffn_bg, L0_ffn_w3, L0_ffn_b3), axis=-1)
    return x

_drawn_inputs = setup_inputs


def setup_inputs(seed=0):
    import zlib

    import numpy as np

    out = dict(_drawn_inputs(seed))
    spreads = {'L0_ffn_gate_b': (0.0, 0.1),
     'L0_ffn_b1': (0.0, 0.8),
     'L0_ffn_b2': (0.0, 0.8),
     'L0_ffn_bg': (0.0, 0.7),
     'L0_ffn_b3': (0.0, 0.8)}
    factors = {'L0_ffn_w1': 8.0, 'L0_ffn_w2': 8.0, 'L0_ffn_wg': 8.0, 'L0_ffn_w3': 4.668}
    for name, (base, spread) in spreads.items():
        noise = np.random.default_rng([zlib.crc32(name.encode()), seed]).standard_normal(out[name].shape)
        drawn = base * np.exp(spread * noise) if base else spread * noise
        out[name] = jnp.asarray(drawn.astype(out[name].dtype))
    for name, factor in factors.items():
        out[name] = (out[name] * factor).astype(out[name].dtype)
    return out
```

```python
from contextlib import ExitStack

import concourse.bass as bass
from concourse import mybir

F32 = mybir.dt.float32
F32R = mybir.dt.float32r
BF16 = mybir.dt.bfloat16
I32 = mybir.dt.int32
U32 = mybir.dt.uint32
ALU = mybir.AluOpType
ACT = mybir.ActivationFunctionType
AX_X = mybir.AxisListType.X

P = 128
HEADS = 16
HD = 8
WINDOW = 64
QT = 64
UNIT = 256
HALO = WINDOW
KEYS = UNIT + HALO
WIN = UNIT // QT
MASKED = -1.0e30
EPS = 1e-5
ROW = P + 2


def count(t, per, add):
    g, c = t
    return g * (4 * per) + (c * per + add)


def wait(eng, sem, value):
    if not (isinstance(value, int) and value <= 0):
        eng.wait_ge(sem, value)


def rounds(t, per):
    g, c = t
    return g * per + (c // 4 + 1) * per


def tile_count(n, per, add):
    g, c = n
    return g * (8 * per) + (c * per + add)


def tile_rounds(n, per):
    g, c = n
    return g * per + (c // 8 + 1) * per


def wait_apart(eng, reg, met, sem, value):
    if not isinstance(value, int):
        eng.reg_mov(reg, value)
        eng.wait_ge(met, 1)
        eng.wait_ge(sem, reg)
    else:
        wait(eng, sem, value)


def later(t, d):
    return (t[0], t[1] + d)


def moe_layer_program(nc, x, w_qkv, w_out, b_out, gate_w, gate_b, w1, b1, w2, b2, wg, bg, w3, b3, out):
    B, S, D = x.shape
    E, _, F = w1.shape
    TOKENS = B * S
    STEPS = TOKENS // P
    PER_BATCH = S // P
    UNITS = TOKENS // UNIT
    SCALE = float(HD) ** -0.5
    assert D == P and HEADS * HD == D and PER_BATCH == 4 and E == 8 and F == 2 * P
    ASSIGNED = 2 * TOKENS
    TILES = ASSIGNED // P + E - 1
    REGION = TOKENS + P
    SPARE = E * REGION
    NOWHERE = 1 << 20

    x_rows = x.rearrange("b s d -> (b s) d")
    out_rows = out.rearrange("b s d -> (b s) d")
    q_scratch = nc.dram_tensor("q_scratch", (2, 2, P, UNIT), F32, kind="Internal").ap()
    k_scratch = nc.dram_tensor("k_scratch", (2, 2, P, KEYS), F32, kind="Internal").ap()
    routed = nc.dram_tensor("routed", (SPARE + P, ROW), F32, kind="Internal").ap()
    expert_out = nc.dram_tensor("expert_out", (ASSIGNED, D), F32, kind="Internal").ap()

    with ExitStack() as ctx:
        def sb(name, shape, dt=F32):
            return ctx.enter_context(nc.sbuf_tensor(name, shape, dt))

        def sem(name):
            return ctx.enter_context(nc.semaphore(name))

        bank = [ctx.enter_context(nc.psum_tensor(f"bank{i}", [P, 512], F32)) for i in range(8)]
        s_bank = bank[0:2]
        t_bank = bank[2:4]
        o_bank = bank[4]
        small = bank[5]
        pj0, pj1 = bank[6], bank[7]
        xt_bank, up_bank, zt_bank, gate_bank, at_bank, down_bank = bank[0:5] + [bank[6]]

        ident = sb("ident", [P, P])
        ident_b = sb("ident_b", [P, P], BF16)
        mask_f = sb("mask_f", [P, 2, P])
        mask_q = sb("mask_q", [P, 2, P], BF16)
        shift_w = sb("shift_w", [P, 2, 2, P], F32R)
        delta = sb("delta", [P, QT])
        below = sb("below", [P, P], BF16)
        ones_b = sb("ones_b", [P, P], BF16)
        head_of = sb("head_of", [P, HEADS])
        half_col = sb("half_col", [P, 2])
        slot_col = sb("slot_col", [P, 8])
        expert_iota = sb("expert_iota", [P, E])
        expert_base = sb("expert_base", [P, E])
        dest_i = sb("dest_i", [P, STEPS, 2], I32)
        minus_half = sb("minus_half", [P, 1])
        minus_one = sb("minus_one", [P, 1])
        w_rows = sb("w_rows", [P, 4, P])
        wo_rows = sb("wo_rows", [P, 2, QT])
        wT = sb("wT", [P, 3, P])
        woT = sb("woT", [QT, 2, P])
        gate = sb("gate", [P, E])
        gate_bias = sb("gate_bias", [P, E])
        bo = sb("bo", [P, P])
        x_all = sb("x_all", [P, STEPS, P])
        x_unit = [sb(f"x_unit{i}", [P, 2, P]) for i in range(2)]
        xT = [sb(f"xT{i}", [P, KEYS]) for i in range(2)]
        q_parts = sb("q_parts", [P, 2, UNIT], F32R)
        k_parts = sb("k_parts", [P, 2, KEYS], F32R)
        q_halves = [sb(f"q_halves{i}", [P, WIN, 2, QT], F32R) for i in range(2)]
        k_slots = [sb(f"k_slots{i}", [P, 8, KEYS], F32R) for i in range(2)]
        q_stack = [sb(f"q_stack{i}", [P, 4, 4, UNIT], F32R) for i in range(2)]
        k_stack = [sb(f"k_stack{i}", [P, 4, KEYS], F32R) for i in range(2)]
        v_aug = [sb(f"v_aug{i}", [P, WIN, HEADS, HD + 1]) for i in range(2)]
        top = [sb(f"top{a}", [P, 8]) for a in range(2)]
        shift = [[sb(f"shift{a}{h}", [P, 8, QT], F32R) for h in range(2)] for a in range(2)]
        probs = [[sb(f"probs{i}{a}", [P, HEADS * QT]) for a in range(2)] for i in range(2)]
        o_den = sb("o_den", [P, 2, 8])
        o_norm = sb("o_norm", [P, 2, 8, HD])
        oT = sb("oT", [QT, 2, 2, QT])
        res = sb("res", [P, P])
        stats = sb("stats", [P, 6])
        mean_var = sb("mean_var", [P, 2])
        inv_std = sb("inv_std", [P, 3])
        rows = [sb(f"rows{i}", [P, 2, ROW]) for i in range(4)]
        x1_all = sb("x1_all", [P, STEPS, P])
        x1T = sb("x1T", [P, P])
        logits = sb("logits", [P, E])
        best = sb("best", [P, 8])
        best_at = sb("best_at", [P, 8], U32)
        gap = sb("gap", [P, 4])
        chosen = sb("chosen", [P, 2, E])
        picked = sb("picked", [P, E], BF16)
        before = [sb(f"before{i}", [P, E], BF16) for i in range(2)]
        place_e = sb("place_e", [P, E])
        place_2 = sb("place_2", [P, 2, E])
        place_f = sb("place_f", [P, 2])
        place = [sb(f"place{i}", [P, 2], I32) for i in range(4)]

        w_up = sb("w_up", [P, E, 2, F])
        w_gate = sb("w_gate", [P, E, 2, F])
        w_down = sb("w_down", [P, E, 2, P])
        b_up = sb("b_up", [P, E, 2, F])
        b_gate = sb("b_gate", [P, E, F])
        b_down = sb("b_down", [P, E, P])
        pad = sb("pad", [P, ROW])
        steps16 = sb("steps16", [1, 16])
        tile_at = sb("tile_at", [1, TILES])
        tile_row0 = sb("tile_row0", [1, TILES])
        iota_i = sb("iota_i", [1, TILES], I32)
        upto = sb("upto", [1, E, E])
        total = sb("total", [1, E])
        need = sb("need", [1, E])
        need_16 = x_all[0:1, 0, :].rearrange("p (e n) -> p e n", e=E)
        ends = sb("ends", [1, E])
        ends_2 = x_all[0:1, 1, 0:E * E].rearrange("p (e n) -> p e n", e=E)
        passed, jumps = (x_all[0:1, i:i + 3, :].rearrange("p a n -> p (a n)")[:, 0:TILES * E].rearrange(
            "p (t e) -> p t e", e=E) for i in (2, 5))
        jump = sb("jump", [1, E])
        table_f = x_all[0:1, 8, 0:2 * TILES].rearrange("p (a t) -> p a t", a=2)
        pad_f = sb("pad_f", [1, E])
        tile_expert = sb("tile_expert", [1, TILES], I32)
        tile_row = sb("tile_row", [1, TILES], I32)
        pad_row = sb("pad_row", [1, E], I32)
        tile_x = [rows[i // 2][:, i % 2, :] for i in range(8)]
        tile_xT = [x_unit[i][:, 0, :] for i in range(2)]
        up = w_rows[:, :, :].rearrange("p (a b) n -> p a (b n)", a=2)
        z = [x_all[:, 8 + 2 * i:10 + 2 * i, :].rearrange("p a n -> p (a n)") for i in range(2)]
        zT = [x_all[:, 12 + 2 * i:14 + 2 * i, :] for i in range(2)]
        old_v = [v[:, :, :, :].rearrange("p w h n -> p (w h n)") for v in v_aug]
        gate_in = [v[:, 0:F] for v in old_v]
        act = [v[:, F:2 * F] for v in old_v]
        actT = [t[:, 0:F].rearrange("p (c n) -> p c n", c=2) for t in xT]
        y_in = res
        y = [x_all[:, i, :] for i in range(8)]
        y_two = [probs[i][0][:, :].rearrange("p (t k n) -> p t k n", t=4, k=2) for i in range(2)]
        total_4 = [probs[i][1][:, 0:512].rearrange("p (t n) -> p t n", t=4) for i in range(2)]
        stats_4 = x_unit[0][:, 1, 0:24].rearrange("p (t n) -> p t n", t=4)
        mean_4 = x_unit[0][:, 1, 32:40].rearrange("p (t n) -> p t n", t=4)
        inv_4 = x_unit[1][:, 1, 0:12].rearrange("p (n t) -> p n t", n=3)
        half_4 = sb("half_4", [P, 4])
        out_4 = [probs[i][1][:, 512:1024].rearrange("p (t n) -> p t n", t=4) for i in range(2)]

        loaded = sem("loaded")
        experts_loaded = sem("experts_loaded")
        spare_written = sem("spare_written")
        totals_made = sem("totals_made")
        table_chain = sem("table_chain")
        padded = sem("padded")
        tile_loaded = [sem(f"tile_loaded{i}") for i in range(8)]
        tile_xT_made = sem("tile_xT_made")
        tile_xT_ready = sem("tile_xT_ready")
        up_made = sem("up_made")
        up_ready = sem("up_ready")
        z_ready = sem("z_ready")
        zT_made = sem("zT_made")
        zT_ready = sem("zT_ready")
        gate_made = sem("gate_made")
        gate_ready = sem("gate_ready")
        act_ready = sem("act_ready")
        actT_made = sem("actT_made")
        actT_ready = sem("actT_ready")
        down_made = sem("down_made")
        down_read = sem("down_read")
        y_ready = sem("y_ready")
        y_sent = [sem(f"y_sent{i}") for i in range(8)]
        all_sent = sem("all_sent")
        two_loaded = [sem(f"two_loaded{i}") for i in range(2)]
        end_chain = sem("end_chain")
        end_inv = sem("end_inv")
        end_sum = sem("end_sum")
        out_ready = sem("out_ready")
        const_ready = sem("const_ready")
        pool_const = sem("pool_const")
        dve_const = sem("dve_const")
        weights_T = sem("weights_T")
        weights_ready = sem("weights_ready")
        xb_ready = sem("xb_ready")
        x_loaded = [sem(f"x_loaded{i}") for i in range(2)]
        xT_made = sem("xT_made")
        xT_ready = sem("xT_ready")
        q_made = sem("q_made")
        q_hi = sem("q_hi")
        q_lo = sem("q_lo")
        k_made = sem("k_made")
        k_hi = sem("k_hi")
        k_lo = sem("k_lo")
        v_made = sem("v_made")
        v_ready = sem("v_ready")
        halves_ready = sem("halves_ready")
        slots_ready = sem("slots_ready")
        q_out = sem("q_out")
        k_out = sem("k_out")
        stacked = [sem(f"stacked{i}") for i in range(2)]
        s_filled = sem("s_filled")
        s_read = sem("s_read")
        top_ready = sem("top_ready")
        shift_ready = sem("shift_ready")
        t_filled = sem("t_filled")
        probs_ready = sem("probs_ready")
        o_filled = sem("o_filled")
        den_ready = sem("den_ready")
        o_ready = sem("o_ready")
        oT_made = sem("oT_made")
        oT_ready = sem("oT_ready")
        y_made = sem("y_made")
        res_chain = sem("res_chain")
        norm_chain = sem("norm_chain")
        x1_ready = sem("x1_ready")
        x1T_made = sem("x1T_made")
        x1T_ready = sem("x1T_ready")
        x1_kept = sem("x1_kept")
        logits_made = sem("logits_made")
        route_chain = sem("route_chain")
        gap_ready = sem("gap_ready")
        gap_exp = sem("gap_exp")
        weight_chain = sem("weight_chain")
        rank_made = sem("rank_made")
        place_chain = sem("place_chain")
        before_ready = sem("before_ready")
        scattered = [sem(f"scattered{i}") for i in range(4)]
        rows_free = [sem(f"rows_free{i}") for i in range(4)]
        done = sem("done")

        block = ctx.enter_context(nc.Block())

        FIRST, LAST = -3, STEPS + 2

        def run_slots(eng, slot):
            for s in range(FIRST, 4):
                slot((0, s), s)
            with eng.Fori(1, STEPS // 4 - 1) as g:
                for c in range(4):
                    slot((g, c), None)
            for s in range(STEPS - 4, LAST + 1):
                slot((0, s), s)

        def has(s, lo, hi):
            return s is None or lo <= s <= hi

        def run_tiles(eng, slot):
            first = 5
            loops = (TILES - 4 - first) // 8
            for s in range(-1, first):
                slot((0, s), s)
            with eng.Fori(0, loops) as g:
                for c in range(first, first + 8):
                    slot((g, c), None)
            for s in range(first + 8 * loops, TILES + 4):
                slot((0, s), s)

        def tile_value(eng, table, n, most):
            g, c = n
            at = table[0:1, c:c + 1] if isinstance(g, int) else table[0:1, bass.ds(g * 8 + c, 1)]
            return eng.value_load(at, min_val=0, max_val=most)

        def of_expert(w, e):
            part = w[:, bass.ds(e, 1)]
            return part.rearrange("p o a n -> p (o a n)") if len(part.shape) == 4 else part.rearrange("p o n -> p (o n)")

        def unit_at(t, d):
            g, c = t
            assert (c + d) % 2 == 0
            return g, (c + d) // 2

        def ucount(u, per, add):
            g, c = u
            return g * (2 * per) + (c * per + add)

        def pcount(u, per):
            g, c = u
            return g * per + (c // 2 + 1) * per

        @block.sync
        def _(eng):
            wait_value = eng.alloc_register("wait_value")
            eng.dma_start(w_rows[:, 0:3, :], w_qkv.rearrange("(c p) i -> p c i", p=P)).then_inc(loaded, 16)
            eng.dma_start(w_rows[:, 3, :], w_out).then_inc(loaded, 16)
            eng.dma_start(gate[:, :], gate_w).then_inc(loaded, 16)
            eng.dma_start(gate_bias[:, :], gate_b.rearrange("(o e) -> o e", o=1).broadcast_to([P, E])).then_inc(loaded, 16)
            eng.dma_start(bo[:, :], b_out.rearrange("(o e) -> o e", o=1).broadcast_to([P, P])).then_inc(loaded, 16)

            def load_unit(u):
                g, c = u
                i = c % 2
                wait(eng, xT_made, ucount(u, 1, -1))
                first = g * (2 * UNIT) + c * UNIT
                src = x_rows[bass.ds(first, UNIT), :] if not isinstance(g, int) else x_rows[first:first + UNIT, :]
                eng.dma_start(x_unit[i][:, :, :], src.rearrange("(j p) d -> p j d", p=P)).then_inc(x_loaded[i], 16)

            load_unit((0, 0))
            load_unit((0, 1))
            eng.dma_start(x_all[:, :, :], x_rows.rearrange("(t p) d -> p t d", p=P)).then_inc(loaded, 16)

            def slot(t, s):
                if s == 0:
                    for c, (w, b) in enumerate(((w1, b1), (w2, b2))):
                        eng.dma_start(w_up[:, :, c, :], w.rearrange("e h f -> h e f")).then_inc(experts_loaded, 16)
                        eng.dma_start(b_up[:, :, c, :], b.unsqueeze(0).broadcast_to([P, E, F])).then_inc(experts_loaded, 16)
                if s == 2:
                    for c in range(2):
                        eng.dma_start(w_gate[:, :, c, :], wg[:, P * c:P * c + P, :].rearrange("e f g -> f e g")).then_inc(experts_loaded, 16)
                        eng.dma_start(w_down[:, :, c, :], w3[:, P * c:P * c + P, :].rearrange("e f g -> f e g")).then_inc(experts_loaded, 16)
                    eng.dma_start(b_gate[:, :, :], bg.unsqueeze(0).broadcast_to([P, E, F])).then_inc(experts_loaded, 16)
                    eng.dma_start(b_down[:, :, :], b3.unsqueeze(0).broadcast_to([P, E, P])).then_inc(experts_loaded, 16)
                    eng.dma_start(routed[SPARE:SPARE + P, :], pad[:, :]).then_inc(spare_written, 16)
                if t[1] % 2 == 0 and has(s, 0, STEPS - 6):
                    load_unit(unit_at(t, 4))
                if t[1] % 2 and has(s, -3, STEPS - 5):
                    u = unit_at(t, 3)
                    i = u[1] % 2
                    wait_apart(eng, wait_value, const_ready, stacked[i], pcount(later(u, -2), 192))
                    wait(eng, q_hi, ucount(u, 1, 1))
                    wait(eng, q_lo, ucount(u, 1, 1))
                    eng.dma_start(q_scratch[i].rearrange("w f n -> f w n"),
                                  q_parts[:, :, :].bitcast(F32)).then_inc(q_out, 16)
                    wait(eng, k_hi, ucount(u, 1, 1))
                    wait(eng, k_lo, ucount(u, 1, 1))
                    eng.dma_start(k_scratch[i].rearrange("w f n -> f w n"),
                                  k_parts[:, :, :].bitcast(F32)).then_inc(k_out, 16)
                    if s is None or s >= 0:
                        wait_apart(eng, wait_value, const_ready, t_filled, count(t, 4, 4))
                    else:
                        eng.wait_ge(const_ready, 1)
                    eng.wait_ge(q_out, ucount(u, 16, 16))
                    for hh in range(4):
                        for dup in range(2):
                            eng.dma_start(
                                q_stack[i][64 * dup + hh:64 * dup + hh + 61:4, :, hh, :].bitcast(F32),
                                q_scratch[i].rearrange("w (d h g) n -> h (w d) g n", d=HD, h=4)[hh],
                            ).then_inc(stacked[i], 16)
                    eng.wait_ge(k_out, ucount(u, 16, 16))
                    for part in range(4):
                        eng.dma_start(
                            k_stack[i][32 * part:32 * part + 32, :, :].bitcast(F32),
                            k_scratch[i][part // 2].rearrange("(r g) n -> r g n", g=4),
                        ).then_inc(stacked[i], 16)
                if has(s, 4, STEPS + 2):
                    v = later(t, -4)
                    wait_apart(eng, wait_value, const_ready, scattered[v[1] % 4], rounds(v, 32))
                    eng.nop().then_inc(rows_free[v[1] % 4], 1)

            run_slots(eng, slot)
            eng.wait_ge(table_chain, 13)
            for e in range(E):
                at = eng.value_load(pad_row[0:1, e:e + 1], min_val=0, max_val=SPARE - P)
                eng.dma_start(routed[bass.ds(at, P), :], pad[:, :]).then_inc(padded, 16)
            eng.wait_ge(table_chain, 15)
            eng.wait_ge(padded, 16 * E)
            eng.wait_ge(spare_written, 16)
            for i in range(4):
                eng.wait_ge(scattered[i], 32 * STEPS // 4)

            def load_tile(n):
                i = n[1] % 8
                at = tile_value(eng, tile_row, n, SPARE)
                wait(eng, y_sent[i], tile_rounds(later(n, -8), 16))
                eng.dma_start(tile_x[i][:, :], routed[bass.ds(at, P), :]).then_inc(tile_loaded[i], 16)

            def tile_slot(n, s):
                if s == -1:
                    for c in range(2):
                        load_tile((0, c))
                if has(s, -1, TILES - 4):
                    load_tile(later(n, 3))

            run_tiles(eng, tile_slot)
            eng.wait_ge(all_sent, 1)

            def store(q):
                eng.wait_ge(out_ready, 4 * (q + 1))
                eng.dma_start(out_rows[512 * q:512 * q + 512, :].rearrange("(t p) d -> p t d", p=P),
                              out_4[q % 2][:, :, :]).then_inc(done, 16)

            for q in range(4):
                i = q % 2
                if q >= 2:
                    eng.wait_ge(end_sum, 2 * (q - 1))
                eng.dma_start(y_two[i][:, :, :, :],
                              expert_out[1024 * q:1024 * q + 1024, :].rearrange("(t p k) d -> p t k d", p=P, k=2)).then_inc(two_loaded[i], 16)
                if q:
                    store(q - 1)
            store(3)
            eng.wait_ge(done, 64)

        @block.gpsimd
        def _(eng):
            wait_value = eng.alloc_register("wait_value")
            n = [0]

            def step(ins):
                n[0] += 1
                ins.then_inc(pool_const, 1)
                eng.wait_ge(pool_const, n[0])

            step(eng.memset(ident[:, :], 0.0))
            step(eng.memset(delta[:, :], 0.0))
            step(eng.memset(mask_f[:, :, :], 0.0))
            step(eng.memset(ones_b[:, :], 1.0))
            step(eng.memset(minus_half[:, :], -0.5))
            step(eng.memset(minus_one[:, :], -1.0))
            step(eng.memset(xT[1][:, :], 0.0))
            step(eng.affine_select(out=ident[:, :], in_=ident[:, :], compare_op=ALU.not_equal, fill=1.0,
                                   base=0, pattern=[[-1, P]], channel_multiplier=1))
            step(eng.affine_select(out=below[:, :], in_=ones_b[:, :], compare_op=ALU.is_ge, fill=0.0,
                                   base=-1, pattern=[[1, P]], channel_multiplier=-1))
            for half in range(2):
                r = slice(64 * half, 64 * half + 64)
                step(eng.affine_select(out=delta[r, :], in_=delta[r, :], compare_op=ALU.not_equal, fill=1.0,
                                       base=0, pattern=[[-1, QT]], channel_multiplier=1))
                step(eng.affine_select(out=mask_f[r, :, :], in_=mask_f[r, :, :], compare_op=ALU.is_ge,
                                       fill=MASKED, base=-1, pattern=[[0, 2], [1, P]], channel_multiplier=-1))
                step(eng.affine_select(out=mask_f[r, :, :], in_=mask_f[r, :, :], compare_op=ALU.is_ge,
                                       fill=MASKED, base=QT, pattern=[[0, 2], [-1, P]], channel_multiplier=1))
                step(eng.affine_select(out=mask_f[r, 1, :], in_=mask_f[r, 1, :], compare_op=ALU.is_ge,
                                       fill=MASKED, base=-QT, pattern=[[1, P]], channel_multiplier=0))
            step(eng.tensor_copy(mask_q[:, :, :], mask_f[:, :, :]))
            step(eng.tensor_copy(ident_b[:, :], ident[:, :]))
            step(eng.iota(dest_i[:, :, :], pattern=[[2 * P, STEPS], [1, 2]], base=0, channel_multiplier=2))
            for half in range(2):
                r, o = slice(64 * half, 64 * half + 64), slice(64 - 64 * half, 128 - 64 * half)
                step(eng.memset(shift_w[r, half, :, :].bitcast(F32), -1.0))
                step(eng.tensor_copy(shift_w[o, half, :, :], mask_f[o, :, :]))
                for a in range(2):
                    step(eng.tensor_copy(shift[a][half][o, :, :], delta[o, :].unsqueeze(1).to_broadcast([64, 8, QT])))
            step(eng.memset(before[0][:, :], 0.0))
            step(eng.memset(pad[:, :], 0.0))
            step(eng.iota(pad[:, P:P + 1].bitcast(I32), pattern=[[0, 1]], base=NOWHERE, channel_multiplier=0))
            step(eng.memset(half_4[:, :], -0.5))
            step(eng.iota(iota_i[:, :], pattern=[[1, TILES]], base=0, channel_multiplier=0))
            step(eng.tensor_copy(tile_at[:, :], iota_i[:, 0:TILES]))
            step(eng.tensor_scalar(steps16[:, :], iota_i[:, 0:16], float(P), None, ALU.mult))
            step(eng.tensor_scalar(tile_row0[:, :], tile_at[:, :], float(P), None, ALU.mult))
            step(eng.memset(upto[:, :, :], 1.0))
            step(eng.affine_select(out=upto[:, :, :], in_=upto[:, :, :], compare_op=ALU.is_ge, fill=0.0,
                                   base=0, pattern=[[1, E], [-1, E]], channel_multiplier=0))
            for e in range(E):
                step(eng.memset(expert_iota[:, e:e + 1], float(e)))
                step(eng.memset(expert_base[:, e:e + 1], float(e * REGION)))
            for i in range(2):
                step(eng.memset(v_aug[i][:, :, :, HD:HD + 1], 1.0))
            step(eng.memset(q_stack[0][:, :, :, :].bitcast(F32), 0.0))
            step(eng.memset(q_stack[1][:, :, :, :].bitcast(F32), 0.0))
            eng.wait_ge(pool_const, n[0])
            eng.nop().then_inc(const_ready, 1)
            for i in range(4):
                eng.nop().then_inc(rows_free[i], 1)
            eng.wait_ge(loaded, 16 * 6)
            eng.tensor_tensor(x_all[:, :, :], x_all[:, :, :], bo[:, :].unsqueeze(1).to_broadcast([P, STEPS, P]),
                              ALU.add).then_inc(xb_ready, 1)
            eng.wait_ge(dve_const, 3)

            def key_slots(u, part):
                i = u[1] % 2
                if part == 0:
                    wait(eng, k_hi, ucount(u, 1, 1))
                    wait(eng, s_filled, ucount(u, 8, -8))
                sl = slice(4 * part, 4 * part + 4)
                eng.tensor_tensor(k_slots[i][:, sl, :],
                                  k_parts[:, 0, :].bitcast(F32).unsqueeze(1).to_broadcast([P, 4, KEYS]),
                                  slot_col[:, sl].unsqueeze(2).to_broadcast([P, 4, KEYS]),
                                  ALU.mult).then_inc(slots_ready, 1)

            def normalise(t):
                i = t[1] % 4
                wait_apart(eng, wait_value, const_ready, res_chain, count(t, 3, 3))
                eng.tensor_scalar(inv_std[:, 0:1], mean_var[:, 1:2], EPS, None, ALU.add).then_inc(norm_chain, 1)
                wait_apart(eng, wait_value, const_ready, x1_ready, count(t, 2, 0))
                eng.tensor_scalar(inv_std[:, 1:2], mean_var[:, 0:1], -1.0, None, ALU.mult).then_inc(norm_chain, 1)
                wait(eng, rows_free[i], rounds(t, 1))
                eng.wait_ge(norm_chain, count(t, 3, 2))
                eng.tensor_tensor(inv_std[:, 2:3], inv_std[:, 0:1], minus_half[:, :], ALU.pow).then_inc(norm_chain, 1)
                wait_apart(eng, wait_value, const_ready, norm_chain, count(t, 3, 3))
                eng.tensor_scalar(rows[i][:, :, 0:P], res[:, :].unsqueeze(1).to_broadcast([P, 2, P]),
                                  inv_std[:, 1:2], inv_std[:, 2:3], ALU.add, ALU.mult).then_inc(x1_ready, 1)
                g, c = t
                dest = dest_i[:, c, :] if isinstance(g, int) else dest_i[:, bass.ds(g * 4 + c, 1), :].rearrange("p o k -> p (o k)")
                eng.tensor_copy(rows[i][:, :, P:P + 1].bitcast(I32).rearrange("p k o -> p (k o)"), dest).then_inc(x1_ready, 1)

            def weights_of_two(t):
                i = t[1] % 4
                wait(eng, route_chain, count(t, 5, 3))
                wait(eng, weight_chain, count(t, 3, 0))
                eng.tensor_tensor(gap[:, 0:1], best[:, 1:2], best[:, 0:1], ALU.subtract).then_inc(gap_ready, 1)
                wait_apart(eng, wait_value, const_ready, gap_exp, count(t, 1, 1))
                eng.tensor_scalar(gap[:, 2:3], gap[:, 1:2], 1.0, None, ALU.add).then_inc(weight_chain, 1)
                eng.wait_ge(weight_chain, count(t, 3, 1))
                eng.tensor_tensor(rows[i][:, 0, P + 1:ROW], gap[:, 2:3], minus_one[:, :], ALU.pow).then_inc(weight_chain, 1)
                eng.wait_ge(weight_chain, count(t, 3, 2))
                eng.tensor_tensor(rows[i][:, 1, P + 1:ROW], gap[:, 1:2], rows[i][:, 0, P + 1:ROW],
                                  ALU.mult).then_inc(weight_chain, 1)

            def scatter(t):
                i = t[1] % 4
                wait_apart(eng, wait_value, const_ready, weight_chain, count(t, 3, 3))
                wait_apart(eng, wait_value, const_ready, x1_ready, count(t, 2, 2))
                wait_apart(eng, wait_value, const_ready, place_chain, count(t, 4, 4))
                for k in range(2):
                    eng.indirect_dma_start(
                        routed, bass.IndirectOffsetOnAxis(ap=place[i][:, k:k + 1], axis=0),
                        rows[i][:, k, :], None, bounds_check=SPARE + P - 1, oob_is_err=False).then_inc(scattered[i], 16)

            def slot(t, s):
                if has(s, 4, STEPS + 3):
                    scatter(later(t, -4))
                if has(s, 2, STEPS + 1):
                    normalise(later(t, -2))
                if t[1] % 2 and has(s, -3, STEPS - 5):
                    key_slots(unit_at(t, 3), 0)
                    key_slots(unit_at(t, 3), 1)
                if has(s, 3, STEPS + 2):
                    weights_of_two(later(t, -3))

            run_slots(eng, slot)
            scatter((0, STEPS - 1))

            def send(n):
                i = n[1] % 8
                wait_apart(eng, wait_value, const_ready, y_ready, tile_count(n, 1, 1))
                eng.indirect_dma_start(
                    expert_out, bass.IndirectOffsetOnAxis(ap=tile_x[i][:, P:P + 1].bitcast(I32), axis=0),
                    y[i][:, :], None, bounds_check=ASSIGNED - 1, oob_is_err=False).then_inc(y_sent[i], 16)

            def tile_slot(n, s):
                if has(s, 4, TILES + 3):
                    send(later(n, -4))

            run_tiles(eng, tile_slot)
            for i in range(8):
                eng.wait_ge(y_sent[i], 16 * ((TILES - 1 - i) // 8 + 1))
            eng.nop().then_inc(all_sent, 1)
            for q in range(4):
                eng.wait_ge(end_chain, 8 * (q + 1))
                if q:
                    eng.wait_ge(out_ready, 4 * q)
                eng.tensor_scalar(inv_4[:, 0, :], mean_4[:, :, 1], EPS, None, ALU.add).then_inc(end_inv, 1)
                eng.wait_ge(end_inv, 3 * q + 1)
                eng.tensor_tensor(inv_4[:, 1, :], inv_4[:, 0, :], half_4[:, :], ALU.pow).then_inc(end_inv, 1)
                eng.wait_ge(end_inv, 3 * q + 2)
                eng.tensor_tensor(inv_4[:, 2, :], mean_4[:, :, 0], inv_4[:, 1, :], ALU.mult).then_inc(end_inv, 1)

        @block.scalar
        def _(eng):
            eng.wait_ge(weights_T, 1)
            for c in range(2):
                eng.copy(wT[:, c, :].rearrange("p (d h g) -> p g h d", d=HD, h=4),
                         pj0[:, P * c:P * c + P].rearrange("p (g h d) -> p g h d", g=4, h=4)).then_inc(weights_ready, 1)
            eng.copy(wT[:, 2, :], pj0[:, 2 * P:3 * P]).then_inc(weights_ready, 1)
            eng.copy(woT[:, :, :], pj1[0:QT, 0:2 * P].rearrange("p (h n) -> p h n", h=2)).then_inc(weights_ready, 1)
            eng.wait_ge(const_ready, 1)
            eng.wait_ge(dve_const, 3)

            def tokens_T(u):
                i = u[1] % 2
                wait(eng, xT_made, ucount(u, 1, 1))
                wait(eng, k_made, ucount(u, 1, -1))
                wait(eng, v_made, ucount(u, 1, -1))
                wait(eng, xT_ready, ucount(u, 2, 0))
                eng.copy(xT[i][:, 0:HALO], xT[1 - i][:, UNIT:KEYS]).then_inc(xT_ready, 1)
                eng.copy(xT[i][:, HALO:KEYS], pj0[:, 0:UNIT]).then_inc(xT_ready, 1)

            def queries(u):
                i = u[1] % 2
                wait(eng, q_made, ucount(u, 1, 1))
                wait(eng, q_out, ucount(u, 16, 0))
                wait(eng, q_lo, ucount(u, 1, 0))
                wait(eng, halves_ready, ucount(u, 2, 0))
                eng.activation(q_parts[:, 0, :], pj1[:, 0:UNIT], ACT.Copy, scale=SCALE).then_inc(q_hi, 1)
                wait(eng, q_hi, ucount(u, 1, 1))
                wait(eng, s_filled, ucount(u, 8, -8))
                for half in range(2):
                    eng.activation(q_halves[i][:, :, half, :],
                                   q_parts[:, 0, :].bitcast(F32).rearrange("p (w q) -> p w q", w=WIN),
                                   ACT.Copy, scale=half_col[:, half:half + 1]).then_inc(halves_ready, 1)

            def keys(u):
                wait(eng, k_made, ucount(u, 1, 1))
                wait(eng, k_out, ucount(u, 16, 0))
                wait(eng, k_lo, ucount(u, 1, 0))
                wait(eng, slots_ready, ucount(u, 2, 0))
                eng.copy(k_parts[:, 0, :], pj0[:, 0:KEYS]).then_inc(k_hi, 1)

            def values(u):
                i = u[1] % 2
                wait(eng, v_made, ucount(u, 1, 1))
                wait(eng, o_filled, ucount(u, 2, -2))
                eng.copy(v_aug[i][:, :, :, 0:HD],
                         pj1[:, :].rearrange("p (w h d) -> p w h d", w=WIN, h=HEADS)).then_inc(v_ready, 1)

            def exps(t, a):
                for h in range(2):
                    wait(eng, t_filled, count(t, 4, 2 * a + h + 1))
                    if h == 0:
                        wait(eng, o_filled, count(t, 1, -1))
                    eng.activation(probs[t[1] % 2][a][:, 512 * h:512 * h + 512], t_bank[h][:, :],
                                   ACT.Exp).then_inc(probs_ready, 1)

            def slot(t, s):
                if has(s, 2, STEPS + 1):
                    v = later(t, -2)
                    wait(eng, oT_made, count(v, 1, 1))
                    wait(eng, y_made, count(v, 1, 0))
                    eng.copy(oT[:, :, :, :].rearrange("c h a q -> c a h q"),
                             small[0:QT, 0:256].rearrange("c (a h q) -> c a h q", a=2, h=2)).then_inc(oT_ready, 1)
                if has(s, 0, STEPS - 1):
                    exps(t, 0)
                if t[1] % 2 and has(s, -3, STEPS - 5):
                    tokens_T(unit_at(t, 3))
                if t[1] % 2 == 0 and has(s, 0, STEPS - 2):
                    values(unit_at(t, 0))
                if has(s, 3, STEPS + 2):
                    v = later(t, -3)
                    wait(eng, x1T_made, count(v, 1, 1))
                    wait(eng, logits_made, count(v, 1, 0))
                    eng.copy(x1T[:, :], small[:, 384:512]).then_inc(x1T_ready, 1)
                if t[1] % 2 and has(s, -3, STEPS - 5):
                    queries(unit_at(t, 3))
                if has(s, 0, STEPS - 1):
                    exps(t, 1)
                if t[1] % 2 and has(s, -3, STEPS - 5):
                    keys(unit_at(t, 3))
                if has(s, 3, STEPS + 2):
                    v = later(t, -3)
                    g, c = v
                    dst = x1_all[:, c, :] if isinstance(g, int) else x1_all[:, bass.ds(g * 4 + c, 1), :].rearrange("p o d -> p (o d)")
                    eng.copy(dst, rows[c % 4][:, 0, 0:P]).then_inc(x1_kept, 1)
                    wait(eng, gap_ready, count(v, 1, 1))
                    eng.activation(gap[:, 1:2], gap[:, 0:1], ACT.Exp).then_inc(gap_exp, 1)

            run_slots(eng, slot)

            def tile_slot(n, s):
                if has(s, -1, TILES - 2):
                    m = later(n, 1)
                    wait(eng, tile_xT_made, tile_count(m, 1, 1))
                    wait(eng, up_made, tile_count(m, 1, -1))
                    eng.copy(tile_xT[m[1] % 2][:, :], xt_bank[:, 0:P]).then_inc(tile_xT_ready, 1)
                if has(s, 1, TILES):
                    m = later(n, -1)
                    wait(eng, zT_made, tile_count(m, 1, 1))
                    wait(eng, gate_made, tile_count(m, 1, -1))
                    eng.copy(zT[m[1] % 2][:, :, :], zt_bank[:, 0:F].rearrange("p (c n) -> p c n", c=2)).then_inc(zT_ready, 1)
                if has(s, 3, TILES + 2):
                    m = later(n, -3)
                    wait(eng, actT_made, tile_count(m, 1, 1))
                    wait(eng, down_made, tile_count(m, 1, -1))
                    eng.copy(actT[m[1] % 2][:, :, :], at_bank[:, 0:F].rearrange("p (c n) -> p c n", c=2)).then_inc(actT_ready, 1)
                if has(s, 2, TILES + 1):
                    m = later(n, -2)
                    wait(eng, gate_ready, tile_count(m, 1, 1))
                    wait(eng, actT_made, tile_count(m, 1, -1))
                    eng.activation(act[m[1] % 2][:, :], gate_in[m[1] % 2][:, :], ACT.Silu).then_inc(act_ready, 1)

            run_tiles(eng, tile_slot)

        @block.vector
        def _(eng):
            wait_value = eng.alloc_register("wait_value")
            eng.wait_ge(const_ready, 1)
            eng.tensor_reduce(head_of[:, :], ident[:, :].rearrange("p (d f) -> p f d", d=HD), AX_X,
                              ALU.add).then_inc(dve_const, 1)
            eng.wait_ge(dve_const, 1)
            eng.tensor_reduce(half_col[:, :], head_of[:, :].rearrange("p (h s l) -> p s h l", h=4, s=2),
                              mybir.AxisListType.XY, ALU.add).then_inc(dve_const, 1)
            eng.tensor_reduce(slot_col[:, :].rearrange("p (l h) -> p l h", l=2),
                              head_of[:, :].rearrange("p (h s l) -> p l h s", h=4, s=2), AX_X,
                              ALU.add).then_inc(dve_const, 1)
            eng.wait_ge(loaded, 16 * 6)
            eng.tensor_copy(wo_rows[:, :, :].rearrange("p h (k d) -> p h k d", k=8),
                            w_rows[:, 3, :].rearrange("p (k h d) -> p h k d", k=8, h=2)).then_inc(dve_const, 1)

            def maxima(t, a):
                wait(eng, shift_ready, count(t, 4, 2 * a - 2))
                for h in range(2):
                    wait(eng, s_filled, count(t, 4, 2 * a + h + 1))
                    eng.tensor_reduce(top[a][:, 4 * h:4 * h + 4],
                                      s_bank[h][:, :].rearrange("p (s k) -> p s k", s=4), AX_X,
                                      ALU.max).then_inc(s_read, 1)
                wait(eng, t_filled, count(t, 4, 2 * a + 2 - 4))
                eng.wait_ge(s_read, count(t, 4, 2 * a + 2))
                for half in range(2):
                    r = slice(64 * half, 64 * half + 64)
                    eng.tensor_tensor(shift[a][half][r, :, :], top[a][r, :].unsqueeze(2).to_broadcast([64, 8, QT]),
                                      delta[r, :].unsqueeze(1).to_broadcast([64, 8, QT]),
                                      ALU.mult).then_inc(shift_ready, 1)

            def normalise_heads(t):
                wait(eng, o_filled, count(t, 1, 1))
                wait(eng, oT_made, count(t, 1, 0))
                wait(eng, o_ready, count(t, 2, 0))
                o = o_bank[:, 0:288].rearrange("p (a h n) -> p a h n", a=2, h=8)
                for half in range(2):
                    r, c = slice(64 * half, 64 * half + 64), 9 * half
                    eng.reciprocal(o_den[r, :, :], o[r, :, :, c + HD:c + HD + 1].rearrange("p a h o -> p a (h o)")).then_inc(den_ready, 1)
                eng.wait_ge(den_ready, count(t, 2, 2))
                for half in range(2):
                    r, c = slice(64 * half, 64 * half + 64), 9 * half
                    eng.tensor_tensor(o_norm[r, :, :, :], o[r, :, :, c:c + HD],
                                      o_den[r, :, :].unsqueeze(3).to_broadcast([64, 2, 8, HD]),
                                      ALU.mult).then_inc(o_ready, 1)

            def residual(t):
                g, c = t
                wait(eng, y_made, count(t, 1, 1))
                wait(eng, x1_ready, count(t, 2, 0))
                wait(eng, res_chain, count(t, 3, 0))
                xs = x_all[:, c, :] if isinstance(g, int) else x_all[:, bass.ds(g * 4 + c, 1), :].rearrange("p o d -> p (o d)")
                eng.tensor_tensor(res[:, :], small[:, 256:384], xs, ALU.add).then_inc(res_chain, 1)
                eng.wait_ge(res_chain, count(t, 3, 1))
                eng.bn_stats(stats[:, :], res[:, :]).then_inc(res_chain, 1)
                wait_apart(eng, wait_value, const_ready, res_chain, count(t, 3, 2))
                eng.bn_aggr(mean_var[:, :], stats[:, :]).then_inc(res_chain, 1)

            def split_queries(u):
                wait(eng, q_hi, ucount(u, 1, 1))
                eng.scalar_tensor_tensor(out=q_parts[:, 1, :], in0=pj1[:, 0:UNIT], scalar=SCALE,
                                         in1=q_parts[:, 0, :].bitcast(F32), op0=ALU.mult,
                                         op1=ALU.subtract).then_inc(q_lo, 1)

            def split_keys(u):
                wait(eng, k_hi, ucount(u, 1, 1))
                eng.tensor_tensor(k_parts[:, 1, :], pj0[:, 0:KEYS], k_parts[:, 0, :].bitcast(F32),
                                  ALU.subtract).then_inc(k_lo, 1)

            def route(t):
                i = t[1] % 2
                wait(eng, logits_made, count(t, 1, 1))
                wait(eng, gap_ready, count(t, 1, 0))
                eng.tensor_tensor(logits[:, :], small[:, 0:E], gate_bias[:, :], ALU.add).then_inc(route_chain, 1)
                wait_apart(eng, wait_value, const_ready, route_chain, count(t, 5, 1))
                eng.max(best[:, :], logits[:, :]).then_inc(route_chain, 1)
                wait_apart(eng, wait_value, const_ready, route_chain, count(t, 5, 2))
                eng.max_index(best_at[:, :], best[:, :], logits[:, :]).then_inc(route_chain, 1)
                eng.wait_ge(route_chain, count(t, 5, 3))
                wait(eng, place_chain, count(t, 4, 0))
                eng.tensor_tensor(chosen[:, :, :], expert_iota[:, :].unsqueeze(1).to_broadcast([P, 2, E]),
                                  best_at[:, 0:2].unsqueeze(2).to_broadcast([P, 2, E]),
                                  ALU.is_equal).then_inc(route_chain, 1)
                eng.wait_ge(route_chain, count(t, 5, 4))
                wait(eng, rank_made, count(t, 1, 0))
                wait(eng, before_ready, count(t, 1, 0))
                eng.tensor_tensor(picked[:, :], chosen[:, 0, :], chosen[:, 1, :], ALU.add).then_inc(route_chain, 1)

            def places(t):
                i = t[1] % 2
                wait(eng, rank_made, count(t, 1, 1))
                eng.tensor_tensor(place_e[:, :], small[:, E:2 * E], expert_base[:, :], ALU.add).then_inc(place_chain, 1)
                eng.wait_ge(route_chain, count(t, 5, 5))
                eng.tensor_tensor(before[1 - i][:, :], before[i][:, :], picked[:, :], ALU.add).then_inc(before_ready, 1)
                eng.wait_ge(place_chain, count(t, 4, 1))
                eng.tensor_tensor(place_2[:, :, :], chosen[:, :, :], place_e[:, :].unsqueeze(1).to_broadcast([P, 2, E]),
                                  ALU.mult).then_inc(place_chain, 1)
                eng.wait_ge(place_chain, count(t, 4, 2))
                eng.tensor_reduce(place_f[:, :], place_2[:, :, :], AX_X, ALU.add).then_inc(place_chain, 1)
                eng.wait_ge(place_chain, count(t, 4, 3))
                wait(eng, rows_free[t[1] % 4], rounds(t, 1))
                eng.tensor_copy(place[t[1] % 4][:, :], place_f[:, :]).then_inc(place_chain, 1)

            def slot(t, s):
                if has(s, -1, STEPS - 2):
                    maxima(later(t, 1), 0)
                if has(s, 2, STEPS + 1):
                    residual(later(t, -2))
                if t[1] % 2 and has(s, -3, STEPS - 5):
                    split_queries(unit_at(t, 3))
                if has(s, -1, STEPS - 2):
                    maxima(later(t, 1), 1)
                if has(s, 3, STEPS + 2):
                    route(later(t, -3))
                if t[1] % 2 and has(s, -3, STEPS - 5):
                    split_keys(unit_at(t, 3))
                if has(s, 1, STEPS):
                    normalise_heads(later(t, -1))
                if has(s, 3, STEPS + 2):
                    places(later(t, -3))

            run_slots(eng, slot)

            links = [0]

            def link(ins):
                links[0] += 1
                ins.then_inc(table_chain, 1)
                eng.wait_ge(table_chain, links[0])

            eng.wait_ge(totals_made, 1)
            link(eng.tensor_copy(total[:, :], small[0:1, 0:E]))
            link(eng.tensor_tensor(need_16[:, :, :], total[:, :].unsqueeze(2).to_broadcast([1, E, 16]),
                                   steps16[:, :].unsqueeze(1).to_broadcast([1, E, 16]), ALU.is_gt))
            link(eng.tensor_reduce(need[:, :], need_16[:, :, :], AX_X, ALU.add))
            link(eng.tensor_tensor(ends_2[:, :, :], upto[:, :, :], need[:, :].unsqueeze(1).to_broadcast([1, E, E]), ALU.mult))
            link(eng.tensor_reduce(ends[:, :], ends_2[:, :, :], AX_X, ALU.add))
            link(eng.tensor_tensor(passed[:, :, :], ends[:, :].unsqueeze(1).to_broadcast([1, TILES, E]),
                                   tile_at[:, :].unsqueeze(2).to_broadcast([1, TILES, E]), ALU.is_le))
            link(eng.tensor_reduce(table_f[:, 0, :], passed[:, :, :], AX_X, ALU.add))
            link(eng.tensor_scalar(jump[:, :], need[:, :], -float(P), float(REGION), ALU.mult, ALU.add))
            link(eng.tensor_tensor(jumps[:, :, :], passed[:, :, :], jump[:, :].unsqueeze(1).to_broadcast([1, TILES, E]), ALU.mult))
            link(eng.tensor_reduce(table_f[:, 1, :], jumps[:, :, :], AX_X, ALU.add))
            link(eng.tensor_tensor(table_f[:, 1, :], table_f[:, 1, :], tile_row0[:, :], ALU.add))
            link(eng.tensor_tensor(pad_f[:, :], total[:, :], expert_base[0:1, :], ALU.add))
            link(eng.tensor_copy(pad_row[:, :], pad_f[:, :]))
            link(eng.tensor_scalar(tile_expert[:, :], table_f[:, 0, :], float(E - 1), None, ALU.min))
            link(eng.tensor_scalar(tile_row[:, :], table_f[:, 1, :], float(SPARE), None, ALU.min))
            eng.wait_ge(experts_loaded, 16 * 10)

            def tile_slot(n, s):
                if has(s, 0, TILES - 1):
                    i = n[1] % 2
                    e = tile_value(eng, tile_expert, n, E - 1)
                    wait(eng, up_made, tile_count(n, 1, 1))
                    wait(eng, z_ready, tile_count(n, 1, 0))
                    eng.tensor_tensor(up[:, :, :].rearrange("p a n -> p (a n)"), up_bank[:, :], of_expert(b_up, e),
                                      ALU.add).then_inc(up_ready, 1)
                    eng.wait_ge(up_ready, tile_count(n, 1, 1))
                    wait(eng, zT_made, tile_count(n, 1, -1))
                    eng.tensor_tensor(z[i][:, :], up[:, 0, :], up[:, 1, :], ALU.mult).then_inc(z_ready, 1)
                if has(s, 2, TILES + 1):
                    m = later(n, -2)
                    e = tile_value(eng, tile_expert, m, E - 1)
                    wait(eng, gate_made, tile_count(m, 1, 1))
                    wait(eng, act_ready, tile_count(m, 1, -1))
                    eng.tensor_tensor(gate_in[m[1] % 2][:, :], gate_bank[:, 0:F], of_expert(b_gate, e),
                                      ALU.add).then_inc(gate_ready, 1)
                if has(s, 4, TILES + 3):
                    m = later(n, -4)
                    e = tile_value(eng, tile_expert, m, E - 1)
                    wait(eng, down_made, tile_count(m, 1, 1))
                    wait(eng, y_ready, tile_count(m, 1, 0))
                    eng.tensor_tensor(y_in[:, :], down_bank[:, 0:P], of_expert(b_down, e), ALU.add).then_inc(down_read, 1)
                    eng.wait_ge(down_read, tile_count(m, 1, 1))
                    eng.tensor_scalar(y[m[1] % 8][:, :], y_in[:, :], tile_x[m[1] % 8][:, P + 1:ROW], None,
                                      ALU.mult).then_inc(y_ready, 1)

            run_tiles(eng, tile_slot)

            def finish(q):
                for j in range(4):
                    eng.wait_ge(end_inv, 3 * (q + 1))
                    eng.tensor_scalar(out_4[q % 2][:, j, :], total_4[q % 2][:, j, :], inv_4[:, 1, j:j + 1],
                                      inv_4[:, 2, j:j + 1], ALU.mult, ALU.subtract).then_inc(out_ready, 1)

            eng.wait_ge(x1_kept, STEPS)
            for q in range(4):
                i = q % 2
                if q >= 2:
                    eng.wait_ge(done, 16 * (q - 1))
                eng.wait_ge(two_loaded[i], 16 * (q // 2 + 1))
                eng.tensor_tensor(total_4[i][:, :, :], y_two[i][:, :, 0, :], y_two[i][:, :, 1, :], ALU.add).then_inc(end_sum, 1)
                eng.wait_ge(end_sum, 2 * q + 1)
                eng.tensor_tensor(total_4[i][:, :, :], total_4[i][:, :, :], x1_all[:, 4 * q:4 * q + 4, :], ALU.add).then_inc(end_sum, 1)
                eng.wait_ge(end_sum, 2 * q + 2)
                if q:
                    eng.wait_ge(end_inv, 3 * q)
                for j in range(4):
                    eng.bn_stats(stats_4[:, j, :], total_4[i][:, j, :]).then_inc(end_chain, 1)
                eng.wait_ge(end_chain, 8 * q + 4)
                for j in range(4):
                    eng.bn_aggr(mean_4[:, j, :], stats_4[:, j, :]).then_inc(end_chain, 1)
                finish(q)

        @block.tensor
        def _(eng):
            wait_value = eng.alloc_register("wait_value")
            eng.wait_ge(loaded, 16 * 6)
            eng.wait_ge(const_ready, 1)
            eng.wait_ge(dve_const, 4)
            for c in range(3):
                eng.transpose(pj0[:, P * c:P * c + P], w_rows[:, c, :], ident[:, :])
            for half in range(2):
                ins = eng.transpose(pj1[0:QT, P * half:P * half + P],
                                    wo_rows[:, half, :], ident[:, :])
            ins.then_inc(weights_T, 1)
            eng.wait_ge(weights_ready, 4)

            def tokens_T(u):
                g, c = u
                i = c % 2
                eng.wait_ge(x_loaded[i], pcount(u, 16))
                wait(eng, k_lo, ucount(u, 1, 0))
                wait(eng, k_hi, ucount(u, 1, 0))
                for j in range(2):
                    ins = eng.transpose(pj0[:, P * j:P * j + P], x_unit[i][:, j, :], ident[:, :])
                ins.then_inc(xT_made, 1)

            def queries(u):
                i = u[1] % 2
                wait(eng, xT_ready, ucount(u, 2, 2))
                wait(eng, v_ready, ucount(u, 1, -1))
                wait(eng, q_lo, ucount(u, 1, 0))
                eng.matmul(pj1[:, 0:UNIT], wT[:, 0, :], xT[i][:, HALO:KEYS]).then_inc(q_made, 1)

            def keys(u):
                i = u[1] % 2
                eng.matmul(pj0[:, 0:KEYS], wT[:, 1, :], xT[i][:, :]).then_inc(k_made, 1)

            def values(u, last):
                i = u[1] % 2
                wait(eng, q_lo, ucount(u, 1, 1 if last else 2))
                for w in range(WIN):
                    ins = eng.matmul(pj1[:, P * w:P * w + P], xT[i][:, QT * w:QT * w + P], wT[:, 2, :])
                ins.then_inc(v_made, 1)

            def max_scores(t, a):
                i, w = (t[1] // 2) % 2, 2 * (t[1] % 2) + a
                first = int(t[1] % PER_BATCH == 0 and a == 0)
                u = (t[0], t[1] // 2)
                wait(eng, halves_ready, ucount(u, 2, 2))
                wait(eng, slots_ready, ucount(u, 2, 2))
                for h in range(2):
                    wait(eng, s_read, count(t, 4, 2 * a + h - 1))
                    eng.matmul(s_bank[h][:, :], ident_b[:, :], mask_q[:, first:first + 1, :].to_broadcast([P, 4, P]),
                               start=True, stop=False)
                    eng.matmul(s_bank[h][:, :], q_halves[i][:, w, :, :],
                               k_slots[i][:, 4 * h:4 * h + 4, QT * w:QT * w + P],
                               start=False, stop=True).then_inc(s_filled, 1)

            def shifted_scores(t, a):
                i, w = (t[1] // 2) % 2, 2 * (t[1] % 2) + a
                first = int(t[1] % PER_BATCH == 0 and a == 0)
                u = (t[0], t[1] // 2)
                wait(eng, shift_ready, count(t, 4, 2 * a + 2))
                wait(eng, stacked[i], pcount(u, 192))
                for h in range(2):
                    wait(eng, probs_ready, count(t, 4, 2 * a + h - 1))
                    for l in range(2):
                        grp = 2 * h + l
                        eng.matmul(t_bank[h][:, 256 * l:256 * l + 256], k_stack[i][:, grp, QT * w:QT * w + P],
                                   q_stack[i][:, grp, :, QT * w:QT * w + QT], start=(l == 0), stop=False,
                                   skip_group_check=True)
                    eng.matmul(t_bank[h][:, :], shift_w[:, h, first, :], shift[a][h][:, :, :], start=False,
                               stop=True, skip_group_check=True).then_inc(t_filled, 1)

            def weighted_values(t, a):
                i, w = (t[1] // 2) % 2, 2 * (t[1] % 2) + a
                wait(eng, v_ready, ucount((t[0], t[1] // 2), 1, 1))
                wait(eng, probs_ready, count(t, 4, 2 * a + 2))
                if a == 0:
                    wait(eng, o_ready, count(t, 2, 0))
                for p in range(8):
                    c = 144 * a + 18 * p
                    ins = eng.matmul(o_bank[:, c:c + 18], probs[t[1] % 2][a][:, P * p:P * p + P],
                                     v_aug[i][:, w, 2 * p:2 * p + 2, :])
                if a == 1:
                    ins.then_inc(o_filled, 1)

            def heads_T(t):
                wait(eng, o_ready, count(t, 2, 2))
                wait_apart(eng, wait_value, const_ready, place_chain, count(t, 4, -7))
                for a in range(2):
                    ins = eng.transpose(small[0:QT, P * a:P * a + P],
                                        o_norm[:, a, :, :].rearrange("p h d -> p (h d)"), ident[:, :])
                ins.then_inc(oT_made, 1)

            def project_out(t):
                wait(eng, oT_ready, count(t, 1, 1))
                for half in range(2):
                    ins = eng.matmul(small[:, 256:384], oT[:, half, :, :], woT[:, half, :],
                                     start=(half == 0), stop=(half == 1))
                ins.then_inc(y_made, 1)

            def x1_T(t, last):
                wait(eng, x1_ready, count(t, 2, 1))
                if last:
                    wait(eng, place_chain, count(t, 4, -3))
                else:
                    wait(eng, res_chain, count(t, 3, 4))
                eng.transpose(small[:, 384:512], rows[t[1] % 4][:, 0, 0:P], ident[:, :]).then_inc(x1T_made, 1)

            def gate_logits(t):
                wait(eng, x1T_ready, count(t, 1, 1))
                eng.matmul(small[:, 0:E], x1T[:, :], gate[:, :]).then_inc(logits_made, 1)

            def ranks(t):
                i = t[1] % 2
                wait(eng, route_chain, count(t, 5, 5))
                wait(eng, before_ready, count(t, 1, 0))
                eng.matmul(small[:, E:2 * E], below[:, :], picked[:, :], start=True, stop=False)
                eng.matmul(small[:, E:2 * E], ones_b[:, :], before[i][:, :], start=False, stop=True).then_inc(rank_made, 1)

            def slot(t, s):
                odd = t[1] % 2 and has(s, -3, STEPS - 5)
                if has(s, -1, STEPS - 2):
                    max_scores(later(t, 1), 0)
                if has(s, 2, STEPS + 1):
                    heads_T(later(t, -2))
                if has(s, 0, STEPS - 1):
                    shifted_scores(t, 0)
                if odd:
                    tokens_T(unit_at(t, 3))
                if t[1] % 2 == 0 and has(s, 0, STEPS - 2):
                    values(unit_at(t, 0), s == STEPS - 2)
                if has(s, 1, STEPS):
                    weighted_values(later(t, -1), 0)
                if has(s, 2, STEPS + 1):
                    project_out(later(t, -2))
                if odd:
                    queries(unit_at(t, 3))
                if has(s, -1, STEPS - 2):
                    max_scores(later(t, 1), 1)
                if has(s, 3, STEPS + 2):
                    x1_T(later(t, -3), s == STEPS + 2)
                if has(s, 0, STEPS - 1):
                    shifted_scores(t, 1)
                if has(s, 3, STEPS + 2):
                    gate_logits(later(t, -3))
                if odd:
                    keys(unit_at(t, 3))
                if has(s, 1, STEPS):
                    weighted_values(later(t, -1), 1)
                if has(s, 3, STEPS + 2):
                    ranks(later(t, -3))

            run_slots(eng, slot)
            eng.wait_ge(place_chain, 4 * STEPS)
            eng.wait_ge(before_ready, STEPS)
            eng.matmul(small[:, 0:E], ones_b[:, :], before[0][:, :]).then_inc(totals_made, 1)
            eng.wait_ge(table_chain, 15)
            eng.wait_ge(experts_loaded, 16 * 10)

            def tile_slot(n, s):
                if has(s, -1, TILES - 2):
                    m = later(n, 1)
                    wait(eng, tile_loaded[m[1] % 8], tile_rounds(m, 16))
                    wait(eng, tile_xT_ready, tile_count(m, 1, 0))
                    eng.transpose(xt_bank[:, 0:P], tile_x[m[1] % 8][:, 0:P], ident[:, :]).then_inc(tile_xT_made, 1)
                if has(s, 0, TILES - 1):
                    e = tile_value(eng, tile_expert, n, E - 1)
                    wait(eng, tile_xT_ready, tile_count(n, 1, 1))
                    wait(eng, up_ready, tile_count(n, 1, 0))
                    eng.matmul(up_bank[:, :], tile_xT[n[1] % 2][:, :], of_expert(w_up, e)).then_inc(up_made, 1)
                if has(s, 1, TILES):
                    m = later(n, -1)
                    wait(eng, z_ready, tile_count(m, 1, 1))
                    wait(eng, zT_ready, tile_count(m, 1, 0))
                    for c in range(2):
                        ins = eng.transpose(zt_bank[:, P * c:P * c + P], z[m[1] % 2][:, P * c:P * c + P], ident[:, :])
                    ins.then_inc(zT_made, 1)
                if has(s, 2, TILES + 1):
                    m = later(n, -2)
                    e = tile_value(eng, tile_expert, m, E - 1)
                    wait(eng, zT_ready, tile_count(m, 1, 1))
                    wait(eng, gate_ready, tile_count(m, 1, 0))
                    for c in range(2):
                        ins = eng.matmul(gate_bank[:, 0:F], zT[m[1] % 2][:, c, :],
                                         w_gate[:, bass.ds(e, 1), c, :].rearrange("p o n -> p (o n)"),
                                         start=(c == 0), stop=(c == 1))
                    ins.then_inc(gate_made, 1)
                if has(s, 3, TILES + 2):
                    m = later(n, -3)
                    wait(eng, act_ready, tile_count(m, 1, 1))
                    wait(eng, actT_ready, tile_count(m, 1, 0))
                    for c in range(2):
                        ins = eng.transpose(at_bank[:, P * c:P * c + P], act[m[1] % 2][:, P * c:P * c + P], ident[:, :])
                    ins.then_inc(actT_made, 1)
                if has(s, 4, TILES + 3):
                    m = later(n, -4)
                    e = tile_value(eng, tile_expert, m, E - 1)
                    wait(eng, actT_ready, tile_count(m, 1, 1))
                    wait(eng, down_read, tile_count(m, 1, 0))
                    for c in range(2):
                        ins = eng.matmul(down_bank[:, 0:P], actT[m[1] % 2][:, c, :],
                                         w_down[:, bass.ds(e, 1), c, :].rearrange("p o n -> p (o n)"),
                                         start=(c == 0), stop=(c == 1))
                    ins.then_inc(down_made, 1)

            run_tiles(eng, tile_slot)


_INS = ["L0_attn_x", "L0_attn_w_qkv", "L0_attn_w_out", "L0_attn_b_out", "L0_ffn_gate_w", "L0_ffn_gate_b",
        "L0_ffn_w1", "L0_ffn_b1", "L0_ffn_w2", "L0_ffn_b2", "L0_ffn_wg", "L0_ffn_bg", "L0_ffn_w3", "L0_ffn_b3"]
_OUTS = [((4, 512, 128), "float32")]


def kernel(**inputs):
    import numpy as _np
    import concourse.bacc as _bacc
    from concourse import mybir as _mybir
    from concourse.bass_utils import run_bass_kernel_spmd as _run

    nc = _bacc.Bacc("TRN2", target_bir_lowering=False, num_devices=1)
    arrays, args = {}, []
    for name in _INS:
        a = _np.ascontiguousarray(inputs[name])
        arrays[f"in_{name}_dram"] = a
        args.append(nc.dram_tensor(f"in_{name}_dram", a.shape, _mybir.dt.from_np(a.dtype), kind="ExternalInput").ap())
    for i, (shape, dtype) in enumerate(_OUTS):
        dt = _mybir.dt.from_np(_np.dtype(dtype))
        args.append(nc.dram_tensor(f"out_{i}_dram", shape, dt, kind="ExternalOutput").ap())
    moe_layer_program(nc, *args)
    r = _run(nc, [arrays], core_ids=[0])
    return r.results[0]["out_0_dram"]
```

```python
from contextlib import ExitStack

import concourse.bass as bass
from concourse import mybir

F32 = mybir.dt.float32
F32R = mybir.dt.float32r
BF16 = mybir.dt.bfloat16
I32 = mybir.dt.int32
U32 = mybir.dt.uint32
ALU = mybir.AluOpType
ACT = mybir.ActivationFunctionType
AX_X = mybir.AxisListType.X

P = 128
HEADS = 16
HD = 8
WINDOW = 64
QT = 64
UNIT = 256
HALO = WINDOW
KEYS = UNIT + HALO
WIN = UNIT // QT
MASKED = -1.0e30
EPS = 1e-5
ROW = P + 2


def count(t, per, add):
    g, c = t
    return g * (4 * per) + (c * per + add)


def wait(eng, sem, value):
    if not (isinstance(value, int) and value <= 0):
        eng.wait_ge(sem, value)


def rounds(t, per):
    g, c = t
    return g * per + (c // 4 + 1) * per


def tile_count(n, per, add):
    g, c = n
    return g * (8 * per) + (c * per + add)


def tile_rounds(n, per):
    g, c = n
    return g * per + (c // 8 + 1) * per


def wait_apart(eng, reg, met, sem, value):
    if not isinstance(value, int):
        eng.reg_mov(reg, value)
        eng.wait_ge(met, 1)
        eng.wait_ge(sem, reg)
    else:
        wait(eng, sem, value)


def later(t, d):
    return (t[0], t[1] + d)


def moe_layer_program(nc, x, w_qkv, w_out, b_out, gate_w, gate_b, w1, b1, w2, b2, wg, bg, w3, b3, out):
    B, S, D = x.shape
    E, _, F = w1.shape
    TOKENS = B * S
    STEPS = TOKENS // P
    PER_BATCH = S // P
    UNITS = TOKENS // UNIT
    SCALE = float(HD) ** -0.5
    assert D == P and HEADS * HD == D and PER_BATCH == 4 and E == 8 == STEPS - 8 and F == 2 * P
    ASSIGNED = 2 * TOKENS
    TILES = ASSIGNED // P + E - 1
    REGION = TOKENS + P
    SPARE = E * REGION
    NOWHERE = 1 << 20

    x_rows = x.rearrange("b s d -> (b s) d")
    out_rows = out.rearrange("b s d -> (b s) d")
    q_scratch = nc.dram_tensor("q_scratch", (2, 2, P, UNIT), F32, kind="Internal").ap()
    k_scratch = nc.dram_tensor("k_scratch", (2, 2, P, KEYS), F32, kind="Internal").ap()
    routed = nc.dram_tensor("routed", (SPARE + P, ROW), F32, kind="Internal").ap()
    expert_out = nc.dram_tensor("expert_out", (ASSIGNED, D), F32, kind="Internal").ap()

    with ExitStack() as ctx:
        def sb(name, shape, dt=F32):
            return ctx.enter_context(nc.sbuf_tensor(name, shape, dt))

        def sem(name):
            return ctx.enter_context(nc.semaphore(name))

        bank = [ctx.enter_context(nc.psum_tensor(f"bank{i}", [P, 512], F32)) for i in range(8)]
        s_bank = bank[0:2]
        t_bank = bank[2:4]
        o_bank = bank[4]
        out_bank = bank[5]
        route_bank = bank[6]
        unit_bank = bank[7]
        xt_bank, up_bank, zt_bank, gate_bank, at_bank, down_bank = bank[0:5] + [bank[7]]

        ident = sb("ident", [P, P])
        ident_b = sb("ident_b", [P, P], BF16)
        mask_f = sb("mask_f", [P, 2, P])
        mask_q = sb("mask_q", [P, 2, P], BF16)
        shift_w = sb("shift_w", [P, 2, 2, P], F32R)
        delta = sb("delta", [P, QT])
        below = sb("below", [P, P], BF16)
        ones_b = sb("ones_b", [P, P], BF16)
        head_of = sb("head_of", [P, HEADS])
        half_col = sb("half_col", [P, 2])
        slot_col = sb("slot_col", [P, 8])
        expert_iota = sb("expert_iota", [P, E])
        expert_base = sb("expert_base", [P, E])
        dest_i = sb("dest_i", [P, STEPS, 2], I32)
        minus_half = sb("minus_half", [P, 1])
        minus_one = sb("minus_one", [P, 1])
        w_rows = sb("w_rows", [P, 4, P])
        wo_rows = sb("wo_rows", [P, 2, QT])
        wT = sb("wT", [P, 3, P])
        woT = sb("woT", [QT, 2, P])
        gate = sb("gate", [P, E])
        gate_bias = sb("gate_bias", [P, E])
        bo = sb("bo", [P, P])
        x_all = sb("x_all", [P, STEPS, P])
        x_unit = [sb(f"x_unit{i}", [P, 2, P]) for i in range(2)]
        xT = [sb(f"xT{i}", [P, KEYS]) for i in range(2)]
        q_parts = sb("q_parts", [P, 2, UNIT], F32R)
        k_parts = sb("k_parts", [P, 2, KEYS], F32R)
        q_halves = [sb(f"q_halves{i}", [P, WIN, 2, QT], F32R) for i in range(2)]
        k_slots = [sb(f"k_slots{i}", [P, 8, KEYS], F32R) for i in range(2)]
        q_stack = [sb(f"q_stack{i}", [P, 4, 4, UNIT], F32R) for i in range(2)]
        k_stack = [sb(f"k_stack{i}", [P, 4, KEYS], F32R) for i in range(2)]
        v_aug = [sb(f"v_aug{i}", [P, WIN, HEADS, HD + 1]) for i in range(2)]
        top = [sb(f"top{a}", [P, 8]) for a in range(2)]
        shift = [[sb(f"shift{a}{h}", [P, 8, QT], F32R) for h in range(2)] for a in range(2)]
        probs = [[sb(f"probs{i}{a}", [P, HEADS * QT]) for a in range(2)] for i in range(2)]
        o_den = sb("o_den", [P, 2, 8])
        o_norm = sb("o_norm", [P, 2, 8, HD])
        oT = sb("oT", [QT, 2, 2, QT])
        res = sb("res", [P, P])
        stats = sb("stats", [P, 6])
        mean_var = sb("mean_var", [P, 2])
        inv_std = sb("inv_std", [P, 3])
        rows = [sb(f"rows{i}", [P, 2, ROW]) for i in range(4)]
        x1_all = sb("x1_all", [P, STEPS, P])
        x1T = sb("x1T", [P, P])
        logits = sb("logits", [P, E])
        best = sb("best", [P, 8])
        best_at = sb("best_at", [P, 8], U32)
        gap = sb("gap", [P, 4])
        chosen = sb("chosen", [P, 2, E])
        picked = sb("picked", [P, E], BF16)
        before = [sb(f"before{i}", [P, E], BF16) for i in range(2)]
        place_e = sb("place_e", [P, E])
        place_2 = sb("place_2", [P, 2, E])
        place_f = sb("place_f", [P, 2])
        place = [sb(f"place{i}", [P, 2], I32) for i in range(4)]

        w_up = sb("w_up", [P, E, 2, F])
        w_gate = sb("w_gate", [P, E, 2, F])
        w_down = sb("w_down", [P, E, 2, P])
        b_up = sb("b_up", [P, E, 2, F])
        b_gate = sb("b_gate", [P, E, F])
        b_down = sb("b_down", [P, E, P])
        pad = sb("pad", [P, ROW])
        steps16 = sb("steps16", [1, 16])
        tile_at = sb("tile_at", [1, TILES])
        tile_row0 = sb("tile_row0", [1, TILES])
        iota_i = sb("iota_i", [1, TILES], I32)
        upto = sb("upto", [1, E, E])
        total = sb("total", [1, E])
        need = sb("need", [1, E])
        need_16 = x_all[0:1, 0, :].rearrange("p (e n) -> p e n", e=E)
        ends = sb("ends", [1, E])
        ends_2 = x_all[0:1, 1, 0:E * E].rearrange("p (e n) -> p e n", e=E)
        passed, jumps = (x_all[0:1, i:i + 3, :].rearrange("p a n -> p (a n)")[:, 0:TILES * E].rearrange(
            "p (t e) -> p t e", e=E) for i in (2, 5))
        jump = sb("jump", [1, E])
        table_f = x_all[0:1, 8, 0:2 * TILES].rearrange("p (a t) -> p a t", a=2)
        pad_f = sb("pad_f", [1, E])
        tile_expert = sb("tile_expert", [1, TILES], I32)
        tile_row = sb("tile_row", [1, TILES], I32)
        pad_row = sb("pad_row", [1, E], I32)
        tile_x = [rows[i // 2][:, i % 2, :] for i in range(8)]
        tile_xT = [x_unit[i][:, 0, :] for i in range(2)]
        up = w_rows[:, :, :].rearrange("p (a b) n -> p a (b n)", a=2)
        z = [x_all[:, 8 + 2 * i:10 + 2 * i, :].rearrange("p a n -> p (a n)") for i in range(2)]
        zT = [x_all[:, 12 + 2 * i:14 + 2 * i, :] for i in range(2)]
        old_v = [v[:, :, :, :].rearrange("p w h n -> p (w h n)") for v in v_aug]
        gate_in = [v[:, 0:F] for v in old_v]
        act = [v[:, F:2 * F] for v in old_v]
        actT = [t[:, 0:F].rearrange("p (c n) -> p c n", c=2) for t in xT]
        y_in = res
        y = [x_all[:, i, :] for i in range(8)]
        y_two = [probs[i][0][:, :].rearrange("p (t k n) -> p t k n", t=4, k=2) for i in range(2)]
        total_4 = [probs[i][1][:, 0:512].rearrange("p (t n) -> p t n", t=4) for i in range(2)]
        stats_4 = x_unit[0][:, 1, 0:24].rearrange("p (t n) -> p t n", t=4)
        mean_4 = x_unit[0][:, 1, 32:40].rearrange("p (t n) -> p t n", t=4)
        inv_4 = x_unit[1][:, 1, 0:12].rearrange("p (n t) -> p n t", n=3)
        half_4 = sb("half_4", [P, 4])
        out_4 = [probs[i][1][:, 512:1024].rearrange("p (t n) -> p t n", t=4) for i in range(2)]

        loaded = sem("loaded")
        experts_loaded = sem("experts_loaded")
        spare_written = sem("spare_written")
        totals_made = sem("totals_made")
        table_chain = sem("table_chain")
        padded = sem("padded")
        tile_loaded = [sem(f"tile_loaded{i}") for i in range(8)]
        tile_xT_made = sem("tile_xT_made")
        tile_xT_ready = sem("tile_xT_ready")
        up_made = sem("up_made")
        up_ready = sem("up_ready")
        z_ready = sem("z_ready")
        zT_made = sem("zT_made")
        zT_ready = sem("zT_ready")
        gate_made = sem("gate_made")
        gate_ready = sem("gate_ready")
        act_ready = sem("act_ready")
        actT_made = sem("actT_made")
        actT_ready = sem("actT_ready")
        down_made = sem("down_made")
        down_read = sem("down_read")
        y_ready = sem("y_ready")
        y_sent = [sem(f"y_sent{i}") for i in range(8)]
        all_sent = sem("all_sent")
        two_loaded = [sem(f"two_loaded{i}") for i in range(2)]
        end_chain = sem("end_chain")
        end_inv = sem("end_inv")
        end_sum = sem("end_sum")
        out_ready = sem("out_ready")
        const_ready = sem("const_ready")
        zeros_ready = sem("zeros_ready")
        pool_const = sem("pool_const")
        dve_const = sem("dve_const")
        weights_T = sem("weights_T")
        weights_ready = sem("weights_ready")
        xb_ready = sem("xb_ready")
        x_loaded = [sem(f"x_loaded{i}") for i in range(2)]
        xT_made = sem("xT_made")
        xT_ready = sem("xT_ready")
        q_made = sem("q_made")
        q_hi = sem("q_hi")
        q_lo = sem("q_lo")
        k_made = sem("k_made")
        k_hi = sem("k_hi")
        k_lo = sem("k_lo")
        v_made = sem("v_made")
        v_ready = sem("v_ready")
        halves_ready = sem("halves_ready")
        slots_low = sem("slots_low")
        slots_high = sem("slots_high")
        q_out = sem("q_out")
        k_out = sem("k_out")
        stacked = [sem(f"stacked{i}") for i in range(2)]
        s_filled = sem("s_filled")
        s_read = sem("s_read")
        top_ready = sem("top_ready")
        shift_ready = sem("shift_ready")
        t_filled = sem("t_filled")
        probs_ready = sem("probs_ready")
        o_filled = sem("o_filled")
        den_ready = sem("den_ready")
        o_ready = sem("o_ready")
        oT_made = sem("oT_made")
        oT_ready = sem("oT_ready")
        y_made = sem("y_made")
        res_chain = sem("res_chain")
        norm_chain = sem("norm_chain")
        x1_ready = sem("x1_ready")
        x1T_made = sem("x1T_made")
        x1T_ready = sem("x1T_ready")
        x1_kept = sem("x1_kept")
        logits_made = sem("logits_made")
        route_chain = sem("route_chain")
        gap_ready = sem("gap_ready")
        gap_exp = sem("gap_exp")
        weight_chain = sem("weight_chain")
        rank_made = sem("rank_made")
        place_chain = sem("place_chain")
        before_ready = sem("before_ready")
        scattered = [sem(f"scattered{i}") for i in range(4)]
        rows_free = [sem(f"rows_free{i}") for i in range(4)]
        done = sem("done")

        block = ctx.enter_context(nc.Block())

        FIRST, LAST = -3, STEPS + 2

        def run_slots(eng, slot):
            for s in range(FIRST, 4):
                slot((0, s), s)
            with eng.Fori(1, STEPS // 4 - 1) as g:
                for c in range(4):
                    slot((g, c), None)
            for s in range(STEPS - 4, LAST + 1):
                slot((0, s), s)

        def has(s, lo, hi):
            return s is None or lo <= s <= hi

        def run_tiles(eng, slot):
            first = 5
            loops = (TILES - 4 - first) // 8
            for s in range(-1, first):
                slot((0, s), s)
            with eng.Fori(0, loops) as g:
                for c in range(first, first + 8):
                    slot((g, c), None)
            for s in range(first + 8 * loops, TILES + 4):
                slot((0, s), s)

        def tile_value(eng, table, n, most):
            g, c = n
            at = table[0:1, c:c + 1] if isinstance(g, int) else table[0:1, bass.ds(g * 8 + c, 1)]
            return eng.value_load(at, min_val=0, max_val=most)

        def of_expert(w, e):
            part = w[:, bass.ds(e, 1)]
            return part.rearrange("p o a n -> p (o a n)") if len(part.shape) == 4 else part.rearrange("p o n -> p (o n)")

        def unit_at(t, d):
            g, c = t
            assert (c + d) % 2 == 0
            return g, (c + d) // 2

        def ucount(u, per, add):
            g, c = u
            return g * (2 * per) + (c * per + add)

        def pcount(u, per):
            g, c = u
            return g * per + (c // 2 + 1) * per

        @block.sync
        def _(eng):
            wait_value = eng.alloc_register("wait_value")
            eng.dma_start(w_rows[:, 0:3, :], w_qkv.rearrange("(c p) i -> p c i", p=P)).then_inc(loaded, 16)
            eng.dma_start(w_rows[:, 3, :], w_out).then_inc(loaded, 16)
            eng.dma_start(gate[:, :], gate_w).then_inc(loaded, 16)
            eng.dma_start(gate_bias[:, :], gate_b.rearrange("(o e) -> o e", o=1).broadcast_to([P, E])).then_inc(loaded, 16)
            eng.dma_start(bo[:, :], b_out.rearrange("(o e) -> o e", o=1).broadcast_to([P, P])).then_inc(loaded, 16)

            def load_unit(u):
                g, c = u
                i = c % 2
                wait(eng, xT_made, ucount(u, 1, -1))
                first = g * (2 * UNIT) + c * UNIT
                src = x_rows[bass.ds(first, UNIT), :] if not isinstance(g, int) else x_rows[first:first + UNIT, :]
                eng.dma_start(x_unit[i][:, :, :], src.rearrange("(j p) d -> p j d", p=P)).then_inc(x_loaded[i], 16)

            load_unit((0, 0))
            load_unit((0, 1))
            eng.dma_start(x_all[:, :, :], x_rows.rearrange("(t p) d -> p t d", p=P)).then_inc(loaded, 16)

            def slot(t, s):
                if t[1] % 2 == 0 and has(s, 0, STEPS - 6):
                    load_unit(unit_at(t, 4))
                if t[1] % 2 and has(s, -3, STEPS - 5):
                    u = unit_at(t, 3)
                    i = u[1] % 2
                    wait_apart(eng, wait_value, const_ready, stacked[i], pcount(later(u, -2), 192))
                    wait(eng, q_hi, ucount(u, 1, 1))
                    wait(eng, q_lo, ucount(u, 1, 1))
                    eng.dma_start(q_scratch[i].rearrange("w f n -> f w n"),
                                  q_parts[:, :, :].bitcast(F32)).then_inc(q_out, 16)
                    if s is None or s >= 0:
                        wait_apart(eng, wait_value, const_ready, t_filled, count(t, 4, 4))
                    else:
                        eng.wait_ge(zeros_ready, 1)
                    eng.wait_ge(q_out, ucount(u, 16, 16))
                    for hh in range(4):
                        for dup in range(2):
                            eng.dma_start(
                                q_stack[i][64 * dup + hh:64 * dup + hh + 61:4, :, hh, :].bitcast(F32),
                                q_scratch[i].rearrange("w (d h g) n -> h (w d) g n", d=HD, h=4)[hh],
                            ).then_inc(stacked[i], 16)
                if t[1] % 2 == 0 and has(s, -2, STEPS - 4):
                    u = unit_at(t, 2)
                    i = u[1] % 2
                    wait(eng, k_hi, ucount(u, 1, 1))
                    wait(eng, k_lo, ucount(u, 1, 1))
                    eng.dma_start(k_scratch[i].rearrange("w f n -> f w n"),
                                  k_parts[:, :, :].bitcast(F32)).then_inc(k_out, 16)
                    eng.wait_ge(k_out, ucount(u, 16, 16))
                    for part in range(4):
                        eng.dma_start(
                            k_stack[i][32 * part:32 * part + 32, :, :].bitcast(F32),
                            k_scratch[i][part // 2].rearrange("(r g) n -> r g n", g=4),
                        ).then_inc(stacked[i], 16)
                if s is None:
                    e = t[0] * 4 + (t[1] - 4)
                    for c, w in enumerate((w1, w2)):
                        eng.dma_start(w_up[:, bass.ds(e, 1), c, :],
                                      w[bass.ds(e, 1)].rearrange("e h f -> h e f")).then_inc(experts_loaded, 16)
                    for held, w in ((w_gate, wg), (w_down, w3)):
                        eng.dma_start(held[:, bass.ds(e, 1), :, :].rearrange("p e c n -> p (e c) n"),
                                      w[bass.ds(e, 1)].rearrange("e (c p) n -> p (e c) n", p=P)).then_inc(experts_loaded, 16)
                if s is not None and STEPS - 4 <= s < STEPS:
                    held, b = ((b_up[:, :, 0, :], b1), (b_up[:, :, 1, :], b2), (b_gate[:, :, :], bg),
                               (b_down[:, :, :], b3))[s - STEPS + 4]
                    eng.dma_start(held, b.unsqueeze(0).broadcast_to([P, *b.shape])).then_inc(experts_loaded, 16)
                if s == 3:
                    eng.dma_start(routed[SPARE:SPARE + P, :], pad[:, :]).then_inc(spare_written, 16)
                if has(s, 4, STEPS + 2):
                    v = later(t, -4)
                    wait_apart(eng, wait_value, const_ready, scattered[v[1] % 4], rounds(v, 32))
                    eng.nop().then_inc(rows_free[v[1] % 4], 1)

            run_slots(eng, slot)
            eng.wait_ge(table_chain, 13)
            for e in range(E):
                at = eng.value_load(pad_row[0:1, e:e + 1], min_val=0, max_val=SPARE - P)
                eng.dma_start(routed[bass.ds(at, P), :], pad[:, :]).then_inc(padded, 16)
            eng.wait_ge(table_chain, 15)
            eng.wait_ge(padded, 16 * E)
            eng.wait_ge(spare_written, 16)
            eng.wait_ge(x1_kept, STEPS)
            for i in range(4):
                eng.wait_ge(scattered[i], 32 * STEPS // 4)

            def load_tile(n):
                i = n[1] % 8
                at = tile_value(eng, tile_row, n, SPARE)
                wait(eng, y_sent[i], tile_rounds(later(n, -8), 16))
                eng.dma_start(tile_x[i][:, :], routed[bass.ds(at, P), :]).then_inc(tile_loaded[i], 16)

            def tile_slot(n, s):
                if s == -1:
                    for c in range(2):
                        load_tile((0, c))
                if has(s, -1, TILES - 4):
                    load_tile(later(n, 3))

            run_tiles(eng, tile_slot)
            eng.wait_ge(all_sent, 1)

            def store(q):
                eng.wait_ge(out_ready, 4 * (q + 1))
                eng.dma_start(out_rows[512 * q:512 * q + 512, :].rearrange("(t p) d -> p t d", p=P),
                              out_4[q % 2][:, :, :]).then_inc(done, 16)

            for q in range(4):
                i = q % 2
                if q >= 2:
                    eng.wait_ge(end_sum, 2 * (q - 1))
                eng.dma_start(y_two[i][:, :, :, :],
                              expert_out[1024 * q:1024 * q + 1024, :].rearrange("(t p k) d -> p t k d", p=P, k=2)).then_inc(two_loaded[i], 16)
                if q:
                    store(q - 1)
            store(3)
            eng.wait_ge(done, 64)

        @block.gpsimd
        def _(eng):
            wait_value = eng.alloc_register("wait_value")
            n = [0]

            def step(ins):
                n[0] += 1
                ins.then_inc(pool_const, 1)
                eng.wait_ge(pool_const, n[0])

            step(eng.memset(ident[:, :], 0.0))
            step(eng.memset(delta[:, :], 0.0))
            step(eng.memset(mask_f[:, :, :], 0.0))
            step(eng.memset(ones_b[:, :], 1.0))
            step(eng.memset(minus_half[:, :], -0.5))
            step(eng.memset(minus_one[:, :], -1.0))
            step(eng.memset(xT[1][:, :], 0.0))
            step(eng.affine_select(out=ident[:, :], in_=ident[:, :], compare_op=ALU.not_equal, fill=1.0,
                                   base=0, pattern=[[-1, P]], channel_multiplier=1))
            step(eng.affine_select(out=below[:, :], in_=ones_b[:, :], compare_op=ALU.is_ge, fill=0.0,
                                   base=-1, pattern=[[1, P]], channel_multiplier=-1))
            for half in range(2):
                r = slice(64 * half, 64 * half + 64)
                step(eng.affine_select(out=delta[r, :], in_=delta[r, :], compare_op=ALU.not_equal, fill=1.0,
                                       base=0, pattern=[[-1, QT]], channel_multiplier=1))
                step(eng.affine_select(out=mask_f[r, :, :], in_=mask_f[r, :, :], compare_op=ALU.is_ge,
                                       fill=MASKED, base=-1, pattern=[[0, 2], [1, P]], channel_multiplier=-1))
                step(eng.affine_select(out=mask_f[r, :, :], in_=mask_f[r, :, :], compare_op=ALU.is_ge,
                                       fill=MASKED, base=QT, pattern=[[0, 2], [-1, P]], channel_multiplier=1))
                step(eng.affine_select(out=mask_f[r, 1, :], in_=mask_f[r, 1, :], compare_op=ALU.is_ge,
                                       fill=MASKED, base=-QT, pattern=[[1, P]], channel_multiplier=0))
            step(eng.tensor_copy(mask_q[:, :, :], mask_f[:, :, :]))
            step(eng.tensor_copy(ident_b[:, :], ident[:, :]))
            step(eng.iota(dest_i[:, :, :], pattern=[[2 * P, STEPS], [1, 2]], base=0, channel_multiplier=2))
            for half in range(2):
                r, o = slice(64 * half, 64 * half + 64), slice(64 - 64 * half, 128 - 64 * half)
                step(eng.memset(shift_w[r, half, :, :].bitcast(F32), -1.0))
                step(eng.tensor_copy(shift_w[o, half, :, :], mask_f[o, :, :]))
                for a in range(2):
                    step(eng.tensor_copy(shift[a][half][o, :, :], delta[o, :].unsqueeze(1).to_broadcast([64, 8, QT])))
            step(eng.memset(before[0][:, :], 0.0))
            step(eng.memset(pad[:, :], 0.0))
            step(eng.iota(pad[:, P:P + 1].bitcast(I32), pattern=[[0, 1]], base=NOWHERE, channel_multiplier=0))
            step(eng.memset(half_4[:, :], -0.5))
            step(eng.iota(iota_i[:, :], pattern=[[1, TILES]], base=0, channel_multiplier=0))
            step(eng.tensor_copy(tile_at[:, :], iota_i[:, 0:TILES]))
            step(eng.tensor_scalar(steps16[:, :], iota_i[:, 0:16], float(P), None, ALU.mult))
            step(eng.tensor_scalar(tile_row0[:, :], tile_at[:, :], float(P), None, ALU.mult))
            step(eng.memset(upto[:, :, :], 1.0))
            step(eng.affine_select(out=upto[:, :, :], in_=upto[:, :, :], compare_op=ALU.is_ge, fill=0.0,
                                   base=0, pattern=[[1, E], [-1, E]], channel_multiplier=0))
            for e in range(E):
                step(eng.memset(expert_iota[:, e:e + 1], float(e)))
                step(eng.memset(expert_base[:, e:e + 1], float(e * REGION)))
            for i in range(2):
                step(eng.memset(v_aug[i][:, :, :, HD:HD + 1], 1.0))
            eng.nop().then_inc(const_ready, 1)
            step(eng.memset(q_stack[0][:, :, :, :].bitcast(F32), 0.0))
            step(eng.memset(q_stack[1][:, :, :, :].bitcast(F32), 0.0))
            eng.nop().then_inc(zeros_ready, 1)
            for i in range(4):
                eng.nop().then_inc(rows_free[i], 1)
            eng.wait_ge(loaded, 16 * 6)
            eng.tensor_tensor(x_all[:, :, :], x_all[:, :, :], bo[:, :].unsqueeze(1).to_broadcast([P, STEPS, P]),
                              ALU.add).then_inc(xb_ready, 1)
            eng.wait_ge(dve_const, 3)

            def key_slots(u):
                i = u[1] % 2
                wait(eng, k_hi, ucount(u, 1, 1))
                wait(eng, s_filled, ucount(u, 8, -8))
                eng.tensor_tensor(k_slots[i][:, 4:8, :],
                                  k_parts[:, 0, :].bitcast(F32).unsqueeze(1).to_broadcast([P, 4, KEYS]),
                                  slot_col[:, 4:8].unsqueeze(2).to_broadcast([P, 4, KEYS]),
                                  ALU.mult).then_inc(slots_high, 1)

            def normalise(t):
                i = t[1] % 4
                wait_apart(eng, wait_value, const_ready, res_chain, count(t, 3, 3))
                eng.tensor_scalar(inv_std[:, 0:1], mean_var[:, 1:2], EPS, None, ALU.add).then_inc(norm_chain, 1)
                wait_apart(eng, wait_value, const_ready, x1_ready, count(t, 2, 0))
                eng.tensor_scalar(inv_std[:, 1:2], mean_var[:, 0:1], -1.0, None, ALU.mult).then_inc(norm_chain, 1)
                wait(eng, rows_free[i], rounds(t, 1))
                eng.wait_ge(norm_chain, count(t, 3, 2))
                eng.tensor_tensor(inv_std[:, 2:3], inv_std[:, 0:1], minus_half[:, :], ALU.pow).then_inc(norm_chain, 1)
                wait_apart(eng, wait_value, const_ready, norm_chain, count(t, 3, 3))
                eng.tensor_scalar(rows[i][:, :, 0:P], res[:, :].unsqueeze(1).to_broadcast([P, 2, P]),
                                  inv_std[:, 1:2], inv_std[:, 2:3], ALU.add, ALU.mult).then_inc(x1_ready, 1)
                g, c = t
                dest = dest_i[:, c, :] if isinstance(g, int) else dest_i[:, bass.ds(g * 4 + c, 1), :].rearrange("p o k -> p (o k)")
                eng.tensor_copy(rows[i][:, :, P:P + 1].bitcast(I32).rearrange("p k o -> p (k o)"), dest).then_inc(x1_ready, 1)

            def gap_of_two(t):
                wait(eng, route_chain, count(t, 5, 3))
                wait(eng, weight_chain, count(t, 3, 0))
                eng.tensor_tensor(gap[:, 0:1], best[:, 1:2], best[:, 0:1], ALU.subtract).then_inc(gap_ready, 1)

            def weights_of_two(t):
                i = t[1] % 4
                wait_apart(eng, wait_value, const_ready, gap_exp, count(t, 1, 1))
                eng.tensor_scalar(gap[:, 2:3], gap[:, 1:2], 1.0, None, ALU.add).then_inc(weight_chain, 1)
                eng.wait_ge(weight_chain, count(t, 3, 1))
                eng.tensor_tensor(rows[i][:, 0, P + 1:ROW], gap[:, 2:3], minus_one[:, :], ALU.pow).then_inc(weight_chain, 1)
                eng.wait_ge(weight_chain, count(t, 3, 2))
                eng.tensor_tensor(rows[i][:, 1, P + 1:ROW], gap[:, 1:2], rows[i][:, 0, P + 1:ROW],
                                  ALU.mult).then_inc(weight_chain, 1)

            def scatter(t):
                i = t[1] % 4
                wait_apart(eng, wait_value, const_ready, weight_chain, count(t, 3, 3))
                wait_apart(eng, wait_value, const_ready, x1_ready, count(t, 2, 2))
                wait_apart(eng, wait_value, const_ready, place_chain, count(t, 4, 4))
                for k in range(2):
                    eng.indirect_dma_start(
                        routed, bass.IndirectOffsetOnAxis(ap=place[i][:, k:k + 1], axis=0),
                        rows[i][:, k, :], None, bounds_check=SPARE + P - 1, oob_is_err=False).then_inc(scattered[i], 16)

            def slot(t, s):
                if has(s, 4, STEPS + 3):
                    scatter(later(t, -4))
                if has(s, 2, STEPS + 1):
                    normalise(later(t, -2))
                if has(s, 3, STEPS + 2):
                    gap_of_two(later(t, -3))
                if t[1] % 2 == 0 and has(s, -2, STEPS - 4):
                    key_slots(unit_at(t, 2))
                if has(s, 3, STEPS + 2):
                    weights_of_two(later(t, -3))

            run_slots(eng, slot)
            scatter((0, STEPS - 1))

            def send(n):
                i = n[1] % 8
                wait_apart(eng, wait_value, const_ready, y_ready, tile_count(n, 1, 1))
                eng.indirect_dma_start(
                    expert_out, bass.IndirectOffsetOnAxis(ap=tile_x[i][:, P:P + 1].bitcast(I32), axis=0),
                    y[i][:, :], None, bounds_check=ASSIGNED - 1, oob_is_err=False).then_inc(y_sent[i], 16)

            def tile_slot(n, s):
                if has(s, 4, TILES + 3):
                    send(later(n, -4))

            run_tiles(eng, tile_slot)
            for i in range(8):
                eng.wait_ge(y_sent[i], 16 * ((TILES - 1 - i) // 8 + 1))
            eng.nop().then_inc(all_sent, 1)
            for q in range(4):
                eng.wait_ge(end_chain, 8 * (q + 1))
                if q:
                    eng.wait_ge(out_ready, 4 * q)
                eng.tensor_scalar(inv_4[:, 0, :], mean_4[:, :, 1], EPS, None, ALU.add).then_inc(end_inv, 1)
                eng.wait_ge(end_inv, 3 * q + 1)
                eng.tensor_tensor(inv_4[:, 1, :], inv_4[:, 0, :], half_4[:, :], ALU.pow).then_inc(end_inv, 1)
                eng.wait_ge(end_inv, 3 * q + 2)
                eng.tensor_tensor(inv_4[:, 2, :], mean_4[:, :, 0], inv_4[:, 1, :], ALU.mult).then_inc(end_inv, 1)

        @block.scalar
        def _(eng):
            eng.wait_ge(weights_T, 1)
            for c in range(2):
                eng.copy(wT[:, c, :].rearrange("p (d h g) -> p g h d", d=HD, h=4),
                         unit_bank[:, P * c:P * c + P].rearrange("p (g h d) -> p g h d", g=4, h=4)).then_inc(weights_ready, 1)
            eng.copy(wT[:, 2, :], unit_bank[:, 2 * P:3 * P]).then_inc(weights_ready, 1)
            eng.copy(woT[:, :, :], out_bank[0:QT, 0:2 * P].rearrange("p (h n) -> p h n", h=2)).then_inc(weights_ready, 1)
            eng.wait_ge(const_ready, 1)
            eng.wait_ge(dve_const, 3)

            def tokens_T(u):
                i = u[1] % 2
                wait(eng, xT_made, ucount(u, 1, 1))
                wait(eng, k_made, ucount(u, 1, -1))
                wait(eng, v_made, ucount(u, 1, -1))
                wait(eng, xT_ready, ucount(u, 2, 0))
                eng.copy(xT[i][:, 0:HALO], xT[1 - i][:, UNIT:KEYS]).then_inc(xT_ready, 1)
                eng.copy(xT[i][:, HALO:KEYS], unit_bank[:, 0:UNIT]).then_inc(xT_ready, 1)

            def queries(u):
                i = u[1] % 2
                wait(eng, q_made, ucount(u, 1, 1))
                wait(eng, q_out, ucount(u, 16, 0))
                wait(eng, q_lo, ucount(u, 1, 0))
                wait(eng, halves_ready, ucount(u, 2, 0))
                eng.activation(q_parts[:, 0, :], unit_bank[:, 0:UNIT], ACT.Copy, scale=SCALE).then_inc(q_hi, 1)
                wait(eng, q_hi, ucount(u, 1, 1))
                wait(eng, s_filled, ucount(u, 8, -8))
                for half in range(2):
                    eng.activation(q_halves[i][:, :, half, :],
                                   q_parts[:, 0, :].bitcast(F32).rearrange("p (w q) -> p w q", w=WIN),
                                   ACT.Copy, scale=half_col[:, half:half + 1]).then_inc(halves_ready, 1)

            def keys(u):
                wait(eng, k_made, ucount(u, 1, 1))
                wait(eng, k_out, ucount(u, 16, 0))
                wait(eng, k_lo, ucount(u, 1, 0))
                wait(eng, slots_high, ucount(u, 1, 0))
                wait(eng, slots_low, ucount(u, 4, 0))
                eng.copy(k_parts[:, 0, :], unit_bank[:, 0:KEYS]).then_inc(k_hi, 1)

            def key_slots(u):
                i = u[1] % 2
                eng.wait_ge(k_hi, ucount(u, 1, 1))
                wait(eng, s_filled, ucount(u, 8, -8))
                for c in range(4):
                    eng.activation(k_slots[i][:, c, :], k_parts[:, 0, :].bitcast(F32), ACT.Copy,
                                   scale=slot_col[:, c:c + 1]).then_inc(slots_low, 1)

            def values(u):
                i = u[1] % 2
                wait(eng, v_made, ucount(u, 1, 1))
                wait(eng, o_filled, ucount(u, 2, -2))
                eng.copy(v_aug[i][:, :, :, 0:HD],
                         unit_bank[:, :].rearrange("p (w h d) -> p w h d", w=WIN, h=HEADS)).then_inc(v_ready, 1)

            def exps(t, a):
                for h in range(2):
                    wait(eng, t_filled, count(t, 4, 2 * a + h + 1))
                    if h == 0:
                        wait(eng, o_filled, count(t, 1, -1))
                    eng.activation(probs[t[1] % 2][a][:, 512 * h:512 * h + 512], t_bank[h][:, :],
                                   ACT.Exp).then_inc(probs_ready, 1)

            def slot(t, s):
                odd = t[1] % 2 and has(s, -3, STEPS - 5)
                if has(s, 0, STEPS - 1):
                    exps(t, 0)
                if has(s, 2, STEPS + 1):
                    v = later(t, -2)
                    wait(eng, oT_made, count(v, 1, 1))
                    wait(eng, y_made, count(v, 1, 0))
                    eng.copy(oT[:, :, :, :].rearrange("c h a q -> c a h q"),
                             out_bank[0:QT, 0:256].rearrange("c (a h q) -> c a h q", a=2, h=2)).then_inc(oT_ready, 1)
                if has(s, 3, STEPS + 2):
                    v = later(t, -3)
                    wait(eng, x1T_made, count(v, 1, 1))
                    wait(eng, logits_made, count(v, 1, 0))
                    eng.copy(x1T[:, :], route_bank[:, 0:P]).then_inc(x1T_ready, 1)
                if odd:
                    tokens_T(unit_at(t, 3))
                if t[1] % 2 == 0 and has(s, -2, STEPS - 4):
                    keys(unit_at(t, 2))
                if has(s, 0, STEPS - 1):
                    exps(t, 1)
                if t[1] % 2 == 0 and has(s, -2, STEPS - 4):
                    key_slots(unit_at(t, 2))
                if odd:
                    queries(unit_at(t, 3))
                if t[1] % 2 == 0 and has(s, 0, STEPS - 2):
                    values(unit_at(t, 0))
                if has(s, 3, STEPS + 2):
                    v = later(t, -3)
                    wait(eng, gap_ready, count(v, 1, 1))
                    eng.activation(gap[:, 1:2], gap[:, 0:1], ACT.Exp).then_inc(gap_exp, 1)
                if has(s, 3, STEPS + 2):
                    v = later(t, -3)
                    g, c = v
                    dst = x1_all[:, c, :] if isinstance(g, int) else x1_all[:, bass.ds(g * 4 + c, 1), :].rearrange("p o d -> p (o d)")
                    eng.copy(dst, rows[c % 4][:, 0, 0:P]).then_inc(x1_kept, 1)

            run_slots(eng, slot)

            def tile_slot(n, s):
                if has(s, -1, TILES - 2):
                    m = later(n, 1)
                    wait(eng, tile_xT_made, tile_count(m, 1, 1))
                    wait(eng, up_made, tile_count(m, 1, -1))
                    eng.copy(tile_xT[m[1] % 2][:, :], xt_bank[:, 0:P]).then_inc(tile_xT_ready, 1)
                if has(s, 1, TILES):
                    m = later(n, -1)
                    wait(eng, zT_made, tile_count(m, 1, 1))
                    wait(eng, gate_made, tile_count(m, 1, -1))
                    eng.copy(zT[m[1] % 2][:, :, :], zt_bank[:, 0:F].rearrange("p (c n) -> p c n", c=2)).then_inc(zT_ready, 1)
                if has(s, 3, TILES + 2):
                    m = later(n, -3)
                    wait(eng, actT_made, tile_count(m, 1, 1))
                    wait(eng, down_made, tile_count(m, 1, -1))
                    eng.copy(actT[m[1] % 2][:, :, :], at_bank[:, 0:F].rearrange("p (c n) -> p c n", c=2)).then_inc(actT_ready, 1)
                if has(s, 2, TILES + 1):
                    m = later(n, -2)
                    wait(eng, gate_ready, tile_count(m, 1, 1))
                    wait(eng, actT_made, tile_count(m, 1, -1))
                    eng.activation(act[m[1] % 2][:, :], gate_in[m[1] % 2][:, :], ACT.Silu).then_inc(act_ready, 1)

            run_tiles(eng, tile_slot)

        @block.vector
        def _(eng):
            wait_value = eng.alloc_register("wait_value")
            eng.wait_ge(const_ready, 1)
            eng.tensor_reduce(head_of[:, :], ident[:, :].rearrange("p (d f) -> p f d", d=HD), AX_X,
                              ALU.add).then_inc(dve_const, 1)
            eng.wait_ge(dve_const, 1)
            eng.tensor_reduce(half_col[:, :], head_of[:, :].rearrange("p (h s l) -> p s h l", h=4, s=2),
                              mybir.AxisListType.XY, ALU.add).then_inc(dve_const, 1)
            eng.tensor_reduce(slot_col[:, :].rearrange("p (l h) -> p l h", l=2),
                              head_of[:, :].rearrange("p (h s l) -> p l h s", h=4, s=2), AX_X,
                              ALU.add).then_inc(dve_const, 1)
            eng.wait_ge(loaded, 16 * 6)
            eng.tensor_copy(wo_rows[:, :, :].rearrange("p h (k d) -> p h k d", k=8),
                            w_rows[:, 3, :].rearrange("p (k h d) -> p h k d", k=8, h=2)).then_inc(dve_const, 1)

            def find_top(t, a, h):
                if h == 0:
                    wait(eng, shift_ready, count(t, 4, 2 * a - 2))
                wait(eng, s_filled, count(t, 4, 2 * a + h + 1))
                eng.tensor_reduce(top[a][:, 4 * h:4 * h + 4],
                                  s_bank[h][:, :].rearrange("p (s k) -> p s k", s=4), AX_X,
                                  ALU.max).then_inc(s_read, 1)

            def spread_top(t, a, half):
                if half == 0:
                    wait(eng, t_filled, count(t, 4, 2 * a + 2 - 4))
                    eng.wait_ge(s_read, count(t, 4, 2 * a + 2))
                r = slice(64 * half, 64 * half + 64)
                eng.tensor_tensor(shift[a][half][r, :, :], top[a][r, :].unsqueeze(2).to_broadcast([64, 8, QT]),
                                  delta[r, :].unsqueeze(1).to_broadcast([64, 8, QT]),
                                  ALU.mult).then_inc(shift_ready, 1)

            o = o_bank[:, 0:288].rearrange("p (a h n) -> p a h n", a=2, h=8)

            def denominators(t, half):
                if half == 0:
                    wait(eng, o_filled, count(t, 1, 1))
                    wait(eng, o_ready, count(t, 2, 0))
                r, c = slice(64 * half, 64 * half + 64), 9 * half
                eng.reciprocal(o_den[r, :, :], o[r, :, :, c + HD:c + HD + 1].rearrange("p a h o -> p a (h o)")).then_inc(den_ready, 1)

            def divide(t, half):
                wait(eng, oT_made, count(t, 1, 0))
                eng.wait_ge(den_ready, count(t, 2, half + 1))
                r, c = slice(64 * half, 64 * half + 64), 9 * half
                eng.tensor_tensor(o_norm[r, :, :, :], o[r, :, :, c:c + HD],
                                  o_den[r, :, :].unsqueeze(3).to_broadcast([64, 2, 8, HD]),
                                  ALU.mult).then_inc(o_ready, 1)

            def residual(t):
                g, c = t
                wait(eng, y_made, count(t, 1, 1))
                wait(eng, x1_ready, count(t, 2, 0))
                wait(eng, res_chain, count(t, 3, 0))
                xs = x_all[:, c, :] if isinstance(g, int) else x_all[:, bass.ds(g * 4 + c, 1), :].rearrange("p o d -> p (o d)")
                eng.tensor_tensor(res[:, :], out_bank[:, 256:384], xs, ALU.add).then_inc(res_chain, 1)

            def statistics(t):
                eng.wait_ge(res_chain, count(t, 3, 1))
                eng.bn_stats(stats[:, :], res[:, :]).then_inc(res_chain, 1)

            def mean_variance(t):
                wait_apart(eng, wait_value, const_ready, res_chain, count(t, 3, 2))
                eng.bn_aggr(mean_var[:, :], stats[:, :]).then_inc(res_chain, 1)

            def split_queries(u):
                wait(eng, q_hi, ucount(u, 1, 1))
                eng.scalar_tensor_tensor(out=q_parts[:, 1, :], in0=unit_bank[:, 0:UNIT], scalar=SCALE,
                                         in1=q_parts[:, 0, :].bitcast(F32), op0=ALU.mult,
                                         op1=ALU.subtract).then_inc(q_lo, 1)

            def split_keys(u):
                wait(eng, k_hi, ucount(u, 1, 1))
                eng.tensor_tensor(k_parts[:, 1, :], unit_bank[:, 0:KEYS], k_parts[:, 0, :].bitcast(F32),
                                  ALU.subtract).then_inc(k_lo, 1)

            def biased_logits(t):
                wait(eng, logits_made, count(t, 1, 1))
                wait(eng, gap_ready, count(t, 1, 0))
                eng.tensor_tensor(logits[:, :], route_bank[:, P:P + E], gate_bias[:, :], ALU.add).then_inc(route_chain, 1)

            def best_logits(t):
                wait_apart(eng, wait_value, const_ready, route_chain, count(t, 5, 1))
                eng.max(best[:, :], logits[:, :]).then_inc(route_chain, 1)

            def best_experts(t):
                wait_apart(eng, wait_value, const_ready, route_chain, count(t, 5, 2))
                eng.max_index(best_at[:, :], best[:, :], logits[:, :]).then_inc(route_chain, 1)

            def mark_chosen(t):
                eng.wait_ge(route_chain, count(t, 5, 3))
                wait(eng, place_chain, count(t, 4, 0))
                eng.tensor_tensor(chosen[:, :, :], expert_iota[:, :].unsqueeze(1).to_broadcast([P, 2, E]),
                                  best_at[:, 0:2].unsqueeze(2).to_broadcast([P, 2, E]),
                                  ALU.is_equal).then_inc(route_chain, 1)

            def mark_picked(t):
                eng.wait_ge(route_chain, count(t, 5, 4))
                wait(eng, rank_made, count(t, 1, 0))
                wait(eng, before_ready, count(t, 1, 0))
                eng.tensor_tensor(picked[:, :], chosen[:, 0, :], chosen[:, 1, :], ALU.add).then_inc(route_chain, 1)

            def places_of_experts(t):
                i = t[1] % 2
                wait(eng, rank_made, count(t, 1, 1))
                eng.tensor_tensor(place_e[:, :], route_bank[:, P + E:P + 2 * E], expert_base[:, :], ALU.add).then_inc(place_chain, 1)
                eng.wait_ge(route_chain, count(t, 5, 5))
                eng.tensor_tensor(before[1 - i][:, :], before[i][:, :], picked[:, :], ALU.add).then_inc(before_ready, 1)

            def places_of_chosen(t):
                eng.wait_ge(place_chain, count(t, 4, 1))
                eng.tensor_tensor(place_2[:, :, :], chosen[:, :, :], place_e[:, :].unsqueeze(1).to_broadcast([P, 2, E]),
                                  ALU.mult).then_inc(place_chain, 1)

            def sum_places(t):
                eng.wait_ge(place_chain, count(t, 4, 2))
                eng.tensor_reduce(place_f[:, :], place_2[:, :, :], AX_X, ALU.add).then_inc(place_chain, 1)

            def whole_places(t):
                eng.wait_ge(place_chain, count(t, 4, 3))
                wait(eng, rows_free[t[1] % 4], rounds(t, 1))
                eng.tensor_copy(place[t[1] % 4][:, :], place_f[:, :]).then_inc(place_chain, 1)

            def slot(t, s):
                top_t, out_t, res_t, route_t = later(t, 1), later(t, -1), later(t, -2), later(t, -3)
                find, divides = has(s, -1, STEPS - 2), has(s, 1, STEPS)
                adds, routes = has(s, 2, STEPS + 1), has(s, 3, STEPS + 2)
                if find:
                    find_top(top_t, 0, 0)
                    find_top(top_t, 0, 1)
                    spread_top(top_t, 0, 0)
                if adds:
                    residual(res_t)
                if find:
                    spread_top(top_t, 0, 1)
                if adds:
                    statistics(res_t)
                if routes:
                    biased_logits(route_t)
                if adds:
                    mean_variance(res_t)
                if routes:
                    best_logits(route_t)
                if t[1] % 2 == 0 and has(s, -2, STEPS - 4):
                    split_keys(unit_at(t, 2))
                if find:
                    find_top(top_t, 1, 0)
                if routes:
                    best_experts(route_t)
                if find:
                    find_top(top_t, 1, 1)
                if routes:
                    mark_chosen(route_t)
                    mark_picked(route_t)
                if find:
                    spread_top(top_t, 1, 0)
                    spread_top(top_t, 1, 1)
                if t[1] % 2 and has(s, -3, STEPS - 5):
                    split_queries(unit_at(t, 3))
                if routes:
                    places_of_experts(route_t)
                    places_of_chosen(route_t)
                if divides:
                    denominators(out_t, 0)
                if routes:
                    sum_places(route_t)
                if divides:
                    denominators(out_t, 1)
                if routes:
                    whole_places(route_t)
                if divides:
                    divide(out_t, 0)
                    divide(out_t, 1)

            run_slots(eng, slot)

            links = [0]

            def link(ins):
                links[0] += 1
                ins.then_inc(table_chain, 1)
                eng.wait_ge(table_chain, links[0])

            eng.wait_ge(totals_made, 1)
            link(eng.tensor_copy(total[:, :], route_bank[0:1, P:P + E]))
            link(eng.tensor_tensor(need_16[:, :, :], total[:, :].unsqueeze(2).to_broadcast([1, E, 16]),
                                   steps16[:, :].unsqueeze(1).to_broadcast([1, E, 16]), ALU.is_gt))
            link(eng.tensor_reduce(need[:, :], need_16[:, :, :], AX_X, ALU.add))
            link(eng.tensor_tensor(ends_2[:, :, :], upto[:, :, :], need[:, :].unsqueeze(1).to_broadcast([1, E, E]), ALU.mult))
            link(eng.tensor_reduce(ends[:, :], ends_2[:, :, :], AX_X, ALU.add))
            link(eng.tensor_tensor(passed[:, :, :], ends[:, :].unsqueeze(1).to_broadcast([1, TILES, E]),
                                   tile_at[:, :].unsqueeze(2).to_broadcast([1, TILES, E]), ALU.is_le))
            link(eng.tensor_reduce(table_f[:, 0, :], passed[:, :, :], AX_X, ALU.add))
            link(eng.tensor_scalar(jump[:, :], need[:, :], -float(P), float(REGION), ALU.mult, ALU.add))
            link(eng.tensor_tensor(jumps[:, :, :], passed[:, :, :], jump[:, :].unsqueeze(1).to_broadcast([1, TILES, E]), ALU.mult))
            link(eng.tensor_reduce(table_f[:, 1, :], jumps[:, :, :], AX_X, ALU.add))
            link(eng.tensor_tensor(table_f[:, 1, :], table_f[:, 1, :], tile_row0[:, :], ALU.add))
            link(eng.tensor_tensor(pad_f[:, :], total[:, :], expert_base[0:1, :], ALU.add))
            link(eng.tensor_copy(pad_row[:, :], pad_f[:, :]))
            link(eng.tensor_scalar(tile_expert[:, :], table_f[:, 0, :], float(E - 1), None, ALU.min))
            link(eng.tensor_scalar(tile_row[:, :], table_f[:, 1, :], float(SPARE), None, ALU.min))
            eng.wait_ge(experts_loaded, 16 * (4 * E + 4))

            def tile_slot(n, s):
                if has(s, 0, TILES - 1):
                    i = n[1] % 2
                    e = tile_value(eng, tile_expert, n, E - 1)
                    wait(eng, up_made, tile_count(n, 1, 1))
                    wait(eng, z_ready, tile_count(n, 1, 0))
                    eng.tensor_tensor(up[:, :, :].rearrange("p a n -> p (a n)"), up_bank[:, :], of_expert(b_up, e),
                                      ALU.add).then_inc(up_ready, 1)
                    eng.wait_ge(up_ready, tile_count(n, 1, 1))
                    wait(eng, zT_made, tile_count(n, 1, -1))
                    eng.tensor_tensor(z[i][:, :], up[:, 0, :], up[:, 1, :], ALU.mult).then_inc(z_ready, 1)
                if has(s, 2, TILES + 1):
                    m = later(n, -2)
                    e = tile_value(eng, tile_expert, m, E - 1)
                    wait(eng, gate_made, tile_count(m, 1, 1))
                    wait(eng, act_ready, tile_count(m, 1, -1))
                    eng.tensor_tensor(gate_in[m[1] % 2][:, :], gate_bank[:, 0:F], of_expert(b_gate, e),
                                      ALU.add).then_inc(gate_ready, 1)
                if has(s, 4, TILES + 3):
                    m = later(n, -4)
                    e = tile_value(eng, tile_expert, m, E - 1)
                    wait(eng, down_made, tile_count(m, 1, 1))
                    wait(eng, y_ready, tile_count(m, 1, 0))
                    eng.tensor_tensor(y_in[:, :], down_bank[:, 0:P], of_expert(b_down, e), ALU.add).then_inc(down_read, 1)
                    eng.wait_ge(down_read, tile_count(m, 1, 1))
                    eng.tensor_scalar(y[m[1] % 8][:, :], y_in[:, :], tile_x[m[1] % 8][:, P + 1:ROW], None,
                                      ALU.mult).then_inc(y_ready, 1)

            run_tiles(eng, tile_slot)

            def finish(q):
                for j in range(4):
                    eng.wait_ge(end_inv, 3 * (q + 1))
                    eng.tensor_scalar(out_4[q % 2][:, j, :], total_4[q % 2][:, j, :], inv_4[:, 1, j:j + 1],
                                      inv_4[:, 2, j:j + 1], ALU.mult, ALU.subtract).then_inc(out_ready, 1)

            eng.wait_ge(x1_kept, STEPS)
            for q in range(4):
                i = q % 2
                if q >= 2:
                    eng.wait_ge(done, 16 * (q - 1))
                eng.wait_ge(two_loaded[i], 16 * (q // 2 + 1))
                eng.tensor_tensor(total_4[i][:, :, :], y_two[i][:, :, 0, :], y_two[i][:, :, 1, :], ALU.add).then_inc(end_sum, 1)
                eng.wait_ge(end_sum, 2 * q + 1)
                eng.tensor_tensor(total_4[i][:, :, :], total_4[i][:, :, :], x1_all[:, 4 * q:4 * q + 4, :], ALU.add).then_inc(end_sum, 1)
                eng.wait_ge(end_sum, 2 * q + 2)
                if q:
                    eng.wait_ge(end_inv, 3 * q)
                for j in range(4):
                    eng.bn_stats(stats_4[:, j, :], total_4[i][:, j, :]).then_inc(end_chain, 1)
                eng.wait_ge(end_chain, 8 * q + 4)
                for j in range(4):
                    eng.bn_aggr(mean_4[:, j, :], stats_4[:, j, :]).then_inc(end_chain, 1)
                finish(q)

        @block.tensor
        def _(eng):
            wait_value = eng.alloc_register("wait_value")
            eng.wait_ge(loaded, 16 * 6)
            eng.wait_ge(const_ready, 1)
            eng.wait_ge(dve_const, 4)
            for c in range(3):
                eng.transpose(unit_bank[:, P * c:P * c + P], w_rows[:, c, :], ident[:, :])
            for half in range(2):
                ins = eng.transpose(out_bank[0:QT, P * half:P * half + P],
                                    wo_rows[:, half, :], ident[:, :])
            ins.then_inc(weights_T, 1)
            eng.wait_ge(weights_ready, 4)

            def tokens_T(u):
                g, c = u
                i = c % 2
                eng.wait_ge(x_loaded[i], pcount(u, 16))
                wait(eng, v_ready, ucount(u, 1, -1))
                wait(eng, k_lo, ucount(u, 1, 0))
                wait(eng, k_hi, ucount(u, 1, 0))
                for j in range(2):
                    ins = eng.transpose(unit_bank[:, P * j:P * j + P], x_unit[i][:, j, :], ident[:, :])
                ins.then_inc(xT_made, 1)

            def queries(u):
                i = u[1] % 2
                wait(eng, xT_ready, ucount(u, 2, 2))
                eng.matmul(unit_bank[:, 0:UNIT], wT[:, 0, :], xT[i][:, HALO:KEYS]).then_inc(q_made, 1)

            def keys(u):
                i = u[1] % 2
                wait(eng, q_hi, ucount(u, 1, 1))
                wait(eng, q_lo, ucount(u, 1, 1))
                eng.matmul(unit_bank[:, 0:KEYS], wT[:, 1, :], xT[i][:, :]).then_inc(k_made, 1)

            def values(u, last):
                i = u[1] % 2
                wait(eng, k_hi, ucount(u, 1, 1 if last else 2))
                wait(eng, k_lo, ucount(u, 1, 1 if last else 2))
                for w in range(WIN):
                    ins = eng.matmul(unit_bank[:, P * w:P * w + P], xT[i][:, QT * w:QT * w + P], wT[:, 2, :])
                ins.then_inc(v_made, 1)

            def max_scores(t, a):
                i, w = (t[1] // 2) % 2, 2 * (t[1] % 2) + a
                first = int(t[1] % PER_BATCH == 0 and a == 0)
                u = (t[0], t[1] // 2)
                wait(eng, halves_ready, ucount(u, 2, 2))
                for h in range(2):
                    if h == 0:
                        wait(eng, slots_low, ucount(u, 4, 4))
                    else:
                        wait(eng, slots_high, ucount(u, 1, 1))
                    wait(eng, s_read, count(t, 4, 2 * a + h - 1))
                    eng.matmul(s_bank[h][:, :], ident_b[:, :], mask_q[:, first:first + 1, :].to_broadcast([P, 4, P]),
                               start=True, stop=False)
                    eng.matmul(s_bank[h][:, :], q_halves[i][:, w, :, :],
                               k_slots[i][:, 4 * h:4 * h + 4, QT * w:QT * w + P],
                               start=False, stop=True).then_inc(s_filled, 1)

            def shifted_scores(t, a):
                i, w = (t[1] // 2) % 2, 2 * (t[1] % 2) + a
                first = int(t[1] % PER_BATCH == 0 and a == 0)
                u = (t[0], t[1] // 2)
                wait(eng, shift_ready, count(t, 4, 2 * a + 2))
                wait(eng, stacked[i], pcount(u, 192))
                for h in range(2):
                    wait(eng, probs_ready, count(t, 4, 2 * a + h - 1))
                    for l in range(2):
                        grp = 2 * h + l
                        eng.matmul(t_bank[h][:, 256 * l:256 * l + 256], k_stack[i][:, grp, QT * w:QT * w + P],
                                   q_stack[i][:, grp, :, QT * w:QT * w + QT], start=(l == 0), stop=False,
                                   skip_group_check=True)
                    eng.matmul(t_bank[h][:, :], shift_w[:, h, first, :], shift[a][h][:, :, :], start=False,
                               stop=True, skip_group_check=True).then_inc(t_filled, 1)

            def weighted_values(t, quarter):
                i, a = (t[1] // 2) % 2, quarter // 2
                w = 2 * (t[1] % 2) + a
                if quarter == 0:
                    wait(eng, v_ready, ucount((t[0], t[1] // 2), 1, 1))
                    wait(eng, o_ready, count(t, 2, 0))
                wait(eng, probs_ready, count(t, 4, 2 * a + 2))
                for p in range(4 * (quarter % 2), 4 * (quarter % 2) + 4):
                    c = 144 * a + 18 * p
                    ins = eng.matmul(o_bank[:, c:c + 18], probs[t[1] % 2][a][:, P * p:P * p + P],
                                     v_aug[i][:, w, 2 * p:2 * p + 2, :])
                if quarter == 3:
                    ins.then_inc(o_filled, 1)

            def heads_T(t):
                wait(eng, o_ready, count(t, 2, 2))
                wait_apart(eng, wait_value, const_ready, res_chain, count(t, 3, -2))
                for a in range(2):
                    ins = eng.transpose(out_bank[0:QT, P * a:P * a + P],
                                        o_norm[:, a, :, :].rearrange("p h d -> p (h d)"), ident[:, :])
                ins.then_inc(oT_made, 1)

            def project_out(t):
                wait(eng, oT_ready, count(t, 1, 1))
                for half in range(2):
                    ins = eng.matmul(out_bank[:, 256:384], oT[:, half, :, :], woT[:, half, :],
                                     start=(half == 0), stop=(half == 1))
                ins.then_inc(y_made, 1)

            def x1_T(t):
                wait(eng, x1_ready, count(t, 2, 1))
                wait(eng, place_chain, count(t, 4, -3))
                eng.transpose(route_bank[:, 0:P], rows[t[1] % 4][:, 0, 0:P], ident[:, :]).then_inc(x1T_made, 1)

            def gate_logits(t):
                wait(eng, x1T_ready, count(t, 1, 1))
                eng.matmul(route_bank[:, P:P + E], x1T[:, :], gate[:, :]).then_inc(logits_made, 1)

            def ranks(t):
                i = t[1] % 2
                wait(eng, route_chain, count(t, 5, 5))
                wait(eng, before_ready, count(t, 1, 0))
                eng.matmul(route_bank[:, P + E:P + 2 * E], below[:, :], picked[:, :], start=True, stop=False)
                eng.matmul(route_bank[:, P + E:P + 2 * E], ones_b[:, :], before[i][:, :], start=False, stop=True).then_inc(rank_made, 1)

            def slot(t, s):
                odd = t[1] % 2 and has(s, -3, STEPS - 5)
                out_t = later(t, -1) if has(s, 1, STEPS) else None
                if has(s, -1, STEPS - 2):
                    max_scores(later(t, 1), 0)
                if has(s, 0, STEPS - 1):
                    shifted_scores(t, 0)
                if has(s, 2, STEPS + 1):
                    heads_T(later(t, -2))
                if has(s, 3, STEPS + 2):
                    x1_T(later(t, -3))
                if odd:
                    tokens_T(unit_at(t, 3))
                if t[1] % 2 == 0 and has(s, -2, STEPS - 4):
                    keys(unit_at(t, 2))
                if has(s, 2, STEPS + 1):
                    project_out(later(t, -2))
                if has(s, 3, STEPS + 2):
                    gate_logits(later(t, -3))
                if out_t is not None:
                    weighted_values(out_t, 0)
                if has(s, -1, STEPS - 2):
                    max_scores(later(t, 1), 1)
                if has(s, 0, STEPS - 1):
                    shifted_scores(t, 1)
                if out_t is not None:
                    weighted_values(out_t, 1)
                if odd:
                    queries(unit_at(t, 3))
                if t[1] % 2 == 0 and has(s, 0, STEPS - 2):
                    values(unit_at(t, 0), s == STEPS - 2)
                if out_t is not None:
                    weighted_values(out_t, 2)
                if has(s, 3, STEPS + 2):
                    ranks(later(t, -3))
                if out_t is not None:
                    weighted_values(out_t, 3)

            run_slots(eng, slot)
            eng.wait_ge(place_chain, 4 * STEPS)
            eng.wait_ge(before_ready, STEPS)
            eng.matmul(route_bank[:, P:P + E], ones_b[:, :], before[0][:, :]).then_inc(totals_made, 1)
            eng.wait_ge(table_chain, 15)
            eng.wait_ge(experts_loaded, 16 * (4 * E + 4))

            def tile_slot(n, s):
                if has(s, -1, TILES - 2):
                    m = later(n, 1)
                    wait(eng, tile_loaded[m[1] % 8], tile_rounds(m, 16))
                    wait(eng, tile_xT_ready, tile_count(m, 1, 0))
                    eng.transpose(xt_bank[:, 0:P], tile_x[m[1] % 8][:, 0:P], ident[:, :]).then_inc(tile_xT_made, 1)
                if has(s, 0, TILES - 1):
                    e = tile_value(eng, tile_expert, n, E - 1)
                    wait(eng, tile_xT_ready, tile_count(n, 1, 1))
                    wait(eng, up_ready, tile_count(n, 1, 0))
                    eng.matmul(up_bank[:, :], tile_xT[n[1] % 2][:, :], of_expert(w_up, e)).then_inc(up_made, 1)
                if has(s, 1, TILES):
                    m = later(n, -1)
                    wait(eng, z_ready, tile_count(m, 1, 1))
                    wait(eng, zT_ready, tile_count(m, 1, 0))
                    for c in range(2):
                        ins = eng.transpose(zt_bank[:, P * c:P * c + P], z[m[1] % 2][:, P * c:P * c + P], ident[:, :])
                    ins.then_inc(zT_made, 1)
                if has(s, 2, TILES + 1):
                    m = later(n, -2)
                    e = tile_value(eng, tile_expert, m, E - 1)
                    wait(eng, zT_ready, tile_count(m, 1, 1))
                    wait(eng, gate_ready, tile_count(m, 1, 0))
                    for c in range(2):
                        ins = eng.matmul(gate_bank[:, 0:F], zT[m[1] % 2][:, c, :],
                                         w_gate[:, bass.ds(e, 1), c, :].rearrange("p o n -> p (o n)"),
                                         start=(c == 0), stop=(c == 1))
                    ins.then_inc(gate_made, 1)
                if has(s, 3, TILES + 2):
                    m = later(n, -3)
                    wait(eng, act_ready, tile_count(m, 1, 1))
                    wait(eng, actT_ready, tile_count(m, 1, 0))
                    for c in range(2):
                        ins = eng.transpose(at_bank[:, P * c:P * c + P], act[m[1] % 2][:, P * c:P * c + P], ident[:, :])
                    ins.then_inc(actT_made, 1)
                if has(s, 4, TILES + 3):
                    m = later(n, -4)
                    e = tile_value(eng, tile_expert, m, E - 1)
                    wait(eng, actT_ready, tile_count(m, 1, 1))
                    wait(eng, down_read, tile_count(m, 1, 0))
                    for c in range(2):
                        ins = eng.matmul(down_bank[:, 0:P], actT[m[1] % 2][:, c, :],
                                         w_down[:, bass.ds(e, 1), c, :].rearrange("p o n -> p (o n)"),
                                         start=(c == 0), stop=(c == 1))
                    ins.then_inc(down_made, 1)

            run_tiles(eng, tile_slot)


_INS = ["L0_attn_x", "L0_attn_w_qkv", "L0_attn_w_out", "L0_attn_b_out", "L0_ffn_gate_w", "L0_ffn_gate_b",
        "L0_ffn_w1", "L0_ffn_b1", "L0_ffn_w2", "L0_ffn_b2", "L0_ffn_wg", "L0_ffn_bg", "L0_ffn_w3", "L0_ffn_b3"]
_OUTS = [((4, 512, 128), "float32")]


def kernel(**inputs):
    import numpy as _np
    import concourse.bacc as _bacc
    from concourse import mybir as _mybir
    from concourse.bass_utils import run_bass_kernel_spmd as _run

    nc = _bacc.Bacc("TRN2", target_bir_lowering=False, num_devices=1)
    arrays, args = {}, []
    for name in _INS:
        a = _np.ascontiguousarray(inputs[name])
        arrays[f"in_{name}_dram"] = a
        args.append(nc.dram_tensor(f"in_{name}_dram", a.shape, _mybir.dt.from_np(a.dtype), kind="ExternalInput").ap())
    for i, (shape, dtype) in enumerate(_OUTS):
        dt = _mybir.dt.from_np(_np.dtype(dtype))
        args.append(nc.dram_tensor(f"out_{i}_dram", shape, dt, kind="ExternalOutput").ap())
    moe_layer_program(nc, *args)
    r = _run(nc, [arrays], core_ids=[0])
    return r.results[0]["out_0_dram"]
```

```python
from contextlib import ExitStack

import concourse.bass as bass
from concourse import mybir

F32 = mybir.dt.float32
F32R = mybir.dt.float32r
BF16 = mybir.dt.bfloat16
I32 = mybir.dt.int32
U32 = mybir.dt.uint32
ALU = mybir.AluOpType
ACT = mybir.ActivationFunctionType
AX_X = mybir.AxisListType.X

P = 128
HEADS = 16
HD = 8
WINDOW = 64
QT = 64
UNIT = 256
HALO = WINDOW
KEYS = UNIT + HALO
WIN = UNIT // QT
MASKED = -1.0e30
EPS = 1e-5
ROW = P + 2


def count(t, per, add):
    g, c = t
    return g * (4 * per) + (c * per + add)


def wait(eng, sem, value):
    if not (isinstance(value, int) and value <= 0):
        eng.wait_ge(sem, value)


def rounds(t, per):
    g, c = t
    return g * per + (c // 4 + 1) * per


def tile_count(n, per, add):
    g, c = n
    return g * (8 * per) + (c * per + add)


def tile_rounds(n, per):
    g, c = n
    return g * per + (c // 8 + 1) * per


def wait_apart(eng, reg, met, sem, value):
    if not isinstance(value, int):
        eng.reg_mov(reg, value)
        eng.wait_ge(met, 1)
        eng.wait_ge(sem, reg)
    else:
        wait(eng, sem, value)


def later(t, d):
    return (t[0], t[1] + d)


def is_step(t, step):
    return isinstance(t[0], int) and t[1] == step


def moe_layer_program(nc, x, w_qkv, w_out, b_out, gate_w, gate_b, w1, b1, w2, b2, wg, bg, w3, b3, out):
    B, S, D = x.shape
    E, _, F = w1.shape
    TOKENS = B * S
    STEPS = TOKENS // P
    PER_BATCH = S // P
    UNITS = TOKENS // UNIT
    SCALE = float(HD) ** -0.5
    assert D == P and HEADS * HD == D and PER_BATCH == 4 and E == 8 == STEPS - 8 and F == 2 * P
    ASSIGNED = 2 * TOKENS
    TILES = ASSIGNED // P + E - 1
    REGION = TOKENS + P
    SPARE = E * REGION
    EARLY = STEPS - 4
    PADS = REGION - EARLY * P
    NOWHERE = 1 << 20

    x_rows = x.rearrange("b s d -> (b s) d")
    out_rows = out.rearrange("b s d -> (b s) d")
    q_scratch = nc.dram_tensor("q_scratch", (2, 2, P, UNIT), F32, kind="Internal").ap()
    k_scratch = nc.dram_tensor("k_scratch", (2, 2, P, KEYS), F32, kind="Internal").ap()
    routed = nc.dram_tensor("routed", (SPARE + P, ROW), F32, kind="Internal").ap()
    expert_out = nc.dram_tensor("expert_out", (ASSIGNED, D), F32, kind="Internal").ap()

    with ExitStack() as ctx:
        def sb(name, shape, dt=F32):
            return ctx.enter_context(nc.sbuf_tensor(name, shape, dt))

        def sem(name):
            return ctx.enter_context(nc.semaphore(name))

        bank = [ctx.enter_context(nc.psum_tensor(f"bank{i}", [P, 512], F32)) for i in range(8)]
        s_bank = bank[0:2]
        t_bank = bank[2:4]
        o_bank = bank[4]
        out_bank = bank[5]
        route_bank = bank[6]
        unit_bank = bank[7]
        xt_bank, up_bank, zt_bank, gate_bank, at_bank, down_bank = bank[0:5] + [bank[7]]

        ident = sb("ident", [P, P])
        ident_b = sb("ident_b", [P, P], BF16)
        mask_f = sb("mask_f", [P, 2, P])
        mask_q = sb("mask_q", [P, 2, P], BF16)
        shift_w = sb("shift_w", [P, 2, 2, P], F32R)
        delta = sb("delta", [P, QT])
        below = sb("below", [P, P], BF16)
        ones_b = sb("ones_b", [P, P], BF16)
        head_of = sb("head_of", [P, HEADS])
        half_col = sb("half_col", [P, 2])
        slot_col = sb("slot_col", [P, 8])
        expert_iota = sb("expert_iota", [P, E])
        expert_base = sb("expert_base", [P, E])
        dest_i = sb("dest_i", [P, STEPS, 2], I32)
        minus_half = sb("minus_half", [P, 1])
        minus_one = sb("minus_one", [P, 1])
        w_rows = sb("w_rows", [P, 4, P])
        wo_rows = sb("wo_rows", [P, 2, QT])
        wT = sb("wT", [P, 3, P])
        woT = sb("woT", [QT, 2, P])
        gate = sb("gate", [P, E])
        gate_bias = sb("gate_bias", [P, E])
        bo = sb("bo", [P, P])
        x_all = sb("x_all", [P, STEPS, P])
        x_unit = [sb(f"x_unit{i}", [P, 2, P]) for i in range(2)]
        xT = [sb(f"xT{i}", [P, KEYS]) for i in range(2)]
        q_parts = sb("q_parts", [P, 2, UNIT], F32R)
        k_parts = sb("k_parts", [P, 2, KEYS], F32R)
        q_halves = [sb(f"q_halves{i}", [P, WIN, 2, QT], F32R) for i in range(2)]
        k_slots = [sb(f"k_slots{i}", [P, 8, KEYS], F32R) for i in range(2)]
        q_stack = [sb(f"q_stack{i}", [P, 4, 4, UNIT], F32R) for i in range(2)]
        k_stack = [sb(f"k_stack{i}", [P, 4, KEYS], F32R) for i in range(2)]
        v_aug = [sb(f"v_aug{i}", [P, WIN, HEADS, HD + 1]) for i in range(2)]
        top = [sb(f"top{a}", [P, 8]) for a in range(2)]
        shift = [[sb(f"shift{a}{h}", [P, 8, QT], F32R) for h in range(2)] for a in range(2)]
        probs = [[sb(f"probs{i}{a}", [P, HEADS * QT]) for a in range(2)] for i in range(2)]
        o_den = sb("o_den", [P, 2, 8])
        o_norm = sb("o_norm", [P, 2, 8, HD])
        oT = sb("oT", [QT, 2, 2, QT])
        res = sb("res", [P, P])
        stats = sb("stats", [P, 6])
        mean_var = sb("mean_var", [P, 2])
        inv_std = sb("inv_std", [P, 3])
        rows = [sb(f"rows{i}", [P, 2, ROW]) for i in range(4)]
        x1_all = sb("x1_all", [P, STEPS, P])
        x1T = sb("x1T", [P, P])
        logits = sb("logits", [P, E])
        best = sb("best", [P, 8])
        best_at = sb("best_at", [P, 8], U32)
        gap = sb("gap", [P, 4])
        chosen = sb("chosen", [P, 2, E])
        picked = sb("picked", [P, E], BF16)
        before = [sb(f"before{i}", [P, E], BF16) for i in range(2)]
        place_e = sb("place_e", [P, E])
        place_2 = sb("place_2", [P, 2, E])
        place_f = sb("place_f", [P, 2])
        place = [sb(f"place{i}", [P, 2], I32) for i in range(4)]

        w_up = sb("w_up", [P, E, 2, F])
        w_gate = sb("w_gate", [P, E, 2, F])
        w_down = sb("w_down", [P, E, 2, P])
        b_up = sb("b_up", [P, E, 2, F])
        b_gate = sb("b_gate", [P, E, F])
        b_down = sb("b_down", [P, E, P])
        pad = sb("pad", [P, ROW])
        steps16 = sb("steps16", [1, 16])
        tile_at = sb("tile_at", [1, TILES])
        tile_row0 = sb("tile_row0", [1, TILES])
        iota_i = sb("iota_i", [P, TILES], I32)
        upto = sb("upto", [1, E, E])
        total = sb("total", [1, E])
        need = sb("need", [1, E])
        need_16 = x_all[0:1, 0, :].rearrange("p (e n) -> p e n", e=E)
        ends = sb("ends", [1, E])
        ends_2 = x_all[0:1, 1, 0:E * E].rearrange("p (e n) -> p e n", e=E)
        passed, jumps = (x_all[0:1, i:i + 3, :].rearrange("p a n -> p (a n)")[:, 0:TILES * E].rearrange(
            "p (t e) -> p t e", e=E) for i in (2, 5))
        jump = sb("jump", [1, E])
        table_f = x_all[0:1, 8, 0:2 * TILES].rearrange("p (a t) -> p a t", a=2)
        pad_f = sb("pad_f", [1, E])
        tile_expert = sb("tile_expert", [1, TILES + 8], I32)
        tile_row = sb("tile_row", [1, TILES], I32)
        pad_row = sb("pad_row", [1, E], I32)
        tile_x = [rows[i // 2][:, i % 2, :] for i in range(8)]
        tile_xT = [x_unit[i][:, 0, :] for i in range(2)]
        up = w_rows[:, :, :].rearrange("p (a b) n -> p a (b n)", a=2)
        z = [x_all[:, 8 + 2 * i:10 + 2 * i, :].rearrange("p a n -> p (a n)") for i in range(2)]
        zT = [x_all[:, 12 + 2 * i:14 + 2 * i, :] for i in range(2)]
        old_v = [v[:, :, :, :].rearrange("p w h n -> p (w h n)") for v in v_aug]
        gate_in = [v[:, 0:F] for v in old_v]
        act = [v[:, F:2 * F] for v in old_v]
        actT = [t[:, 0:F].rearrange("p (c n) -> p c n", c=2) for t in xT]
        y_in = res
        y = [x_all[:, i, :] for i in range(8)]
        y_two = w_up[:, :, :, :].rearrange("p e c (k n) -> p (e c) k n", k=2)
        total_all = w_gate[:, 0:4, :, :].rearrange("p e c (k n) -> p (e c k) n", k=2)
        out_all = w_gate[:, 4:8, :, :].rearrange("p e c (k n) -> p (e c k) n", k=2)
        stats_all = x_unit[0][:, 1, 0:96].rearrange("p (t n) -> p t n", t=STEPS)
        mean_all = x_unit[0][:, 1, 96:128].rearrange("p (t n) -> p t n", t=STEPS)
        inv_all = x_unit[1][:, 1, 0:64].rearrange("p (n t) -> p n t", n=4)
        half_4 = sb("half_4", [P, 4])

        loaded = sem("loaded")
        weights_loaded = sem("weights_loaded")
        ident_ready = sem("ident_ready")
        masks_ready = sem("masks_ready")
        halo_ready = sem("halo_ready")
        last_ready = sem("last_ready")
        first_stacked = sem("first_stacked")
        shift_const = sem("shift_const")
        experts_loaded = sem("experts_loaded")
        spare_written = sem("spare_written")
        totals_made = sem("totals_made")
        table_chain = sem("table_chain")
        padded = sem("padded")
        pad_chain = sem("pad_chain")
        tile_loaded = [sem(f"tile_loaded{i}") for i in range(8)]
        tile_xT_made = sem("tile_xT_made")
        tile_xT_ready = sem("tile_xT_ready")
        up_made = sem("up_made")
        up_ready = sem("up_ready")
        z_ready = sem("z_ready")
        zT_made = sem("zT_made")
        zT_ready = sem("zT_ready")
        gate_made = sem("gate_made")
        gate_ready = sem("gate_ready")
        act_ready = sem("act_ready")
        actT_made = sem("actT_made")
        actT_ready = sem("actT_ready")
        down_made = sem("down_made")
        down_read = sem("down_read")
        y_ready = sem("y_ready")
        y_sent = [sem(f"y_sent{i}") for i in range(8)]
        all_sent = sem("all_sent")
        two_loaded = [sem(f"two_loaded{q}") for q in range(4)]
        end_chain = sem("end_chain")
        end_inv = sem("end_inv")
        end_sum = sem("end_sum")
        pool_sum = sem("pool_sum")
        out_ready = sem("out_ready")
        const_ready = sem("const_ready")
        zeros_ready = [sem(f"zeros_ready{i}") for i in range(2)]
        pool_const = sem("pool_const")
        dve_const = sem("dve_const")
        weights_T = sem("weights_T")
        weights_ready = sem("weights_ready")
        xb_ready = sem("xb_ready")
        x_loaded = [sem(f"x_loaded{i}") for i in range(2)]
        xT_made = sem("xT_made")
        xT_ready = sem("xT_ready")
        q_made = sem("q_made")
        q_hi = sem("q_hi")
        q_lo = sem("q_lo")
        k_made = sem("k_made")
        k_hi = sem("k_hi")
        k_lo = sem("k_lo")
        v_made = sem("v_made")
        v_ready = sem("v_ready")
        halves_ready = sem("halves_ready")
        slots_low = sem("slots_low")
        slots_high = sem("slots_high")
        q_out = sem("q_out")
        k_out = sem("k_out")
        stacked = [sem(f"stacked{i}") for i in range(2)]
        s_filled = sem("s_filled")
        s_read = sem("s_read")
        top_ready = sem("top_ready")
        shift_ready = sem("shift_ready")
        t_filled = sem("t_filled")
        probs_ready = sem("probs_ready")
        o_filled = sem("o_filled")
        den_ready = sem("den_ready")
        o_ready = sem("o_ready")
        oT_made = sem("oT_made")
        oT_ready = sem("oT_ready")
        y_made = sem("y_made")
        res_chain = sem("res_chain")
        norm_chain = sem("norm_chain")
        x1_ready = sem("x1_ready")
        x1T_made = sem("x1T_made")
        x1T_ready = sem("x1T_ready")
        x1_kept = sem("x1_kept")
        logits_made = sem("logits_made")
        route_chain = sem("route_chain")
        gap_ready = sem("gap_ready")
        gap_exp = sem("gap_exp")
        weight_chain = sem("weight_chain")
        rank_made = sem("rank_made")
        place_chain = sem("place_chain")
        before_ready = sem("before_ready")
        scattered = [sem(f"scattered{i}") for i in range(4)]
        rows_free = [sem(f"rows_free{i}") for i in range(4)]
        done = sem("done")

        block = ctx.enter_context(nc.Block())

        FIRST, LAST = -3, STEPS + 2

        def run_slots(eng, slot):
            for s in range(FIRST, 4):
                slot((0, s), s)
            with eng.Fori(1, STEPS // 4 - 1) as g:
                for c in range(4):
                    slot((g, c), None)
            for s in range(STEPS - 4, LAST + 1):
                slot((0, s), s)

        def values_bank(t):
            return s_bank[0] if is_step(t, STEPS - 1) else o_bank

        def has(s, lo, hi):
            return s is None or lo <= s <= hi

        def run_tiles(eng, slot):
            first = 5
            loops = (TILES - 4 - first) // 8
            for s in range(-1, first):
                slot((0, s), s)
            with eng.Fori(0, loops) as g:
                for c in range(first, first + 8):
                    slot((g, c), None)
            for s in range(first + 8 * loops, TILES + 4):
                slot((0, s), s)

        def tile_value(eng, table, n, most):
            g, c = n
            at = table[0:1, c:c + 1] if isinstance(g, int) else table[0:1, bass.ds(g * 8 + c, 1)]
            return eng.value_load(at, min_val=0, max_val=most)

        def experts_at(engine, n, s):
            if not has(s, 0, TILES + 3):
                return {}
            g, c = n
            five = tile_expert[0:1, c:c + 5] if isinstance(g, int) else tile_expert[0:1, bass.ds(g * 8 + c, 5)]
            _, values = nc.values_load_multi_w_load_instructions(
                five[:, 0:5:2], engines=[engine], min_val=0, max_val=E - 1,
                skip_runtime_bounds_check_because="the table counts experts and is cut at the last")
            return {d: v for d, v in zip((4, 2, 0), values) if has(s, d, TILES - 1 + d)}

        def of_expert(w, e):
            part = w[:, bass.ds(e, 1)]
            return part.rearrange("p o a n -> p (o a n)") if len(part.shape) == 4 else part.rearrange("p o n -> p (o n)")

        def unit_at(t, d):
            g, c = t
            assert (c + d) % 2 == 0
            return g, (c + d) // 2

        def ucount(u, per, add):
            g, c = u
            return g * (2 * per) + (c * per + add)

        def pcount(u, per):
            g, c = u
            return g * per + (c // 2 + 1) * per

        POOL_PARTS = 2

        def stack_queries(eng, i, part):
            hh, dup = part // 2, part % 2
            return eng.dma_start(
                q_stack[i][64 * dup + hh:64 * dup + hh + 61:4, :, hh, :].bitcast(F32),
                q_scratch[i].rearrange("w (d h g) n -> h (w d) g n", d=HD, h=4)[hh])

        @block.sync
        def _(eng):
            wait_value = eng.alloc_register("wait_value")
            def load_unit(u):
                g, c = u
                i = c % 2
                wait(eng, xT_made, ucount(u, 1, -1))
                first = g * (2 * UNIT) + c * UNIT
                src = x_rows[bass.ds(first, UNIT), :] if not isinstance(g, int) else x_rows[first:first + UNIT, :]
                eng.dma_start(x_unit[i][:, :, :], src.rearrange("(j p) d -> p j d", p=P)).then_inc(x_loaded[i], 16)

            load_unit((0, 0))
            eng.dma_start(w_rows[:, 0:3, :], w_qkv.rearrange("(c p) i -> p c i", p=P)).then_inc(weights_loaded, 16)
            eng.dma_start(w_rows[:, 3, :], w_out).then_inc(weights_loaded, 16)
            load_unit((0, 1))
            eng.dma_start(gate[:, :], gate_w).then_inc(loaded, 16)
            eng.dma_start(gate_bias[:, :], gate_b.rearrange("(o e) -> o e", o=1).broadcast_to([P, E])).then_inc(loaded, 16)
            eng.dma_start(bo[:, :], b_out.rearrange("(o e) -> o e", o=1).broadcast_to([P, P])).then_inc(loaded, 16)
            eng.dma_start(x_all[:, :, :], x_rows.rearrange("(t p) d -> p t d", p=P)).then_inc(loaded, 16)

            def slot(t, s):
                if s == EARLY + 3:
                    eng.wait_ge(pad_chain, 2)
                    for e in range(0, E, 4):
                        _, rows_at = nc.values_load_multi_w_load_instructions(
                            pad_row[0:1, e:e + 4], engines=[mybir.EngineType.SP], min_val=0, max_val=SPARE - PADS)
                        for at in rows_at:
                            eng.dma_start(routed[bass.ds(at, PADS), :].rearrange("(c p) r -> p c r", p=P),
                                          pad[:, :].unsqueeze(1).to_broadcast([P, PADS // P, ROW])).then_inc(padded, 16)
                if t[1] % 2 == 0 and has(s, 0, STEPS - 6):
                    load_unit(unit_at(t, 4))
                if t[1] % 2 and has(s, -3, STEPS - 5):
                    u = unit_at(t, 3)
                    i = u[1] % 2
                    wait_apart(eng, wait_value, const_ready, stacked[i], pcount(later(u, -2), 192))
                    wait(eng, q_hi, ucount(u, 1, 1))
                    wait(eng, q_lo, ucount(u, 1, 1))
                    eng.dma_start(q_scratch[i].rearrange("w f n -> f w n"),
                                  q_parts[:, :, :].bitcast(F32)).then_inc(q_out, 16)
                if t[1] % 2 == 0 and has(s, -2, STEPS - 4):
                    u = unit_at(t, 2)
                    i = u[1] % 2
                    wait(eng, k_hi, ucount(u, 1, 1))
                    wait(eng, k_lo, ucount(u, 1, 1))
                    eng.dma_start(k_scratch[i].rearrange("w f n -> f w n"),
                                  k_parts[:, :, :].bitcast(F32)).then_inc(k_out, 16)
                    if s is None or s >= 2:
                        wait_apart(eng, wait_value, const_ready, t_filled, count(t, 4, 0))
                    else:
                        eng.wait_ge(zeros_ready[i], 1)
                    eng.wait_ge(q_out, ucount(u, 16, 16))
                    for part in range(8):
                        if s != -2 or part < 8 - POOL_PARTS:
                            stack_queries(eng, i, part).then_inc(stacked[i], 16)
                    eng.wait_ge(k_out, ucount(u, 16, 16))
                    for part in range(4):
                        eng.dma_start(
                            k_stack[i][32 * part:32 * part + 32, :, :].bitcast(F32),
                            k_scratch[i][part // 2].rearrange("(r g) n -> r g n", g=4),
                        ).then_inc(stacked[i], 16)
                if s == 3:
                    eng.wait_ge(const_ready, 1)
                    eng.dma_start(routed[SPARE:SPARE + P, :], pad[:, :]).then_inc(spare_written, 16)
                if s is None:
                    e = t[0] * 4 + (t[1] - 4)
                    for c, w in enumerate((w1, w2)):
                        eng.dma_start(w_up[:, bass.ds(e, 1), c, :],
                                      w[bass.ds(e, 1)].rearrange("e h f -> h e f")).then_inc(experts_loaded, 16)
                    for held, w in ((w_gate, wg), (w_down, w3)):
                        eng.dma_start(held[:, bass.ds(e, 1), :, :].rearrange("p e c n -> p (e c) n"),
                                      w[bass.ds(e, 1)].rearrange("e (c p) n -> p (e c) n", p=P)).then_inc(experts_loaded, 16)
                if has(s, 4, STEPS + 2):
                    v = later(t, -4)
                    wait_apart(eng, wait_value, const_ready, scattered[v[1] % 4], rounds(v, 32))
                    eng.nop().then_inc(rows_free[v[1] % 4], 1)
                if s is not None and STEPS - 4 <= s < STEPS:
                    held, b = ((b_up[:, :, 0, :], b1), (b_up[:, :, 1, :], b2), (b_gate[:, :, :], bg),
                               (b_down[:, :, :], b3))[s - STEPS + 4]
                    eng.dma_start(held, b.unsqueeze(0).broadcast_to([P, *b.shape])).then_inc(experts_loaded, 16)

            run_slots(eng, slot)
            eng.wait_ge(table_chain, 13)
            eng.wait_ge(padded, 16 * E)
            eng.wait_ge(spare_written, 16)
            eng.wait_ge(x1_kept, STEPS)
            for i in range(4):
                eng.wait_ge(scattered[i], 32 * STEPS // 4)

            def load_tile(n):
                i = n[1] % 8
                at = tile_value(eng, tile_row, n, SPARE)
                wait(eng, y_sent[i], tile_rounds(later(n, -8), 16))
                eng.dma_start(tile_x[i][:, :], routed[bass.ds(at, P), :]).then_inc(tile_loaded[i], 16)

            def tile_slot(n, s):
                if s == -1:
                    for c in range(2):
                        load_tile((0, c))
                if has(s, -1, TILES - 4):
                    load_tile(later(n, 3))

            run_tiles(eng, tile_slot)
            eng.wait_ge(all_sent, 1)

            for q in range(4):
                eng.dma_start(y_two[:, 4 * q:4 * q + 4, :, :],
                              expert_out[1024 * q:1024 * q + 1024, :].rearrange("(t p k) d -> p t k d", p=P, k=2)).then_inc(two_loaded[q], 16)
            for q in range(4):
                if q < 3:
                    eng.wait_ge(out_ready, 4 * (q + 1))
                else:
                    eng.wait_ge(last_ready, 4)
                eng.dma_start(out_rows[512 * q:512 * q + 512, :].rearrange("(t p) d -> p t d", p=P),
                              out_all[:, 4 * q:4 * q + 4, :]).then_inc(done, 16)
            eng.wait_ge(done, 64)

        @block.gpsimd
        def _(eng):
            wait_value = eng.alloc_register("wait_value")
            n = [0]

            def step(ins):
                n[0] += 1
                ins.then_inc(pool_const, 1)
                eng.wait_ge(pool_const, n[0])

            step(eng.memset(ident[:, :], 0.0))
            step(eng.affine_select(out=ident[:, :], in_=ident[:, :], compare_op=ALU.not_equal, fill=1.0,
                                   base=0, pattern=[[-1, P]], channel_multiplier=1))
            eng.nop().then_inc(ident_ready, 1)
            step(eng.memset(delta[:, :], 0.0))
            step(eng.memset(mask_f[:, :, :], 0.0))
            for half in range(2):
                r = slice(64 * half, 64 * half + 64)
                step(eng.affine_select(out=delta[r, :], in_=delta[r, :], compare_op=ALU.not_equal, fill=1.0,
                                       base=0, pattern=[[-1, QT]], channel_multiplier=1))
                step(eng.affine_select(out=mask_f[r, :, :], in_=mask_f[r, :, :], compare_op=ALU.is_ge,
                                       fill=MASKED, base=-1, pattern=[[0, 2], [1, P]], channel_multiplier=-1))
                step(eng.affine_select(out=mask_f[r, :, :], in_=mask_f[r, :, :], compare_op=ALU.is_ge,
                                       fill=MASKED, base=QT, pattern=[[0, 2], [-1, P]], channel_multiplier=1))
                step(eng.affine_select(out=mask_f[r, 1, :], in_=mask_f[r, 1, :], compare_op=ALU.is_ge,
                                       fill=MASKED, base=-QT, pattern=[[1, P]], channel_multiplier=0))
            step(eng.tensor_copy(mask_q[:, :, :], mask_f[:, :, :]))
            step(eng.tensor_copy(ident_b[:, :], ident[:, :]))
            eng.nop().then_inc(masks_ready, 1)
            step(eng.memset(ones_b[:, :], 1.0))
            step(eng.memset(minus_half[:, :], -0.5))
            step(eng.memset(minus_one[:, :], -1.0))
            step(eng.affine_select(out=below[:, :], in_=ones_b[:, :], compare_op=ALU.is_ge, fill=0.0,
                                   base=-1, pattern=[[1, P]], channel_multiplier=-1))
            step(eng.iota(dest_i[:, :, :], pattern=[[2 * P, STEPS], [1, 2]], base=0, channel_multiplier=2))
            step(eng.memset(before[0][:, :], 0.0))
            step(eng.memset(tile_expert[:, :], 0))
            step(eng.memset(pad[:, :], 0.0))
            step(eng.iota(pad[:, P:P + 1].bitcast(I32), pattern=[[0, 1]], base=NOWHERE, channel_multiplier=0))
            step(eng.memset(half_4[:, :], -0.5))
            step(eng.iota(iota_i[:, :], pattern=[[1, TILES]], base=0, channel_multiplier=0))
            step(eng.tensor_copy(tile_at[:, :], iota_i[0:1, 0:TILES]))
            step(eng.tensor_scalar(steps16[:, :], iota_i[0:1, 0:16], float(P), None, ALU.mult))
            step(eng.tensor_scalar(tile_row0[:, :], tile_at[:, :], float(P), None, ALU.mult))
            step(eng.memset(upto[:, :, :], 1.0))
            step(eng.affine_select(out=upto[:, :, :], in_=upto[:, :, :], compare_op=ALU.is_ge, fill=0.0,
                                   base=0, pattern=[[1, E], [-1, E]], channel_multiplier=0))
            step(eng.tensor_copy(expert_iota[:, :], iota_i[:, 0:E]))
            step(eng.tensor_scalar(expert_base[:, :], expert_iota[:, :], float(REGION), None, ALU.mult))
            eng.nop().then_inc(const_ready, 1)
            for i in range(4):
                eng.nop().then_inc(rows_free[i], 1)
            eng.wait_ge(dve_const, 3)

            def key_slots(u):
                i = u[1] % 2
                wait(eng, k_hi, ucount(u, 1, 1))
                wait(eng, s_filled, ucount(u, 8, -8))
                eng.tensor_tensor(k_slots[i][:, 4:8, :],
                                  k_parts[:, 0, :].bitcast(F32).unsqueeze(1).to_broadcast([P, 4, KEYS]),
                                  slot_col[:, 4:8].unsqueeze(2).to_broadcast([P, 4, KEYS]),
                                  ALU.mult).then_inc(slots_high, 1)

            def normalise(t):
                i = t[1] % 4
                wait_apart(eng, wait_value, const_ready, res_chain, count(t, 3, 3))
                eng.tensor_scalar(inv_std[:, 0:1], mean_var[:, 1:2], EPS, None, ALU.add).then_inc(norm_chain, 1)
                wait_apart(eng, wait_value, const_ready, x1_ready, count(t, 2, 0))
                eng.tensor_scalar(inv_std[:, 1:2], mean_var[:, 0:1], -1.0, None, ALU.mult).then_inc(norm_chain, 1)
                wait(eng, rows_free[i], rounds(t, 1))
                eng.wait_ge(norm_chain, count(t, 3, 2))
                eng.tensor_tensor(inv_std[:, 2:3], inv_std[:, 0:1], minus_half[:, :], ALU.pow).then_inc(norm_chain, 1)
                wait_apart(eng, wait_value, const_ready, norm_chain, count(t, 3, 3))
                eng.tensor_scalar(rows[i][:, :, 0:P], res[:, :].unsqueeze(1).to_broadcast([P, 2, P]),
                                  inv_std[:, 1:2], inv_std[:, 2:3], ALU.add, ALU.mult).then_inc(x1_ready, 1)
                g, c = t
                dest = dest_i[:, c, :] if isinstance(g, int) else dest_i[:, bass.ds(g * 4 + c, 1), :].rearrange("p o k -> p (o k)")
                eng.tensor_copy(rows[i][:, :, P:P + 1].bitcast(I32).rearrange("p k o -> p (k o)"), dest).then_inc(x1_ready, 1)

            def gap_of_two(t):
                wait(eng, route_chain, count(t, 5, 3))
                wait(eng, weight_chain, count(t, 3, 0))
                eng.tensor_tensor(gap[:, 0:1], best[:, 1:2], best[:, 0:1], ALU.subtract).then_inc(gap_ready, 1)

            def weights_of_two(t):
                i = t[1] % 4
                wait_apart(eng, wait_value, const_ready, gap_exp, count(t, 1, 1))
                eng.tensor_scalar(gap[:, 2:3], gap[:, 1:2], 1.0, None, ALU.add).then_inc(weight_chain, 1)
                eng.wait_ge(weight_chain, count(t, 3, 1))
                eng.tensor_tensor(rows[i][:, 0, P + 1:ROW], gap[:, 2:3], minus_one[:, :], ALU.pow).then_inc(weight_chain, 1)
                eng.wait_ge(weight_chain, count(t, 3, 2))
                eng.tensor_tensor(rows[i][:, 1, P + 1:ROW], gap[:, 1:2], rows[i][:, 0, P + 1:ROW],
                                  ALU.mult).then_inc(weight_chain, 1)

            def scatter(t, picks=(0, 1)):
                i = t[1] % 4
                if is_step(t, EARLY):
                    eng.wait_ge(padded, 16 * E)
                wait_apart(eng, wait_value, const_ready, weight_chain, count(t, 3, 3))
                wait_apart(eng, wait_value, const_ready, x1_ready, count(t, 2, 2))
                wait_apart(eng, wait_value, const_ready, place_chain, count(t, 4, 4))
                for k in picks:
                    eng.indirect_dma_start(
                        routed, bass.IndirectOffsetOnAxis(ap=place[i][:, k:k + 1], axis=0),
                        rows[i][:, k, :], None, bounds_check=SPARE + P - 1, oob_is_err=False).then_inc(scattered[i], 16)

            def slot(t, s):
                if has(s, 4, STEPS):
                    scatter(later(t, -4))
                if has(s, 2, STEPS + 1):
                    normalise(later(t, -2))
                if s == -1:
                    eng.memset(q_stack[1][:, :, :, :].bitcast(F32), 0.0).then_inc(zeros_ready[1], 1)
                if s == 1:
                    eng.wait_ge(loaded, 16 * 4)
                    eng.tensor_tensor(x_all[:, :, :], x_all[:, :, :], bo[:, :].unsqueeze(1).to_broadcast([P, STEPS, P]),
                                      ALU.add).then_inc(xb_ready, 1)
                if has(s, 3, STEPS + 2):
                    gap_of_two(later(t, -3))
                if t[1] % 2 == 0 and has(s, -2, STEPS - 4):
                    key_slots(unit_at(t, 2))
                if s == -2:
                    eng.wait_ge(q_out, 16)
                    eng.wait_ge(zeros_ready[0], 1)
                    for part in range(8 - POOL_PARTS, 8):
                        stack_queries(eng, 0, part).then_inc(first_stacked, 16)
                    eng.wait_ge(first_stacked, 16 * POOL_PARTS)
                    eng.nop().then_inc(stacked[0], 16 * POOL_PARTS)
                if s == STEPS + 2:
                    scatter(later(t, -4))
                if has(s, 3, STEPS + 2):
                    weights_of_two(later(t, -3))
                if s == STEPS:
                    scatter(later(t, -3), (0,))
                if s == STEPS + 1:
                    scatter(later(t, -4), (1,))

            run_slots(eng, slot)
            scatter((0, STEPS - 1))

            def send(n):
                i = n[1] % 8
                wait_apart(eng, wait_value, const_ready, y_ready, tile_count(n, 1, 1))
                eng.indirect_dma_start(
                    expert_out, bass.IndirectOffsetOnAxis(ap=tile_x[i][:, P:P + 1].bitcast(I32), axis=0),
                    y[i][:, :], None, bounds_check=ASSIGNED - 1, oob_is_err=False).then_inc(y_sent[i], 16)

            def tile_slot(n, s):
                if has(s, 4, TILES + 3):
                    send(later(n, -4))

            run_tiles(eng, tile_slot)
            for i in range(8):
                eng.wait_ge(y_sent[i], 16 * ((TILES - 1 - i) // 8 + 1))
            eng.nop().then_inc(all_sent, 1)
            for q in range(3):
                eng.wait_ge(end_chain, 8 * (q + 1))
                t = slice(4 * q, 4 * q + 4)
                eng.tensor_scalar(inv_all[:, 0, t], mean_all[:, t, 1], EPS, None, ALU.add).then_inc(end_inv, 1)
                eng.tensor_scalar(inv_all[:, 1, t], mean_all[:, t, 0], -1.0, None, ALU.mult).then_inc(end_inv, 1)
                eng.wait_ge(end_inv, 4 * q + 2)
                eng.tensor_tensor(inv_all[:, 2, t], inv_all[:, 0, t], half_4[:, :], ALU.pow).then_inc(end_inv, 1)
                eng.wait_ge(end_inv, 4 * q + 3)
                eng.tensor_tensor(inv_all[:, 3, t], inv_all[:, 1, t], inv_all[:, 2, t], ALU.mult).then_inc(end_inv, 1)
                if q == 0:
                    eng.wait_ge(two_loaded[3], 16)
                    eng.tensor_tensor(total_all[:, 12:16, :], y_two[:, 12:16, 0, :], y_two[:, 12:16, 1, :],
                                      ALU.add).then_inc(pool_sum, 1)
            eng.wait_ge(end_chain, 33)
            t = slice(12, 16)
            eng.tensor_tensor(inv_all[:, 2, t], inv_all[:, 0, t], half_4[:, :], ALU.pow).then_inc(end_inv, 1)

        @block.scalar
        def _(eng):
            eng.wait_ge(weights_T, 1)
            for c in range(2):
                eng.copy(wT[:, c, :].rearrange("p (d h g) -> p g h d", d=HD, h=4),
                         unit_bank[:, P * c:P * c + P].rearrange("p (g h d) -> p g h d", g=4, h=4)).then_inc(weights_ready, 1)
            eng.copy(wT[:, 2, :], unit_bank[:, 2 * P:3 * P]).then_inc(weights_ready, 1)
            eng.copy(woT[:, :, :], out_bank[0:QT, 0:2 * P].rearrange("p (h n) -> p h n", h=2)).then_inc(weights_ready, 1)
            eng.wait_ge(halo_ready, 1)
            eng.wait_ge(dve_const, 3)

            def tokens_T(u):
                i = u[1] % 2
                wait(eng, xT_made, ucount(u, 1, 1))
                wait(eng, k_made, ucount(u, 1, -1))
                wait(eng, v_made, ucount(u, 1, -1))
                wait(eng, xT_ready, ucount(u, 2, 0))
                eng.copy(xT[i][:, 0:HALO], xT[1 - i][:, UNIT:KEYS]).then_inc(xT_ready, 1)
                eng.copy(xT[i][:, HALO:KEYS], unit_bank[:, 0:UNIT]).then_inc(xT_ready, 1)

            def queries(u):
                i = u[1] % 2
                wait(eng, q_made, ucount(u, 1, 1))
                wait(eng, q_out, ucount(u, 16, 0))
                wait(eng, q_lo, ucount(u, 1, 0))
                wait(eng, halves_ready, ucount(u, 2, 0))
                eng.activation(q_parts[:, 0, :], unit_bank[:, 0:UNIT], ACT.Copy, scale=SCALE).then_inc(q_hi, 1)
                wait(eng, q_hi, ucount(u, 1, 1))
                wait(eng, s_filled, ucount(u, 8, -8))
                for half in range(2):
                    eng.activation(q_halves[i][:, :, half, :],
                                   q_parts[:, 0, :].bitcast(F32).rearrange("p (w q) -> p w q", w=WIN),
                                   ACT.Copy, scale=half_col[:, half:half + 1]).then_inc(halves_ready, 1)

            def keys(u):
                wait(eng, k_made, ucount(u, 1, 1))
                wait(eng, k_out, ucount(u, 16, 0))
                wait(eng, k_lo, ucount(u, 1, 0))
                wait(eng, slots_high, ucount(u, 1, 0))
                wait(eng, slots_low, ucount(u, 4, 0))
                eng.copy(k_parts[:, 0, :], unit_bank[:, 0:KEYS]).then_inc(k_hi, 1)

            def key_slots(u):
                i = u[1] % 2
                eng.wait_ge(k_hi, ucount(u, 1, 1))
                wait(eng, s_filled, ucount(u, 8, -8))
                for c in range(4):
                    eng.activation(k_slots[i][:, c, :], k_parts[:, 0, :].bitcast(F32), ACT.Copy,
                                   scale=slot_col[:, c:c + 1]).then_inc(slots_low, 1)

            def values(u):
                i = u[1] % 2
                wait(eng, v_made, ucount(u, 1, 1))
                wait(eng, o_filled, ucount(u, 2, -2))
                eng.copy(v_aug[i][:, :, :, 0:HD],
                         unit_bank[:, :].rearrange("p (w h d) -> p w h d", w=WIN, h=HEADS)).then_inc(v_ready, 1)

            def exps(t, a):
                for h in range(2):
                    wait(eng, t_filled, count(t, 4, 2 * a + h + 1))
                    if h == 0:
                        wait(eng, o_filled, count(t, 1, -1))
                    eng.activation(probs[t[1] % 2][a][:, 512 * h:512 * h + 512], t_bank[h][:, :],
                                   ACT.Exp).then_inc(probs_ready, 1)

            def slot(t, s):
                odd = t[1] % 2 and has(s, -3, STEPS - 5)
                if has(s, 0, STEPS - 1):
                    exps(t, 0)
                if has(s, 2, STEPS + 1):
                    v = later(t, -2)
                    wait(eng, oT_made, count(v, 1, 1))
                    wait(eng, y_made, count(v, 1, 0))
                    eng.copy(oT[:, :, :, :].rearrange("c h a q -> c a h q"),
                             out_bank[0:QT, 0:256].rearrange("c (a h q) -> c a h q", a=2, h=2)).then_inc(oT_ready, 1)
                if has(s, 3, STEPS + 2):
                    v = later(t, -3)
                    wait(eng, x1T_made, count(v, 1, 1))
                    wait(eng, logits_made, count(v, 1, 0))
                    eng.copy(x1T[:, :], route_bank[:, 0:P]).then_inc(x1T_ready, 1)
                if odd:
                    tokens_T(unit_at(t, 3))
                if t[1] % 2 == 0 and has(s, -2, STEPS - 4):
                    keys(unit_at(t, 2))
                if has(s, 0, STEPS - 1):
                    exps(t, 1)
                if t[1] % 2 == 0 and has(s, -2, STEPS - 4):
                    key_slots(unit_at(t, 2))
                if t[1] % 2 == 0 and has(s, 0, STEPS - 2):
                    values(unit_at(t, 0))
                if has(s, 3, STEPS + 2):
                    v = later(t, -3)
                    g, c = v
                    dst = x1_all[:, c, :] if isinstance(g, int) else x1_all[:, bass.ds(g * 4 + c, 1), :].rearrange("p o d -> p (o d)")
                    eng.copy(dst, rows[c % 4][:, 0, 0:P]).then_inc(x1_kept, 1)
                if odd:
                    queries(unit_at(t, 3))
                if has(s, 3, STEPS + 2):
                    v = later(t, -3)
                    wait(eng, gap_ready, count(v, 1, 1))
                    eng.activation(gap[:, 1:2], gap[:, 0:1], ACT.Exp).then_inc(gap_exp, 1)

            run_slots(eng, slot)

            def tile_slot(n, s):
                if has(s, -1, TILES - 2):
                    m = later(n, 1)
                    wait(eng, tile_xT_made, tile_count(m, 1, 1))
                    wait(eng, up_made, tile_count(m, 1, -1))
                    eng.copy(tile_xT[m[1] % 2][:, :], xt_bank[:, 0:P]).then_inc(tile_xT_ready, 1)
                if has(s, 3, TILES + 2):
                    m = later(n, -3)
                    wait(eng, actT_made, tile_count(m, 1, 1))
                    wait(eng, down_made, tile_count(m, 1, -1))
                    eng.copy(actT[m[1] % 2][:, :, :], at_bank[:, 0:F].rearrange("p (c n) -> p c n", c=2)).then_inc(actT_ready, 1)
                if has(s, 1, TILES):
                    m = later(n, -1)
                    wait(eng, zT_made, tile_count(m, 1, 1))
                    wait(eng, gate_made, tile_count(m, 1, -1))
                    eng.copy(zT[m[1] % 2][:, :, :], zt_bank[:, 0:F].rearrange("p (c n) -> p c n", c=2)).then_inc(zT_ready, 1)
                if has(s, 2, TILES + 1):
                    m = later(n, -2)
                    wait(eng, gate_ready, tile_count(m, 1, 1))
                    wait(eng, actT_made, tile_count(m, 1, -1))
                    eng.activation(act[m[1] % 2][:, :], gate_in[m[1] % 2][:, :], ACT.Silu).then_inc(act_ready, 1)

            run_tiles(eng, tile_slot)
            for q in range(3):
                eng.wait_ge(end_inv, 4 * (q + 1))
                for t in range(4 * q, 4 * q + 4):
                    eng.activation(out_all[:, t, :], total_all[:, t, :], ACT.Identity, bias=inv_all[:, 3, t:t + 1],
                                   scale=inv_all[:, 2, t:t + 1]).then_inc(out_ready, 1)

        @block.vector
        def _(eng):
            wait_value = eng.alloc_register("wait_value")
            eng.memset(xT[1][:, :], 0.0).then_inc(halo_ready, 1)
            eng.wait_ge(ident_ready, 1)
            eng.tensor_reduce(head_of[:, :], ident[:, :].rearrange("p (d f) -> p f d", d=HD), AX_X,
                              ALU.add).then_inc(dve_const, 1)
            eng.wait_ge(dve_const, 1)
            eng.tensor_reduce(half_col[:, :], head_of[:, :].rearrange("p (h s l) -> p s h l", h=4, s=2),
                              mybir.AxisListType.XY, ALU.add).then_inc(dve_const, 1)
            eng.tensor_reduce(slot_col[:, :].rearrange("p (l h) -> p l h", l=2),
                              head_of[:, :].rearrange("p (h s l) -> p l h s", h=4, s=2), AX_X,
                              ALU.add).then_inc(dve_const, 1)
            eng.wait_ge(weights_loaded, 32)
            eng.tensor_copy(wo_rows[:, :, :].rearrange("p h (k d) -> p h k d", k=8),
                            w_rows[:, 3, :].rearrange("p (k h d) -> p h k d", k=8, h=2)).then_inc(dve_const, 1)
            eng.memset(q_stack[0][:, :, :, :].bitcast(F32), 0.0).then_inc(zeros_ready[0], 1)

            def beside_maxima():
                eng.wait_ge(masks_ready, 1)
                for half in range(2):
                    r, o = slice(64 * half, 64 * half + 64), slice(64 - 64 * half, 128 - 64 * half)
                    eng.memset(shift_w[r, half, :, :].bitcast(F32), -1.0).then_inc(shift_const, 1)
                    eng.tensor_copy(shift_w[o, half, :, :], mask_f[o, :, :]).then_inc(shift_const, 1)
                    for a in range(2):
                        eng.tensor_copy(shift[a][half][o, :, :],
                                        delta[o, :].unsqueeze(1).to_broadcast([64, 8, QT])).then_inc(shift_const, 1)
                for i in range(2):
                    eng.memset(v_aug[i][:, :, :, HD:HD + 1], 1.0).then_inc(shift_const, 1)

            def find_top(t, a, h):
                if h == 0:
                    wait(eng, shift_ready, count(t, 4, 2 * a - 2))
                wait(eng, s_filled, count(t, 4, 2 * a + h + 1))
                eng.tensor_reduce(top[a][:, 4 * h:4 * h + 4],
                                  s_bank[h][:, :].rearrange("p (s k) -> p s k", s=4), AX_X,
                                  ALU.max).then_inc(s_read, 1)

            def spread_top(t, a, half):
                if half == 0:
                    wait(eng, t_filled, count(t, 4, 2 * a + 2 - 4))
                    eng.wait_ge(s_read, count(t, 4, 2 * a + 2))
                r = slice(64 * half, 64 * half + 64)
                eng.tensor_tensor(shift[a][half][r, :, :], top[a][r, :].unsqueeze(2).to_broadcast([64, 8, QT]),
                                  delta[r, :].unsqueeze(1).to_broadcast([64, 8, QT]),
                                  ALU.mult).then_inc(shift_ready, 1)

            def values_of(t):
                return values_bank(t)[:, 0:288].rearrange("p (a h n) -> p a h n", a=2, h=8)

            def denominators(t, half):
                if half == 0:
                    wait(eng, o_filled, count(t, 1, 1))
                    wait(eng, o_ready, count(t, 2, 0))
                r, c = slice(64 * half, 64 * half + 64), 9 * half
                eng.reciprocal(o_den[r, :, :], values_of(t)[r, :, :, c + HD:c + HD + 1].rearrange("p a h o -> p a (h o)")).then_inc(den_ready, 1)

            def divide(t, half):
                wait(eng, oT_made, count(t, 1, 0))
                eng.wait_ge(den_ready, count(t, 2, half + 1))
                r, c = slice(64 * half, 64 * half + 64), 9 * half
                eng.tensor_tensor(o_norm[r, :, :, :], values_of(t)[r, :, :, c:c + HD],
                                  o_den[r, :, :].unsqueeze(3).to_broadcast([64, 2, 8, HD]),
                                  ALU.mult).then_inc(o_ready, 1)

            def residual(t):
                g, c = t
                if is_step(t, 0):
                    eng.wait_ge(xb_ready, 1)
                wait(eng, y_made, count(t, 1, 1))
                wait(eng, x1_ready, count(t, 2, 0))
                wait(eng, res_chain, count(t, 3, 0))
                xs = x_all[:, c, :] if isinstance(g, int) else x_all[:, bass.ds(g * 4 + c, 1), :].rearrange("p o d -> p (o d)")
                eng.tensor_tensor(res[:, :], out_bank[:, 256:384], xs, ALU.add).then_inc(res_chain, 1)

            def statistics(t):
                eng.wait_ge(res_chain, count(t, 3, 1))
                eng.bn_stats(stats[:, :], res[:, :]).then_inc(res_chain, 1)

            def mean_variance(t):
                wait_apart(eng, wait_value, const_ready, res_chain, count(t, 3, 2))
                eng.bn_aggr(mean_var[:, :], stats[:, :]).then_inc(res_chain, 1)

            def split_queries(u):
                wait(eng, q_hi, ucount(u, 1, 1))
                eng.scalar_tensor_tensor(out=q_parts[:, 1, :], in0=unit_bank[:, 0:UNIT], scalar=SCALE,
                                         in1=q_parts[:, 0, :].bitcast(F32), op0=ALU.mult,
                                         op1=ALU.subtract).then_inc(q_lo, 1)

            def split_keys(u):
                wait(eng, k_hi, ucount(u, 1, 1))
                eng.tensor_tensor(k_parts[:, 1, :], unit_bank[:, 0:KEYS], k_parts[:, 0, :].bitcast(F32),
                                  ALU.subtract).then_inc(k_lo, 1)

            def biased_logits(t):
                if is_step(t, 0):
                    eng.wait_ge(loaded, 16 * 4)
                    eng.wait_ge(const_ready, 1)
                wait(eng, logits_made, count(t, 1, 1))
                wait(eng, gap_ready, count(t, 1, 0))
                eng.tensor_tensor(logits[:, :], route_bank[:, P:P + E], gate_bias[:, :], ALU.add).then_inc(route_chain, 1)

            def best_logits(t):
                wait_apart(eng, wait_value, const_ready, route_chain, count(t, 5, 1))
                eng.max(best[:, :], logits[:, :]).then_inc(route_chain, 1)

            def best_experts(t):
                wait_apart(eng, wait_value, const_ready, route_chain, count(t, 5, 2))
                eng.max_index(best_at[:, :], best[:, :], logits[:, :]).then_inc(route_chain, 1)

            def mark_chosen(t):
                eng.wait_ge(route_chain, count(t, 5, 3))
                wait(eng, place_chain, count(t, 4, 0))
                eng.tensor_tensor(chosen[:, :, :], expert_iota[:, :].unsqueeze(1).to_broadcast([P, 2, E]),
                                  best_at[:, 0:2].unsqueeze(2).to_broadcast([P, 2, E]),
                                  ALU.is_equal).then_inc(route_chain, 1)

            def mark_picked(t):
                eng.wait_ge(route_chain, count(t, 5, 4))
                wait(eng, rank_made, count(t, 1, 0))
                wait(eng, before_ready, count(t, 1, 0))
                eng.tensor_tensor(picked[:, :], chosen[:, 0, :], chosen[:, 1, :], ALU.add).then_inc(route_chain, 1)

            def places_of_experts(t):
                i = t[1] % 2
                wait(eng, rank_made, count(t, 1, 1))
                eng.tensor_tensor(place_e[:, :], route_bank[:, P + E:P + 2 * E], expert_base[:, :], ALU.add).then_inc(place_chain, 1)
                eng.wait_ge(route_chain, count(t, 5, 5))
                eng.tensor_tensor(before[1 - i][:, :], before[i][:, :], picked[:, :], ALU.add).then_inc(before_ready, 1)

            def places_of_chosen(t):
                eng.wait_ge(place_chain, count(t, 4, 1))
                eng.tensor_tensor(place_2[:, :, :], chosen[:, :, :], place_e[:, :].unsqueeze(1).to_broadcast([P, 2, E]),
                                  ALU.mult).then_inc(place_chain, 1)

            def sum_places(t):
                eng.wait_ge(place_chain, count(t, 4, 2))
                eng.tensor_reduce(place_f[:, :], place_2[:, :, :], AX_X, ALU.add).then_inc(place_chain, 1)

            def whole_places(t):
                eng.wait_ge(place_chain, count(t, 4, 3))
                wait(eng, rows_free[t[1] % 4], rounds(t, 1))
                eng.tensor_copy(place[t[1] % 4][:, :], place_f[:, :]).then_inc(place_chain, 1)

            def slot(t, s):
                if s == EARLY + 3:
                    eng.wait_ge(totals_made, 1)
                    eng.tensor_tensor(pad_f[:, :], route_bank[0:1, 2 * P:2 * P + E], expert_base[0:1, :],
                                      ALU.add).then_inc(pad_chain, 1)
                    eng.wait_ge(pad_chain, 1)
                    eng.tensor_copy(pad_row[:, :], pad_f[:, :]).then_inc(pad_chain, 1)
                top_t, out_t, res_t, route_t = later(t, 1), later(t, -1), later(t, -2), later(t, -3)
                find, divides = has(s, -1, STEPS - 2), has(s, 1, STEPS)
                adds, routes = has(s, 2, STEPS + 1), has(s, 3, STEPS + 2)
                if find:
                    find_top(top_t, 0, 0)
                    find_top(top_t, 0, 1)
                    spread_top(top_t, 0, 0)
                if find:
                    spread_top(top_t, 0, 1)
                if adds:
                    residual(res_t)
                if adds:
                    statistics(res_t)
                if t[1] % 2 == 0 and has(s, -2, STEPS - 4):
                    split_keys(unit_at(t, 2))
                if routes:
                    biased_logits(route_t)
                if adds:
                    mean_variance(res_t)
                if routes:
                    best_logits(route_t)
                if find:
                    find_top(top_t, 1, 0)
                if routes:
                    best_experts(route_t)
                if find:
                    find_top(top_t, 1, 1)
                if routes:
                    mark_chosen(route_t)
                    mark_picked(route_t)
                if find:
                    spread_top(top_t, 1, 0)
                    spread_top(top_t, 1, 1)
                if t[1] % 2 and has(s, -3, STEPS - 5):
                    split_queries(unit_at(t, 3))
                if s == -3:
                    beside_maxima()
                if routes:
                    places_of_experts(route_t)
                    places_of_chosen(route_t)
                if routes:
                    sum_places(route_t)
                if divides:
                    denominators(out_t, 0)
                if divides:
                    denominators(out_t, 1)
                if routes:
                    whole_places(route_t)
                if divides:
                    divide(out_t, 0)
                    divide(out_t, 1)

            run_slots(eng, slot)

            links = [0]

            def link(ins):
                links[0] += 1
                ins.then_inc(table_chain, 1)
                eng.wait_ge(table_chain, links[0])

            eng.wait_ge(totals_made, 2)
            link(eng.tensor_copy(total[:, :], route_bank[0:1, P:P + E]))
            link(eng.tensor_tensor(need_16[:, :, :], total[:, :].unsqueeze(2).to_broadcast([1, E, 16]),
                                   steps16[:, :].unsqueeze(1).to_broadcast([1, E, 16]), ALU.is_gt))
            link(eng.tensor_reduce(need[:, :], need_16[:, :, :], AX_X, ALU.add))
            link(eng.tensor_tensor(ends_2[:, :, :], upto[:, :, :], need[:, :].unsqueeze(1).to_broadcast([1, E, E]), ALU.mult))
            link(eng.tensor_reduce(ends[:, :], ends_2[:, :, :], AX_X, ALU.add))
            link(eng.tensor_tensor(passed[:, :, :], ends[:, :].unsqueeze(1).to_broadcast([1, TILES, E]),
                                   tile_at[:, :].unsqueeze(2).to_broadcast([1, TILES, E]), ALU.is_le))
            link(eng.tensor_reduce(table_f[:, 0, :], passed[:, :, :], AX_X, ALU.add))
            link(eng.tensor_scalar(jump[:, :], need[:, :], -float(P), float(REGION), ALU.mult, ALU.add))
            link(eng.tensor_tensor(jumps[:, :, :], passed[:, :, :], jump[:, :].unsqueeze(1).to_broadcast([1, TILES, E]), ALU.mult))
            link(eng.tensor_reduce(table_f[:, 1, :], jumps[:, :, :], AX_X, ALU.add))
            link(eng.tensor_tensor(table_f[:, 1, :], table_f[:, 1, :], tile_row0[:, :], ALU.add))
            link(eng.tensor_scalar(tile_expert[:, 4:4 + TILES], table_f[:, 0, :], float(E - 1), None, ALU.min))
            link(eng.tensor_scalar(tile_row[:, :], table_f[:, 1, :], float(SPARE), None, ALU.min))
            eng.wait_ge(experts_loaded, 16 * (4 * E + 4))

            def tile_slot(n, s):
                e = experts_at(mybir.EngineType.DVE, n, s)
                if 4 in e:
                    m = later(n, -4)
                    wait(eng, down_made, tile_count(m, 1, 1))
                    wait(eng, y_ready, tile_count(m, 1, 0))
                    eng.tensor_tensor(y_in[:, :], down_bank[:, 0:P], of_expert(b_down, e[4]), ALU.add).then_inc(down_read, 1)
                if 2 in e:
                    m = later(n, -2)
                    wait(eng, gate_made, tile_count(m, 1, 1))
                    wait(eng, act_ready, tile_count(m, 1, -1))
                    eng.tensor_tensor(gate_in[m[1] % 2][:, :], gate_bank[:, 0:F], of_expert(b_gate, e[2]),
                                      ALU.add).then_inc(gate_ready, 1)
                if 4 in e:
                    m = later(n, -4)
                    eng.wait_ge(down_read, tile_count(m, 1, 1))
                    eng.tensor_scalar(y[m[1] % 8][:, :], y_in[:, :], tile_x[m[1] % 8][:, P + 1:ROW], None,
                                      ALU.mult).then_inc(y_ready, 1)
                if 0 in e:
                    wait(eng, up_made, tile_count(n, 1, 1))
                    wait(eng, z_ready, tile_count(n, 1, 0))
                    eng.tensor_tensor(up[:, :, :].rearrange("p a n -> p (a n)"), up_bank[:, :], of_expert(b_up, e[0]),
                                      ALU.add).then_inc(up_ready, 1)
                    eng.wait_ge(up_ready, tile_count(n, 1, 1))
                    wait(eng, zT_made, tile_count(n, 1, -1))
                    eng.tensor_tensor(z[n[1] % 2][:, :], up[:, 0, :], up[:, 1, :], ALU.mult).then_inc(z_ready, 1)

            run_tiles(eng, tile_slot)

            eng.wait_ge(x1_kept, STEPS)
            for q in range(4):
                t = slice(4 * q, 4 * q + 4)
                if q < 3:
                    eng.wait_ge(two_loaded[q], 16)
                    eng.tensor_tensor(total_all[:, t, :], y_two[:, t, 0, :], y_two[:, t, 1, :], ALU.add).then_inc(end_sum, 1)
                    eng.wait_ge(end_sum, 2 * q + 1)
                else:
                    eng.wait_ge(pool_sum, 1)
                eng.tensor_tensor(total_all[:, t, :], total_all[:, t, :], x1_all[:, t, :], ALU.add).then_inc(end_sum, 1)
                eng.wait_ge(end_sum, 2 * q + 2 if q < 3 else 7)
                for j in range(4 * q, 4 * q + 4):
                    eng.bn_stats(stats_all[:, j, :], total_all[:, j, :]).then_inc(end_chain, 1)
                eng.wait_ge(end_chain, 8 * q + 4)
                for j in range(4 * q, 4 * q + 4):
                    eng.bn_aggr(mean_all[:, j, :], stats_all[:, j, :]).then_inc(end_chain, 1)
            t = slice(12, 16)
            eng.wait_ge(end_chain, 32)
            eng.tensor_scalar(inv_all[:, 0, t], mean_all[:, t, 1], EPS, None, ALU.add).then_inc(end_chain, 1)
            eng.wait_ge(end_inv, 3 * 4 + 1)
            for j in range(12, 16):
                eng.tensor_scalar(out_all[:, j, :], total_all[:, j, :], mean_all[:, j, 0:1], inv_all[:, 2, j:j + 1],
                                  ALU.subtract, ALU.mult).then_inc(last_ready, 1)

        @block.tensor
        def _(eng):
            wait_value = eng.alloc_register("wait_value")
            eng.wait_ge(weights_loaded, 32)
            eng.wait_ge(ident_ready, 1)
            eng.wait_ge(dve_const, 4)
            for c in range(3):
                eng.transpose(unit_bank[:, P * c:P * c + P], w_rows[:, c, :], ident[:, :])
            for half in range(2):
                ins = eng.transpose(out_bank[0:QT, P * half:P * half + P],
                                    wo_rows[:, half, :], ident[:, :])
            ins.then_inc(weights_T, 1)
            eng.wait_ge(weights_ready, 4)

            def tokens_T(u):
                g, c = u
                i = c % 2
                eng.wait_ge(x_loaded[i], pcount(u, 16))
                wait(eng, v_ready, ucount(u, 1, -1))
                wait(eng, k_lo, ucount(u, 1, 0))
                wait(eng, k_hi, ucount(u, 1, 0))
                for j in range(2):
                    ins = eng.transpose(unit_bank[:, P * j:P * j + P], x_unit[i][:, j, :], ident[:, :])
                ins.then_inc(xT_made, 1)

            def queries(u):
                i = u[1] % 2
                wait(eng, xT_ready, ucount(u, 2, 2))
                eng.matmul(unit_bank[:, 0:UNIT], wT[:, 0, :], xT[i][:, HALO:KEYS]).then_inc(q_made, 1)

            def keys(u):
                i = u[1] % 2
                wait(eng, q_hi, ucount(u, 1, 1))
                wait(eng, q_lo, ucount(u, 1, 1))
                eng.matmul(unit_bank[:, 0:KEYS], wT[:, 1, :], xT[i][:, :]).then_inc(k_made, 1)

            def values(u, last):
                i = u[1] % 2
                wait(eng, k_hi, ucount(u, 1, 1 if last else 2))
                wait(eng, k_lo, ucount(u, 1, 1 if last else 2))
                for w in range(WIN):
                    ins = eng.matmul(unit_bank[:, P * w:P * w + P], xT[i][:, QT * w:QT * w + P], wT[:, 2, :])
                ins.then_inc(v_made, 1)

            def max_scores(t, a):
                i, w = (t[1] // 2) % 2, 2 * (t[1] % 2) + a
                first = int(t[1] % PER_BATCH == 0 and a == 0)
                u = (t[0], t[1] // 2)
                wait(eng, halves_ready, ucount(u, 2, 2))
                if is_step(t, 0):
                    eng.wait_ge(masks_ready, 1)
                for h in range(2):
                    if h == 0:
                        wait(eng, slots_low, ucount(u, 4, 4))
                    else:
                        wait(eng, slots_high, ucount(u, 1, 1))
                    wait(eng, s_read, count(t, 4, 2 * a + h - 1))
                    eng.matmul(s_bank[h][:, :], ident_b[:, :], mask_q[:, first:first + 1, :].to_broadcast([P, 4, P]),
                               start=True, stop=False)
                    eng.matmul(s_bank[h][:, :], q_halves[i][:, w, :, :],
                               k_slots[i][:, 4 * h:4 * h + 4, QT * w:QT * w + P],
                               start=False, stop=True).then_inc(s_filled, 1)

            def shifted_scores(t, a):
                i, w = (t[1] // 2) % 2, 2 * (t[1] % 2) + a
                first = int(t[1] % PER_BATCH == 0 and a == 0)
                u = (t[0], t[1] // 2)
                if is_step(t, 0):
                    eng.wait_ge(shift_const, 10)
                wait(eng, shift_ready, count(t, 4, 2 * a + 2))
                wait(eng, stacked[i], pcount(u, 192))
                for h in range(2):
                    wait(eng, probs_ready, count(t, 4, 2 * a + h - 1))
                    for l in range(2):
                        grp = 2 * h + l
                        eng.matmul(t_bank[h][:, 256 * l:256 * l + 256], k_stack[i][:, grp, QT * w:QT * w + P],
                                   q_stack[i][:, grp, :, QT * w:QT * w + QT], start=(l == 0), stop=False,
                                   skip_group_check=True)
                    eng.matmul(t_bank[h][:, :], shift_w[:, h, first, :], shift[a][h][:, :, :], start=False,
                               stop=True, skip_group_check=True).then_inc(t_filled, 1)

            def weighted_values(t, quarter):
                i, a = (t[1] // 2) % 2, quarter // 2
                w = 2 * (t[1] % 2) + a
                if quarter == 0:
                    wait(eng, v_ready, ucount((t[0], t[1] // 2), 1, 1))
                    if is_step(t, STEPS - 1):
                        eng.wait_ge(s_read, 4 * STEPS)
                    else:
                        wait(eng, o_ready, count(t, 2, 0))
                wait(eng, probs_ready, count(t, 4, 2 * a + 2))
                for p in range(4 * (quarter % 2), 4 * (quarter % 2) + 4):
                    c = 144 * a + 18 * p
                    ins = eng.matmul(values_bank(t)[:, c:c + 18], probs[t[1] % 2][a][:, P * p:P * p + P],
                                     v_aug[i][:, w, 2 * p:2 * p + 2, :])
                if quarter == 3:
                    ins.then_inc(o_filled, 1)

            def heads_T(t):
                wait(eng, o_ready, count(t, 2, 2))
                wait_apart(eng, wait_value, const_ready, res_chain, count(t, 3, -2))
                for a in range(2):
                    ins = eng.transpose(out_bank[0:QT, P * a:P * a + P],
                                        o_norm[:, a, :, :].rearrange("p h d -> p (h d)"), ident[:, :])
                ins.then_inc(oT_made, 1)

            def project_out(t):
                wait(eng, oT_ready, count(t, 1, 1))
                for half in range(2):
                    ins = eng.matmul(out_bank[:, 256:384], oT[:, half, :, :], woT[:, half, :],
                                     start=(half == 0), stop=(half == 1))
                ins.then_inc(y_made, 1)

            def early_totals():
                eng.wait_ge(before_ready, EARLY)
                eng.wait_ge(place_chain, 4 * EARLY - 3)
                eng.matmul(route_bank[:, 2 * P:2 * P + E], ones_b[:, :], before[EARLY % 2][:, :]).then_inc(totals_made, 1)

            def x1_T(t):
                if is_step(t, EARLY):
                    early_totals()
                    eng.wait_ge(pad_chain, 1)
                wait(eng, x1_ready, count(t, 2, 1))
                wait(eng, place_chain, count(t, 4, -3))
                eng.transpose(route_bank[:, 0:P], rows[t[1] % 4][:, 0, 0:P], ident[:, :]).then_inc(x1T_made, 1)

            def gate_logits(t):
                if is_step(t, 0):
                    eng.wait_ge(loaded, 16 * 4)
                    eng.wait_ge(const_ready, 1)
                wait(eng, x1T_ready, count(t, 1, 1))
                eng.matmul(route_bank[:, P:P + E], x1T[:, :], gate[:, :]).then_inc(logits_made, 1)

            def ranks(t):
                i = t[1] % 2
                wait(eng, route_chain, count(t, 5, 5))
                wait(eng, before_ready, count(t, 1, 0))
                eng.matmul(route_bank[:, P + E:P + 2 * E], below[:, :], picked[:, :], start=True, stop=False)
                eng.matmul(route_bank[:, P + E:P + 2 * E], ones_b[:, :], before[i][:, :], start=False, stop=True).then_inc(rank_made, 1)

            def slot(t, s):
                odd = t[1] % 2 and has(s, -3, STEPS - 5)
                out_t = later(t, -1) if has(s, 1, STEPS) else None
                if s == STEPS:
                    for quarter in range(1):
                        weighted_values(later(t, -1), quarter)
                if has(s, -1, STEPS - 2):
                    max_scores(later(t, 1), 0)
                if has(s, 0, STEPS - 1):
                    shifted_scores(t, 0)
                if has(s, 2, STEPS + 1):
                    heads_T(later(t, -2))
                if has(s, 3, STEPS + 2):
                    x1_T(later(t, -3))
                if odd:
                    tokens_T(unit_at(t, 3))
                if t[1] % 2 == 0 and has(s, -2, STEPS - 4):
                    keys(unit_at(t, 2))
                if out_t is not None and s != STEPS:
                    weighted_values(out_t, 0)
                if has(s, 2, STEPS + 1):
                    project_out(later(t, -2))
                if has(s, 3, STEPS + 2):
                    gate_logits(later(t, -3))
                if has(s, -1, STEPS - 2):
                    max_scores(later(t, 1), 1)
                if has(s, 0, STEPS - 1):
                    shifted_scores(t, 1)
                if out_t is not None:
                    weighted_values(out_t, 1)
                if t[1] % 2 == 0 and has(s, 0, STEPS - 2):
                    values(unit_at(t, 0), s == STEPS - 2)
                if odd:
                    queries(unit_at(t, 3))
                if out_t is not None:
                    weighted_values(out_t, 2)
                if has(s, 3, STEPS + 2):
                    ranks(later(t, -3))
                if out_t is not None:
                    weighted_values(out_t, 3)

            run_slots(eng, slot)
            eng.wait_ge(place_chain, 4 * STEPS)
            eng.wait_ge(before_ready, STEPS)
            eng.matmul(route_bank[:, P:P + E], ones_b[:, :], before[STEPS % 2][:, :]).then_inc(totals_made, 1)
            eng.wait_ge(table_chain, 13)
            for _ in range(11):
                eng.matmul(out_bank[:, :], ident_b[:, :], mask_q[:, 0:1, :].to_broadcast([P, 4, P]))
            eng.wait_ge(experts_loaded, 16 * (4 * E + 4))

            def tile_slot(n, s):
                e = experts_at(mybir.EngineType.PE, n, s)
                if 4 in e:
                    m = later(n, -4)
                    wait(eng, actT_ready, tile_count(m, 1, 1))
                    wait(eng, down_read, tile_count(m, 1, 0))
                    for c in range(2):
                        ins = eng.matmul(down_bank[:, 0:P], actT[m[1] % 2][:, c, :],
                                         w_down[:, bass.ds(e[4], 1), c, :].rearrange("p o n -> p (o n)"),
                                         start=(c == 0), stop=(c == 1))
                    ins.then_inc(down_made, 1)
                if 2 in e:
                    m = later(n, -2)
                    wait(eng, zT_ready, tile_count(m, 1, 1))
                    wait(eng, gate_ready, tile_count(m, 1, 0))
                    for c in range(2):
                        ins = eng.matmul(gate_bank[:, 0:F], zT[m[1] % 2][:, c, :],
                                         w_gate[:, bass.ds(e[2], 1), c, :].rearrange("p o n -> p (o n)"),
                                         start=(c == 0), stop=(c == 1))
                    ins.then_inc(gate_made, 1)
                if has(s, -1, TILES - 2):
                    m = later(n, 1)
                    wait(eng, tile_loaded[m[1] % 8], tile_rounds(m, 16))
                    wait(eng, tile_xT_ready, tile_count(m, 1, 0))
                    eng.transpose(xt_bank[:, 0:P], tile_x[m[1] % 8][:, 0:P], ident[:, :]).then_inc(tile_xT_made, 1)
                if has(s, 3, TILES + 2):
                    m = later(n, -3)
                    wait(eng, act_ready, tile_count(m, 1, 1))
                    wait(eng, actT_ready, tile_count(m, 1, 0))
                    for c in range(2):
                        ins = eng.transpose(at_bank[:, P * c:P * c + P], act[m[1] % 2][:, P * c:P * c + P], ident[:, :])
                    ins.then_inc(actT_made, 1)
                if has(s, 1, TILES):
                    m = later(n, -1)
                    wait(eng, z_ready, tile_count(m, 1, 1))
                    wait(eng, zT_ready, tile_count(m, 1, 0))
                    for c in range(2):
                        ins = eng.transpose(zt_bank[:, P * c:P * c + P], z[m[1] % 2][:, P * c:P * c + P], ident[:, :])
                    ins.then_inc(zT_made, 1)
                if 0 in e:
                    wait(eng, tile_xT_ready, tile_count(n, 1, 1))
                    wait(eng, up_ready, tile_count(n, 1, 0))
                    eng.matmul(up_bank[:, :], tile_xT[n[1] % 2][:, :], of_expert(w_up, e[0])).then_inc(up_made, 1)

            run_tiles(eng, tile_slot)


_INS = ["L0_attn_x", "L0_attn_w_qkv", "L0_attn_w_out", "L0_attn_b_out", "L0_ffn_gate_w", "L0_ffn_gate_b",
        "L0_ffn_w1", "L0_ffn_b1", "L0_ffn_w2", "L0_ffn_b2", "L0_ffn_wg", "L0_ffn_bg", "L0_ffn_w3", "L0_ffn_b3"]
_OUTS = [((4, 512, 128), "float32")]


def kernel(**inputs):
    import numpy as _np
    import concourse.bacc as _bacc
    from concourse import mybir as _mybir
    from concourse.bass_utils import run_bass_kernel_spmd as _run

    nc = _bacc.Bacc("TRN2", target_bir_lowering=False, num_devices=1)
    arrays, args = {}, []
    for name in _INS:
        a = _np.ascontiguousarray(inputs[name])
        arrays[f"in_{name}_dram"] = a
        args.append(nc.dram_tensor(f"in_{name}_dram", a.shape, _mybir.dt.from_np(a.dtype), kind="ExternalInput").ap())
    for i, (shape, dtype) in enumerate(_OUTS):
        dt = _mybir.dt.from_np(_np.dtype(dtype))
        args.append(nc.dram_tensor(f"out_{i}_dram", shape, dt, kind="ExternalOutput").ap())
    moe_layer_program(nc, *args)
    r = _run(nc, [arrays], core_ids=[0])
    return r.results[0]["out_0_dram"]
```
